# Optimizing a Trainium2 kernel written in Bass

```python
import numpy as np
import jax
import jax.numpy as jnp

def _softmax(x, axis=-1):
    return jax.nn.softmax(x, axis=axis)

def _gelu(x):
    return jax.nn.gelu(x, approximate=True)

def _silu(x):
    return jax.nn.silu(x)

def _sigmoid(x):
    return jax.nn.sigmoid(x)

def _layernorm(x, axis=-1, eps=1e-05):
    m = jnp.mean(x, axis=axis, keepdims=True)
    v = jnp.var(x, axis=axis, keepdims=True)
    return (x - m) / jnp.sqrt(v + eps)

def _scatter_add(tgt, idx, src, axis=0):
    return tgt.at[idx].add(src)

def _segment_sum(src, seg, n):
    return jax.ops.segment_sum(src, seg, n)
kernel_name = 'mk_prb_d2_jaxref_r8_eceb97'

def setup_inputs(seed: int=0):
    np.random.seed(seed)
    _w = jnp.asarray

    def _L0_attn_setup():
        import jax, jax.numpy as jnp
        import numpy as np
        LR = 0.001

        def _mlp(params, h):
            W1, b1, W2, b2 = params
            return jax.nn.silu(h @ W1 + b1) @ W2 + b2
        key = jax.random.key(seed)
        ks = jax.random.split(key, 6)
        B, S, D = (8, 256, 128)
        sc = 1.0 / np.sqrt(D)
        x = jax.random.normal(ks[0], (B, S, D), dtype=jnp.float32)
        W_Q = jax.random.normal(ks[1], (D, D), dtype=jnp.float32) * sc
        W_KV = jax.random.normal(ks[2], (D, 2 * D), dtype=jnp.float32) * sc
        W1 = jax.random.normal(ks[3], (D, D), dtype=jnp.float32) * sc
        b1 = jnp.zeros((D,), dtype=jnp.float32)
        W2 = jax.random.normal(ks[4], (D, D), dtype=jnp.float32) * sc
        b2 = jnp.zeros((D,), dtype=jnp.float32)
        return {'x': x, 'W_Q': W_Q, 'W_KV': W_KV, 'W1': W1, 'b1': b1, 'W2': W2, 'b2': b2}
    _L0_attn_in = _L0_attn_setup()

    def _L0_ffn_setup():
        import jax, jax.numpy as jnp
        import numpy as np
        DIM = 128
        HEADS = 16
        HD = DIM // HEADS
        M = 32
        E = 4
        K = 2
        HID = 256
        MID = 256
        LB = 0.01
        EPS = 1.1920929e-07

        def _rms(x, w):
            return x * jax.lax.rsqrt(jnp.mean(x * x, axis=-1, keepdims=True) + EPS) * w

        def _gelu(x):
            return jax.nn.gelu(x, approximate=False)
        key = jax.random.key(seed)
        ks = jax.random.split(key, 20)
        d = DIM
        w = lambda k, s: jax.random.normal(k, s, jnp.float32) * 0.02
        return {'x': jax.random.normal(ks[0], (4, 128, d), jnp.float32), 'n1_w': jnp.ones((d,), jnp.float32), 'n2_w': jnp.ones((d,), jnp.float32), 'wq': w(ks[1], (d, d)), 'wk': w(ks[2], (d, d)), 'wv': w(ks[3], (d, d)), 'wo': w(ks[4], (d, d)), 'qn_w': jnp.ones((HD,), jnp.float32), 'kn_w': jnp.ones((HD,), jnp.float32), 'gate_w': w(ks[5], (E, d)), 'e0_up': w(ks[6], (HID, d)), 'e0_down': w(ks[7], (d, HID)), 'e1_w1': w(ks[8], (HID, d)), 'e1_w2': w(ks[9], (HID, d)), 'e1_down': w(ks[10], (d, HID)), 'e2_l1': w(ks[11], (MID, d)), 'e2_l2': w(ks[12], (HID, MID)), 'e2_l3': w(ks[13], (MID, HID)), 'e2_l4': w(ks[14], (d, MID)), 'e3_down': w(ks[15], (d, d)), 'e3_up': w(ks[16], (HID, d)), 'e3_out': w(ks[17], (d, HID))}
    _L0_ffn_in = _L0_ffn_setup()

    def _L1_attn_setup():
        import jax, jax.numpy as jnp
        import numpy as np
        D_MODEL, NUM_HEADS, D_HEAD, SEQ, BATCH = (128, 16, 64, 512, 1)
        key = jax.random.key(seed)
        ks = jax.random.split(key, 5)
        scale = 1.0 / np.sqrt(D_MODEL)
        x = jax.random.normal(ks[0], (BATCH, SEQ, D_MODEL), dtype=jnp.float32)
        W_K = jax.random.normal(ks[1], (NUM_HEADS, D_HEAD, D_MODEL), dtype=jnp.float32) * scale
        W_Q = jax.random.normal(ks[2], (NUM_HEADS, D_HEAD, D_MODEL), dtype=jnp.float32) * scale
        W_V = jax.random.normal(ks[3], (NUM_HEADS, D_HEAD, D_MODEL), dtype=jnp.float32) * scale
        W_O = jax.random.normal(ks[4], (D_MODEL, NUM_HEADS * D_HEAD), dtype=jnp.float32) * scale
        return {'x': x, 'W_K': W_K, 'W_Q': W_Q, 'W_V': W_V, 'W_O': W_O}
    _L1_attn_in = _L1_attn_setup()

    def _L1_ffn_setup():
        import jax, jax.numpy as jnp
        import numpy as np
        B, S, H, I, E, K = (2, 256, 128, 256, 8, 2)
        key = jax.random.key(seed)
        k1, k2, k3, k4, k5 = jax.random.split(key, 5)
        scale_h = 1.0 / np.sqrt(H)
        scale_i = 1.0 / np.sqrt(I)
        return {'x': jax.random.normal(k1, (B, S, H), dtype=jnp.float32), 'Wg': jax.random.normal(k2, (H, E), dtype=jnp.float32) * scale_h, 'W11': jax.random.normal(k3, (E, H, I), dtype=jnp.float32) * scale_h, 'W12': jax.random.normal(k4, (E, H, I), dtype=jnp.float32) * scale_h, 'W2': jax.random.normal(k5, (E, I, H), dtype=jnp.float32) * scale_i}
    _L1_ffn_in = _L1_ffn_setup()
    _d = {'L0_attn_x': _L0_attn_in['x'], 'L0_attn_W_Q': _L0_attn_in['W_Q'], 'L0_attn_W_KV': _L0_attn_in['W_KV'], 'L0_attn_W1': _L0_attn_in['W1'], 'L0_attn_b1': _L0_attn_in['b1'], 'L0_attn_W2': _L0_attn_in['W2'], 'L0_attn_b2': _L0_attn_in['b2'], 'L0_ffn_n1_w': _L0_ffn_in['n1_w'], 'L0_ffn_n2_w': _L0_ffn_in['n2_w'], 'L0_ffn_wq': _L0_ffn_in['wq'], 'L0_ffn_wk': _L0_ffn_in['wk'], 'L0_ffn_wv': _L0_ffn_in['wv'], 'L0_ffn_wo': _L0_ffn_in['wo'], 'L0_ffn_qn_w': _L0_ffn_in['qn_w'], 'L0_ffn_kn_w': _L0_ffn_in['kn_w'], 'L0_ffn_gate_w': _L0_ffn_in['gate_w'], 'L0_ffn_e0_up': _L0_ffn_in['e0_up'], 'L0_ffn_e0_down': _L0_ffn_in['e0_down'], 'L0_ffn_e1_w1': _L0_ffn_in['e1_w1'], 'L0_ffn_e1_w2': _L0_ffn_in['e1_w2'], 'L0_ffn_e1_down': _L0_ffn_in['e1_down'], 'L0_ffn_e2_l1': _L0_ffn_in['e2_l1'], 'L0_ffn_e2_l2': _L0_ffn_in['e2_l2'], 'L0_ffn_e2_l3': _L0_ffn_in['e2_l3'], 'L0_ffn_e2_l4': _L0_ffn_in['e2_l4'], 'L0_ffn_e3_down': _L0_ffn_in['e3_down'], 'L0_ffn_e3_up': _L0_ffn_in['e3_up'], 'L0_ffn_e3_out': _L0_ffn_in['e3_out'], 'L1_attn_W_K': _L1_attn_in['W_K'], 'L1_attn_W_Q': _L1_attn_in['W_Q'], 'L1_attn_W_V': _L1_attn_in['W_V'], 'L1_attn_W_O': _L1_attn_in['W_O'], 'L1_ffn_Wg': _L1_ffn_in['Wg'], 'L1_ffn_W11': _L1_ffn_in['W11'], 'L1_ffn_W12': _L1_ffn_in['W12'], 'L1_ffn_W2': _L1_ffn_in['W2']}
    _x0 = _d['L0_attn_x']
    _d['L0_attn_x'] = jax.random.normal(jax.random.fold_in(jax.random.key(seed), 1), (2, 1024, 128), dtype=_x0.dtype)
    del _x0
    return _d

def reference(L0_attn_x, L0_attn_W_Q, L0_attn_W_KV, L0_attn_W1, L0_attn_b1, L0_attn_W2, L0_attn_b2, L0_ffn_n1_w, L0_ffn_n2_w, L0_ffn_wq, L0_ffn_wk, L0_ffn_wv, L0_ffn_wo, L0_ffn_qn_w, L0_ffn_kn_w, L0_ffn_gate_w, L0_ffn_e0_up, L0_ffn_e0_down, L0_ffn_e1_w1, L0_ffn_e1_w2, L0_ffn_e1_down, L0_ffn_e2_l1, L0_ffn_e2_l2, L0_ffn_e2_l3, L0_ffn_e2_l4, L0_ffn_e3_down, L0_ffn_e3_up, L0_ffn_e3_out, L1_attn_W_K, L1_attn_W_Q, L1_attn_W_V, L1_attn_W_O, L1_ffn_Wg, L1_ffn_W11, L1_ffn_W12, L1_ffn_W2):

    def _L0_attn_ref(x, W_Q, W_KV, W1, b1, W2, b2):
        import jax, jax.numpy as jnp
        import numpy as np
        LR = 0.001

        def _mlp(params, h):
            W1, b1, W2, b2 = params
            return jax.nn.silu(h @ W1 + b1) @ W2 + b2
        kv = x @ W_KV
        k, v = jnp.split(kv, 2, axis=-1)
        k = jnp.swapaxes(k, 0, 1)
        v = jnp.swapaxes(v, 0, 1)

        def loss_fn(params, k_t, v_t):
            return jnp.mean((_mlp(params, k_t) - v_t) ** 2)

        def step(params, kvt):
            k_t, v_t = kvt
            g = jax.grad(loss_fn)(params, k_t, v_t)
            new_params = tuple((p - LR * gp for p, gp in zip(params, g)))
            return (new_params, None)
        params, _ = jax.lax.scan(step, (W1, b1, W2, b2), (k, v))
        q = x @ W_Q
        return _mlp(params, q)

    def _L0_ffn_ref(x, n1_w, n2_w, wq, wk, wv, wo, qn_w, kn_w, gate_w, e0_up, e0_down, e1_w1, e1_w2, e1_down, e2_l1, e2_l2, e2_l3, e2_l4, e3_down, e3_up, e3_out):
        import jax, jax.numpy as jnp
        import numpy as np
        DIM = 128
        HEADS = 16
        HD = DIM // HEADS
        M = 32
        E = 4
        K = 2
        HID = 256
        MID = 256
        LB = 0.01
        EPS = 1.1920929e-07

        def _rms(x, w):
            return x * jax.lax.rsqrt(jnp.mean(x * x, axis=-1, keepdims=True) + EPS) * w

        def _gelu(x):
            return jax.nn.gelu(x, approximate=False)
        B, T, C = x.shape
        h = _rms(x, n1_w)
        heads = lambda w_: (h @ w_.T).reshape(B, T, HEADS, HD).transpose(0, 2, 1, 3)
        q = _rms(heads(wq), qn_w)
        k = _rms(heads(wk), kn_w)
        v = heads(wv)
        scores = jnp.einsum('bhqd,bhkd->bhqk', q, k) * HD ** (-0.5)
        causal = jnp.tril(jnp.ones((T, T), bool))
        scores = jnp.where(causal[None, None], scores, -jnp.inf)
        attn = jax.nn.softmax(scores, axis=-1)
        ao = jnp.einsum('bhqk,bhkd->bhqd', attn, v).transpose(0, 2, 1, 3).reshape(B, T, C) @ wo.T
        ao = ao.at[:, :, :M].set(0.0)
        x = x + ao
        xf = _rms(x, n2_w).reshape(-1, C)
        N = xf.shape[0]
        logits = jnp.nan_to_num(xf @ gate_w.T)
        probs = jax.nn.softmax(logits, axis=-1)
        topv, topi = jax.lax.top_k(probs, K)
        topv = topv / (topv.sum(-1, keepdims=True) + 1e-08)
        wts = jnp.zeros((N, E), x.dtype).at[jnp.arange(N)[:, None], topi].add(topv)
        o0 = _gelu(xf @ e0_up.T) @ e0_down.T
        o1 = jax.nn.silu(xf @ e1_w1.T) * (xf @ e1_w2.T) @ e1_down.T
        o2 = _gelu(_gelu(_gelu(xf @ e2_l1.T) @ e2_l2.T) @ e2_l3.T) @ e2_l4.T
        o3 = _gelu(_gelu(xf @ e3_down.T) @ e3_up.T) @ e3_out.T
        moe = wts[:, 0:1] * o0 + wts[:, 1:2] * o1 + wts[:, 2:3] * o2 + wts[:, 3:4] * o3
        moe = moe.reshape(B, T, C).at[:, :, :M].set(0.0)
        return x + moe

    def _L1_attn_ref(x, W_K, W_Q, W_V, W_O):
        import jax, jax.numpy as jnp
        import numpy as np
        D_MODEL, NUM_HEADS, D_HEAD, SEQ, BATCH = (128, 16, 64, 512, 1)
        B, S, D = x.shape
        d_head = W_K.shape[1]
        k = jnp.einsum('ihd,bpd->biph', W_K, x)
        q = jnp.einsum('ihd,bpd->biph', W_Q, x)
        v = jnp.einsum('ihd,bpd->biph', W_V, x)
        scores = jnp.einsum('biph,biqh->biqp', k, q)
        mask = jnp.tril(jnp.ones((S, S), dtype=x.dtype))
        scores_masked = jnp.tril(scores) - 10000000000.0 * (1.0 - mask)
        attn = jax.nn.softmax(scores_masked / np.sqrt(d_head), axis=-1)
        z = jnp.einsum('biph,biqp->biqh', v, attn)
        z_flat = jnp.transpose(z, (0, 2, 1, 3)).reshape(B, S, -1)
        out = jnp.einsum('df,bqf->bqd', W_O, z_flat)
        return out

    def _L1_ffn_ref(x, Wg, W11, W12, W2):
        import jax, jax.numpy as jnp
        import numpy as np
        B, S, H, I, E, K = (2, 256, 128, 256, 8, 2)
        gate_scores = jax.nn.softmax(x @ Wg, axis=-1)
        topk_scores, topk_idx = jax.lax.top_k(gate_scores, K)
        topk_scores = topk_scores / (topk_scores.sum(-1, keepdims=True) + 1e-08)
        gate = jnp.einsum('bsh,ehi->bsei', x, W11)
        value = jnp.einsum('bsh,ehi->bsei', x, W12)
        fused = gate * jax.nn.sigmoid(gate) * value
        expert_out = jnp.einsum('bsei,eih->bseh', fused, W2)
        gathered = jnp.take_along_axis(expert_out, topk_idx[..., None], axis=2)
        out = jnp.sum(topk_scores[..., None] * gathered, axis=2)
        return out
    x = L0_attn_x
    xn = _layernorm(x, axis=-1)
    x = x + _L0_attn_ref(xn, L0_attn_W_Q, L0_attn_W_KV, L0_attn_W1, L0_attn_b1, L0_attn_W2, L0_attn_b2) + _L0_ffn_ref(xn, L0_ffn_n1_w, L0_ffn_n2_w, L0_ffn_wq, L0_ffn_wk, L0_ffn_wv, L0_ffn_wo, L0_ffn_qn_w, L0_ffn_kn_w, L0_ffn_gate_w, L0_ffn_e0_up, L0_ffn_e0_down, L0_ffn_e1_w1, L0_ffn_e1_w2, L0_ffn_e1_down, L0_ffn_e2_l1, L0_ffn_e2_l2, L0_ffn_e2_l3, L0_ffn_e2_l4, L0_ffn_e3_down, L0_ffn_e3_up, L0_ffn_e3_out)
    xn = _layernorm(x, axis=-1)
    x = x + _L1_attn_ref(xn, L1_attn_W_K, L1_attn_W_Q, L1_attn_W_V, L1_attn_W_O) + _L1_ffn_ref(xn, L1_ffn_Wg, L1_ffn_W11, L1_ffn_W12, L1_ffn_W2)
    return x

_drawn_inputs = setup_inputs


def setup_inputs(seed=0):
    import zlib

    import numpy as np

    out = dict(_drawn_inputs(seed))
    spreads = {'L0_attn_b1': (0.0, 0.8),
     'L0_attn_b2': (0.0, 0.499),
     'L0_ffn_n1_w': (1.0, 0.6),
     'L0_ffn_n2_w': (1.0, 0.6),
     'L0_ffn_qn_w': (1.0, 0.6),
     'L0_ffn_kn_w': (1.0, 0.6)}
    factors = {'L0_attn_W_KV': 4.076,
     'L0_ffn_wq': 6.252,
     'L0_ffn_wk': 7.301,
     'L0_ffn_wv': 6.231,
     'L0_ffn_wo': 5.949,
     'L0_ffn_gate_w': 7.121,
     'L0_ffn_e0_up': 5.126,
     'L0_ffn_e0_down': 4.726,
     'L0_ffn_e1_w1': 8.0,
     'L0_ffn_e1_w2': 8.0,
     'L0_ffn_e1_down': 8.0,
     'L0_ffn_e2_l1': 8.0,
     'L0_ffn_e2_l2': 8.0,
     'L0_ffn_e2_l3': 8.0,
     'L0_ffn_e2_l4': 8.0,
     'L0_ffn_e3_down': 8.0,
     'L0_ffn_e3_up': 8.0,
     'L0_ffn_e3_out': 8.0}
    for name, (base, spread) in spreads.items():
        noise = np.random.default_rng([zlib.crc32(name.encode()), seed]).standard_normal(out[name].shape)
        drawn = base * np.exp(spread * noise) if base else spread * noise
        out[name] = jnp.asarray(drawn.astype(out[name].dtype))
    for name, factor in factors.items():
        out[name] = (out[name] * factor).astype(out[name].dtype)
    return out
```

```python
from contextlib import ExitStack

import numpy as np

import concourse.bass as bass
from concourse import mybir

F32 = mybir.dt.float32
F32R = mybir.dt.float32r
BF16 = mybir.dt.bfloat16
I32 = mybir.dt.int32
ALU = mybir.AluOpType
ACT = mybir.ActivationFunctionType
AX = mybir.AxisListType

P = 128
B, S, D = 2, 1024, 128
NT = B * S // P
TB = S // P
NC = B * S // 512
LN_EPS = 1e-5
RMS_EPS = 1.1920929e-07
MASKED = -1e30

LR = 1e-3
CS = 64
CHUNKS = S // CS
SWEEPS = 6
CONVERGED = 2.0 ** -15

H0, HD0 = 16, 8
HG = 4
QM = 24
M_ZERO = 32

H1, HD1 = 16, 64
E0, E1, HID = 4, 8, 256

W0_PARTS = [("wq_ttt", 128), ("wk_ttt", 128), ("wv_ttt", 128), ("w1", 128), ("w2", 128), ("w2t", 128),
            ("b1_rows", 128), ("b2_rows", 128), ("b1_col", 1), ("b2_col", 1), ("n1", 1), ("n2", 1),
            ("qn", 8), ("kn", 8), ("wqkv", 384), ("wo", 128), ("gate", 4),
            ("e0_up", 256), ("e0_down", 256), ("e1_w1", 256), ("e1_w2", 256), ("e1_down", 256),
            ("e2_l1", 256), ("e2_l2", 512), ("e2_l3", 512), ("e2_l4", 256),
            ("e3_down", 128), ("e3_up", 256), ("e3_out", 256)]
W1_PARTS = [("wq", H1 * HD1), ("wk", H1 * HD1), ("wv", H1 * HD1), ("wo", H1 * HD1), ("gate", E1),
            ("w11", E1 * HID), ("w12", E1 * HID), ("w2", E1 * HID)]


def offsets(parts):
    at, out = 0, {}
    for name, n in parts:
        out[name] = (at, at + n)
        at += n
    return out, at


W0_AT, W0_N = offsets(W0_PARTS)
W1_AT, W1_N = offsets(W1_PARTS)


class Steps:

    def __init__(self, sem, names):
        self.sem, self.names = sem, list(names)
        self.per_trip = len(self.names)
        self.index = {n: i + 1 for i, n in enumerate(self.names)}

    def at(self, name, trip, back=0):
        return trip * self.per_trip + (self.index[name] + self.per_trip * (1 - back))


def program(nc, x_in, w0_in, w1_in, out):
    with ExitStack() as ctx:
        def sb(name, shape, dt=F32):
            return ctx.enter_context(nc.sbuf_tensor(name, shape, dt))

        def sem(name):
            return ctx.enter_context(nc.semaphore(name))

        PS = ctx.enter_context(nc.psum_tensor("PS", [P, 8, 512], F32))
        X = sb("X", [P, NT, D])
        XN = sb("XN", [P, NT, D])
        XT = sb("XT", [P, B * S])
        W0 = sb("W0", [P, W0_N])
        W1 = sb("W1", [P, W1_N])
        ident = sb("ident", [P, P])
        ident_b = sb("ident_b", [P, P], BF16)
        mask_qk = sb("mask_qk", [P, P], BF16)
        mask_kq = sb("mask_kq", [P, P], BF16)
        lr_mask = sb("lr_mask", [P, P])
        lr_mask_h = sb("lr_mask_h", [P, P])
        ones = sb("ones", [P, P])
        eps = sb("eps", [P, 2])
        stats = sb("stats", [P, NT, 6])
        mv = sb("mv", [P, NT, 2])
        sd = sb("sd", [P, NT])
        rstd = sb("rstd", [P, NT])
        ssq = sb("ssq", [P, NT])
        rms_sd = sb("rms_sd", [P, NT])
        rms_r = sb("rms_r", [P, NT])
        junk = sb("junk", [P, D])

        xc = sb("xc", [P, 2, CS])
        kv = sb("kv", [P, 4, P])
        vb = sb("vb", [P, 2, P])
        g1 = sb("g1", [P, P])
        g2 = sb("g2", [P, P])
        g3 = sb("g3", [P, P])
        zb = sb("zb", [P, 2, P])
        zh = sb("zh", [P, 2, P])
        th = sb("th", [P, 2, P])
        sl = sb("sl", [P, 2, P])
        du = sb("du", [P, P])
        dd = sb("dd", [P, P])
        gr = sb("gr", [P, 2, 3, P])
        STN = 3 * P + 2 * P + 2
        st = sb("st", [P, STN])
        st0 = sb("st0", [P, STN])
        cdiff = sb("cdiff", [P, 2, P])
        cin = sb("cin", [P, 2, 2, P])
        cmax = sb("cmax", [P, 2])
        cok = sb("cok", [P, 1])
        okay = sb("okay", [P, 1])
        flag_f = sb("flag_f", [1, 1])
        flag_i = sb("flag_i", [1, 1], I32)
        ST_W1, ST_W2, ST_W2T = st[:, 0:P], st[:, P:2 * P], st[:, 2 * P:3 * P]
        ST_B1, ST_B2 = st[:, 3 * P:4 * P], st[:, 4 * P:5 * P]
        ST_B1C, ST_B2C = st[:, 5 * P:5 * P + 1], st[:, 5 * P + 1:5 * P + 2]

        arena = sb("arena", [P, 15360])
        taken = [0]

        def area(n):
            taken[0] += n
            assert taken[0] <= 15360, taken
            return arena[:, taken[0] - n:taken[0]]

        QKV = area(NT * 3 * D).rearrange("p (t n) -> p t n", t=NT)
        LO = area(NT * 2 * D).rearrange("p (t n) -> p t n", t=NT)
        tmq = area(TB * P).rearrange("p (t n) -> p t n", t=TB)
        tmk = area(TB * P).rearrange("p (t n) -> p t n", t=TB)
        tmv = area(TB * P).rearrange("p (t n) -> p t n", t=TB)
        Z0 = area(NT * D).rearrange("p (t n) -> p t n", t=NT)
        taken[0] = 0
        Z0T = area(B * S)
        taken[0] = 0
        hid = area(15 * 512).rearrange("p (u n) -> p u n", u=15)
        e1t = area(2 * 512).rearrange("p (u n) -> p u n", u=2)
        taken[0] = 0
        QH = area(2 * S).rearrange("p (h n) -> p h n", h=2)
        KH = area(2 * S).rearrange("p (h n) -> p h n", h=2)
        VH = area(2 * TB * P).rearrange("p (h t n) -> p h t n", h=2, t=TB)
        ZT = area(2 * S).rearrange("p (b n) -> p b n", b=2)
        wqk_s = area(2 * P).rearrange("p (a n) -> p a n", a=2)
        RC = area(2 * 512).rearrange("p (h n) -> p h n", h=2)
        NM = area(2 * TB).rearrange("p (h t) -> p h t", h=2)
        w11_s = area(2 * HID).rearrange("p (a n) -> p a n", a=2)
        w12_s = area(2 * HID).rearrange("p (a n) -> p a n", a=2)
        GS = area(3 * 512).rearrange("p (u n) -> p u n", u=3)
        HB = area(4 * 512).rearrange("p (m u n) -> p m u n", m=2, u=2)

        qta = sb("qta", [P, S], F32R)
        qtb = sb("qtb", [P, S], F32R)
        kta = sb("kta", [P, S], F32R)
        pe_ = sb("pe_", [P, 4, 2, 512])
        HI = pe_[:, :, :, :].rearrange("p h m n -> p (h m n)").rearrange("p (t n) -> p t n", t=NT)
        QZT, hq = pe_[:, 0, :, :], pe_[:, 1, :, :]
        ots = sb("ots", [P, 2, 512])
        rz = sb("rz", [P, 2, 16])
        hss, hsd = ots[:, 0, :], ots[:, 1, :]
        wqkv_n = sb("wqkv_n", [P, 3 * D])

        lg = sb("lg", [P, NT, 8])
        lgm = sb("lgm", [P, NT, 8], I32)
        lgx = sb("lgx", [P, NT])
        ge = sb("ge", [P, NT, 8])
        gp = sb("gp", [P, NT, 8])
        gc = ots[:, :, :].rearrange("p a n -> p (a n)").rearrange("p (f n) -> p f n", f=8)
        rank = sb("rank", [P, NT, 8])
        wt0 = sb("wt0", [P, E0, NT])
        wt1 = sb("wt1", [P, E1, NT])
        wsum = sb("wsum", [P, NT])

        def w0(name, lo=0, hi=None):
            a, b = W0_AT[name]
            return W0[:, a + lo:(b if hi is None else a + hi)]

        def w1(name, lo=0, hi=None):
            a, b = W1_AT[name]
            return W1[:, a + lo:(b if hi is None else a + hi)]

        x_loaded, w0_loaded, w1_loaded = sem("x_loaded"), sem("w0_loaded"), sem("w1_loaded")
        const_ready = sem("const_ready")
        stored = sem("stored")
        dve_chain, act_chain, pool_chain = sem("dve_chain"), sem("act_chain"), sem("pool_chain")
        N_CONST = 1


        class Ttt:
            def __init__(self, tag, sweeps, checked):
                self.trips, self.sweeps, self.checked = sweeps // 2, sweeps, checked
                self.staged = sem(f"ttt_{tag}_chunk_staged")
                self.mm = sem(f"ttt_{tag}_products")
                self.ew = sem(f"ttt_{tag}_elementwise")
                self.th = sem(f"ttt_{tag}_tanh")
                self.pe0, self.pes, self.pe1 = ["kv", "base"], ["zc", "ys", "yc", "ds", "dc"], ["up"]
                self.dv0 = ["vbt", "vb", "g1", "zbt", "zb", "zero"]
                self.dvs = ["z", "s", "g2", "u", "d", "dy", "g3", "dz"]
                self.dv1 = (["cd", "cm", "ct", "cp", "cn", "cr", "ck"] if checked else []) + ["w", "b1", "b2", "b1c", "b2c"]
                self.tm = len(self.pe0) + sweeps * len(self.pes) + len(self.pe1)
                self.td = len(self.dv0) + sweeps * len(self.dvs) + len(self.dv1)
                self.ta = 1 + sweeps

            def pe(self, chunk, name, sweep=None):
                if name in self.pe0:
                    return chunk * self.tm + (2 + self.pe0.index(name))
                if name in self.pes:
                    return chunk * self.tm + sweep * len(self.pes) + (2 + len(self.pe0) + self.pes.index(name))
                return (chunk + 1) * self.tm + 1

            def dv(self, chunk, name, sweep=None):
                if name in self.dv0:
                    return chunk * self.td + (2 + self.dv0.index(name))
                if name in self.dvs:
                    return chunk * self.td + sweep * len(self.dvs) + (2 + len(self.dv0) + self.dvs.index(name))
                return chunk * self.td + (2 + len(self.dv0) + self.sweeps * len(self.dvs) + self.dv1.index(name))

            def dv_before(self, chunk, sweep):
                return chunk * self.td + sweep * len(self.dvs) + (1 + len(self.dv0))

            def ac(self, chunk, sweep=None):
                return chunk * self.ta + (2 if sweep is None else sweep + 3)

        ttt_fast = Ttt("fast", SWEEPS, True)
        ttt_full = Ttt("full", CS, False)
        ttt_credit = sem("ttt_credit")
        ttt_okay, ttt_sum, ttt_flag, ttt_reset, ttt_settled = (
            sem("ttt_okay"), sem("ttt_okay_summed"), sem("ttt_flag_ready"), sem("ttt_state_reset"),
            sem("ttt_settled"))

        SWEEP_B = [(c, j) for c in range(2) for j in range(4 * c + 4)]
        NB = len(SWEEP_B)
        LAST = [3, NB - 1]
        pe_names = ["tq", "tk"] + [("a", h, i) for h in range(HG) for i in range(TB)] + ["tq2"]
        for n in range(NB + 1):
            if n < NB:
                pe_names += [("st", n, h) for h in range(HG)]
            if n >= 1:
                pe_names += [("pv", n - 1)]
            if n == 7:
                pe_names += [("to", 0)]
        pe_names += [("to", 1)]
        a0_pe = Steps(sem("a0_products"), pe_names)
        a0_act = Steps(sem("a0_scalar"), ["qa", "qb"] + [("ex", n, h) for n in range(NB) for h in range(HG)])
        a0_dve = Steps(sem("a0_vector"), ["ka"] + [("mx", h, i) for h in range(HG) for i in range(TB)]
                       + [(k, c) for c in range(2) for k in ("oc", "rc", "zt")])
        a0_pool = Steps(sem("a0_staged"), ["k", "q", "v"])

        units = []

        def unit(name, blocks, rhs, then, dst):
            units.append((name, blocks, rhs, then, dst))

        HU = {}

        def slot(name):
            HU.setdefault(name, len(HU))
            return HU[name]

        def layer(tag, wname, k_blocks, m_blocks, src, then):
            for m in range(m_blocks):
                blocks = [w0(wname, kb * 128 * m_blocks + m * 128, kb * 128 * m_blocks + m * 128 + 128)
                          for kb in range(k_blocks)]
                rhs = [None] * k_blocks if src is None else [slot((src, kb)) for kb in range(k_blocks)]
                unit((tag, m), blocks, rhs, then, slot((tag, m)) if then != "none" else None)

        order0 = []
        layer("e0h", "e0_up", 1, 2, None, "gelu")
        layer("e1g", "e1_w1", 1, 2, None, "silu")
        layer("e1v", "e1_w2", 1, 2, None, "times")
        layer("e2a", "e2_l1", 1, 2, None, "gelu")
        layer("e3a", "e3_down", 1, 1, None, "gelu")
        layer("e2b", "e2_l2", 2, 2, "e2a", "gelu")
        layer("e3b", "e3_up", 1, 2, "e3a", "gelu")
        layer("e2c", "e2_l3", 2, 2, "e2b", "gelu")
        assert len(units) == 15 and len(HU) == 15
        seq0 = []
        for u, spec in enumerate(units):
            seq0.append(("u", u))
            if spec[0] == ("e2b", 1):
                seq0.append(("dn", 0))
            if spec[0] == ("e3b", 1):
                seq0.append(("dn", 1))
        seq0 += [("dn", 3), ("dn", 2)]
        DOWN = {0: ("e0_down", "e0h"), 1: ("e1_down", "e1v"), 2: ("e2_l4", "e2c"), 3: ("e3_out", "e3b")}
        dn_order = [s[1] for s in seq0 if s[0] == "dn"]
        m0_pe = Steps(sem("m0_products"), seq0)
        m0_act = Steps(sem("m0_scalar"), [("u", u) for u, s in enumerate(units) if s[3] in ("gelu", "silu")])
        dve0 = []
        for kind, u in seq0:
            if kind == "u" and units[u][3] == "silu":
                dve0.append(("sg", u))
            elif kind == "u" and units[u][3] == "times":
                dve0.append(("tm", u))
            elif kind == "dn":
                dve0 += [("ac", u, i) for i in range(4)]
        m0_dve = Steps(sem("m0_vector"), dve0)

        def unit_freed(u):
            then = units[u][3]
            return (m0_act, ("u", u)) if then == "gelu" else (m0_dve, ("sg", u) if then == "silu" else ("tm", u))

        pe1, act1, dve1 = [], [], []
        for b in range(B):
            pe1 += [("qp", b), ("kp", b), ("vp", b)] + ([("wo", 0)] if b else [])
            pe1 += [("a", b, h, i) for h in range(2) for i in range(TB)] + [("mr", b, 0), ("mr", b, 1)]
            for n in range(NB + 1):
                if n < NB:
                    pe1 += [("st", b, n, h) for h in range(2)]
                if n >= 1:
                    pe1 += [("pv", b, n - 1, h) for h in range(2)]
            act1 += [("qe", b, 0), ("qe", b, 1), ("ve", b, 0), ("ve", b, 1), ("me", b, 0), ("me", b, 1)]
            act1 += [("ex", b, n, h) for n in range(NB) for h in range(2)]
            dve1 += [("ke", b, 0), ("ke", b, 1)] + ([("xa", 0, 0), ("xa", 0, 1)] if b else [])
            dve1 += [("mx", b, h, i) for h in range(2) for i in range(TB)]
            dve1 += [(k, b, c, h) for c in range(2) for h in range(2) for k in ("rc", "zt")]
        pe1 += [("wo", 1)]
        dve1 += [("xa", 1, 0), ("xa", 1, 1)]
        a1_pe = Steps(sem("a1_products"), pe1)
        a1_act = Steps(sem("a1_scalar"), act1)
        a1_dve = Steps(sem("a1_vector"), dve1)
        a1_pool = Steps(sem("a1_staged"), ["w"])

        NM1 = 2 * NC
        m1pe, m1dve = [], []
        for m in range(NM1 + 1):
            if m < NM1:
                m1pe += [("u", 2 * m), ("u", 2 * m + 1)]
                m1dve += [("mu", 2 * m), ("mu", 2 * m + 1)]
            if m >= 1:
                m1pe += [("dn", m - 1)]
                m1dve += [("ac", m - 1, i) for i in range(4)]
        m1_pe = Steps(sem("m1_products"), m1pe)
        m1_act = Steps(sem("m1_silu"), [("u", u) for u in range(2 * NM1)])
        m1_dve = Steps(sem("m1_vector"), m1dve)
        m1_pool = Steps(sem("m1_staged"), ["w0", "w1"])

        def two(name):
            return sem(name + "_0"), sem(name + "_1")

        ln_var, ln_sd, ln_done, xt_ps, xt_done = (two("ln_var"), two("ln_sd"), two("ln_tile"), two("xt_turned"),
                                                  two("xt_copied"))
        rms_ss, rms_sq = two("rms_sum"), two("rms_root")
        qkv_w, qkv_ps, qkv_done, hsq, hsum, hroot, hnorm, hhi, hlo = (
            sem("qkv_weights"), sem("qkv_products"), sem("qkv_copied"), sem("head_squares"), sem("head_sums"),
            sem("head_roots"), sem("head_normed"), sem("head_high"), sem("head_low"))
        tq_q, tq_z, tq_y, tq_qc, tq_th, tq_s, tq_acc = (
            sem("ttt_q_product"), sem("ttt_hidden_product"), sem("ttt_out_product"), sem("ttt_q_copied"),
            sem("ttt_out_tanh"), sem("ttt_out_silu"), sem("ttt_out_added"))
        z0_ps, z0_cp, ao_ps, ao_add, xf_tile, xf_ps, xf_cp = (
            sem("z0_turned"), sem("z0_copied"), sem("ao_products"), sem("ao_added"), sem("xf_tile"),
            sem("xf_turned"), sem("xf_copied"))
        gl_ps, gl_sub, gl_exp, gl_done = two("gate_logits"), two("gate_shifted"), two("gate_exp"), two("gate_done")
        a0_zero, a1_ones = sem("a0_stacks_cleared"), sem("a1_ones_set")
        x_plus = sem("residual_added")

        def wait(e, steps, name, trip, back=0):
            e.wait_ge(steps.sem, steps.at(name, trip, back))

        def tiles(ap, t, n=1):
            return ap[:, bass.ds(t, n), :]

        block = ctx.enter_context(nc.Block())

        @block.sync
        def _(sp):
            xs = x_in.rearrange("(t p) d -> p t d", p=P)
            sp.dma_start(X[:, 0:TB, :], xs[:, 0:TB, :]).then_inc(x_loaded, 16)
            sp.dma_start(X[:, TB:NT, :], xs[:, TB:NT, :]).then_inc(x_loaded, 16)
            sp.dma_start(W0[:, :], w0_in).then_inc(w0_loaded, 16)
            sp.dma_start(W1[:, :], w1_in).then_inc(w1_loaded, 16)
            sp.wait_ge(m1_dve.sem, m1_dve.at(("ac", NM1 - 1, 3), E1 // 2 - 1))
            sp.dma_start(out.rearrange("(t p) d -> p t d", p=P), X[:, :, :]).then_inc(stored, 16)
            sp.wait_ge(stored, 16)

        @block.gpsimd
        def _(pool):
            count = [0]

            def link(ins):
                count[0] += 1
                ins.then_inc(pool_chain, 1)
                pool.wait_ge(pool_chain, count[0])

            for m in (ident, ident_b):
                link(pool.memset(m[:, :], 0.0))
                link(pool.affine_select(out=m[:, :], in_=m[:, :], compare_op=ALU.not_equal, fill=1.0, base=0,
                                        pattern=[[-1, P]], channel_multiplier=1))
            for m, sign in ((mask_qk, 1), (mask_kq, -1)):
                link(pool.memset(m[:, :], 0.0))
                link(pool.affine_select(out=m[:, :], in_=m[:, :], compare_op=ALU.is_ge, fill=MASKED, base=0,
                                        pattern=[[-sign, P]], channel_multiplier=sign))
            for m, v in ((lr_mask, -LR), (lr_mask_h, -LR / 2)):
                link(pool.memset(m[:, :], v))
                for half in range(2):
                    rows = m[half * CS:(half + 1) * CS, :].rearrange("p (b s) -> p b s", b=2)
                    link(pool.affine_select(out=rows, in_=rows, compare_op=ALU.is_ge, fill=0.0, base=-1,
                                            pattern=[[0, 2], [1, CS]], channel_multiplier=-1))
            link(pool.memset(ones[:, :], 1.0))
            link(pool.memset(eps[:, 0:1], LN_EPS))
            link(pool.memset(eps[:, 1:2], RMS_EPS))
            link(pool.memset(okay[:, :], 1.0))
            for tm, at in ((tmk, QM), (tmv, HD0)):
                link(pool.memset(tm, 0.0))
                link(pool.memset(tm.rearrange("p t (h n) -> p t h n", h=HG)[:, :, :, at:at + 1], 1.0))
            pool.memset(tmq, 0.0).then_inc(const_ready, 1)
            pool.wait_ge(const_ready, N_CONST)

            def ttt(run):
                with pool.Fori(0, CHUNKS) as c:
                    pool.wait_ge(run.mm, c * run.tm + 1)
                    src = XT[:, :].rearrange("p (b s) -> p b s", b=B)[:, :, bass.ts(c, CS)]
                    pool.tensor_copy(xc[:, :, :], src).then_inc(run.staged, 1)

            pool.wait_ge(xt_done[0], NC)
            ttt(ttt_fast)
            pool.wait_ge(ttt_flag, 1)
            settled = pool.value_load(flag_i[0:1, 0:1], min_val=0, max_val=1)
            with pool.If(settled == 0):
                ttt(ttt_full)
            with pool.Else():
                pool.nop()

            pool.wait_ge(hlo, 1)
            with pool.Fori(0, B) as b:
                with pool.Fori(0, H0 // HG) as g:
                    trip = b * (H0 // HG) + g

                    def heads(ap, off):
                        v = ap[:, bass.ts(b, TB), bass.ds(g * (HG * HD0) + off, HG * HD0)]
                        return v.rearrange("p t (h e) -> p t h e", h=HG)

                    def put(tm, at):
                        return tm.rearrange("p t (h n) -> p t h n", h=HG)[:, :, :, at:at + HD0]

                    wait(pool, a0_pe, "tk", trip, 1)
                    pool.tensor_copy(put(tmk, 0), heads(QKV, D))
                    pool.tensor_copy(put(tmk, HD0), heads(LO, D))
                    pool.tensor_copy(put(tmk, 2 * HD0), heads(QKV, D)).then_inc(a0_pool.sem, 1)
                    wait(pool, a0_pe, "tq2", trip, 1)
                    pool.tensor_copy(put(tmq, 0), heads(QKV, 0))
                    pool.tensor_copy(put(tmq, HD0), heads(QKV, 0))
                    pool.tensor_copy(put(tmq, 2 * HD0), heads(LO, 0))
                    pool.memset(tmq.rearrange("p t (h n) -> p t h n", h=HG)[:, :, :, QM:QM + 1], 0.0)\
                        .then_inc(a0_pool.sem, 1)
                    wait(pool, a0_pe, ("pv", NB - 1), trip, 1)
                    pool.tensor_copy(put(tmv, 0), heads(QKV, 2 * D)).then_inc(a0_pool.sem, 1)

            pool.wait_ge(m0_pe.sem, m0_pe.at(seq0[-1], NC - 1))
            pool.wait_ge(m0_dve.sem, m0_dve.at(dve0[-1], NC - 1))
            link(pool.memset(VH[:, :, :, HD1:P], 1.0))
            pool.memset(KH[HD1:HD1 + 1, :, :], 1.0).then_inc(a1_ones, 1)
            pool.wait_ge(a1_ones, 1)
            pool.wait_ge(w1_loaded, 16)
            with pool.Fori(0, H1 // 2) as hp:
                wait(pool, a1_pe, ("kp", 1), hp, 1)
                for a, name in enumerate(("wq", "wk")):
                    at = W1_AT[name][0]
                    ins = pool.tensor_copy(wqk_s[:, a, :], W1[:, bass.ds(hp * P + at, P)])
                ins.then_inc(a1_pool.sem, 1)
            pool.wait_ge(a1_pe.sem, a1_pe.at(("wo", 1), H1 // 2 - 1))
            with pool.Fori(0, E1 // 2) as ep:
                for k in range(2):
                    wait(pool, m1_pe, ("u", NM1 * (k + 1) - 1), ep, 1)
                    for dst, name in ((w11_s, "w11"), (w12_s, "w12")):
                        at = W1_AT[name][0] + k * HID
                        ins = pool.tensor_copy(dst[:, k, :], W1[:, bass.ds(ep * (2 * HID) + at, HID)])
                    ins.then_inc(m1_pool.sem, 1)

        @block.scalar
        def _(act):
            act.sem_inc(a0_act.sem, a0_act.per_trip)
            act.sem_inc(m0_act.sem, m0_act.per_trip)
            act.sem_inc(a1_act.sem, a1_act.per_trip)
            act.sem_inc(m1_act.sem, m1_act.per_trip)
            act.sem_inc(ttt_fast.th, 1)
            act.sem_inc(ttt_full.th, 1)
            act.wait_ge(const_ready, N_CONST)

            def norm(layer):
                act.wait_ge(ln_var[layer], NT)
                act.activation(sd[:, :], mv[:, :, 1], ACT.Sqrt, bias=eps[:, 0:1]).then_inc(ln_sd[layer], 1)
                for c in range(NC):
                    act.wait_ge(xt_ps[layer], c + 1)
                    act.copy(XT[:, c * 512:(c + 1) * 512], PS[:, c, :]).then_inc(xt_done[layer], 1)

            norm(0)
            act.wait_ge(rms_ss[0], NT)
            act.activation(rms_sd[:, :], ssq[:, :], ACT.Sqrt, bias=eps[:, 1:2], scale=1.0 / D)\
                .then_inc(rms_sq[0], 1)
            act.wait_ge(ln_done[0], NT + 1)
            for t in range(NT):
                act.wait_ge(qkv_ps, t + 1)
                act.activation(QKV[:, t, :], PS[:, 4 + t % 4, 0:3 * D], ACT.Copy, scale=rms_r[:, t:t + 1])\
                    .then_inc(qkv_done, 1)
            act.wait_ge(qkv_done, NT)
            act.activation(LO, QKV[:, :, 0:2 * D], ACT.Square).then_inc(hsq, 1)
            act.wait_ge(hsum, 1)
            act.activation(hsd, hss, ACT.Sqrt, bias=eps[:, 1:2], scale=1.0 / HD0).then_inc(hroot, 1)
            act.wait_ge(hnorm, 1)
            act.copy(HI.bitcast(F32R), QKV[:, :, 0:2 * D]).then_inc(hhi, 1)

            def ttt(run):
                with act.Fori(0, CHUNKS) as c:
                    act.wait_ge(run.mm, run.pe(c, "kv"))
                    act.copy(kv[:, :, :], PS[:, 0, :].rearrange("p (a n) -> p a n", a=4)).then_inc(run.th, 1)
                    with act.Fori(0, run.trips) as trip:
                        for par in range(2):
                            sweep = trip * 2 + par
                            act.wait_ge(run.ew, run.dv(c, "z", sweep))
                            act.activation(th[:, :, :], zh[:, :, :], ACT.Tanh).then_inc(run.th, 1)

            ttt(ttt_fast)
            act.wait_ge(ttt_flag, 1)
            settled = act.value_load(flag_i[0:1, 0:1], min_val=0, max_val=1)
            with act.If(settled == 0):
                ttt(ttt_full)
            with act.Else():
                act.nop()

            for c in range(NC):
                act.wait_ge(tq_q, c + 1)
                act.copy(QZT[:, 0, :], PS[:, 0, :]).then_inc(tq_qc, 1)
                if c:
                    act.wait_ge(tq_s, c)
                act.wait_ge(tq_z, c + 1)
                act.activation(hq[:, 0, :], PS[:, 1, :], ACT.Identity, bias=ST_B1C).then_inc(tq_th, 1)
                act.wait_ge(tq_th, 2 * c + 1)
                act.activation(hq[:, 1, :], hq[:, 0, :], ACT.Tanh, scale=0.5).then_inc(tq_th, 1)

            with act.Fori(0, B * H0 // HG) as trip:
                wait(act, a0_pe, "tq", trip)
                act.copy(qta[:, :], PS[:, 4:6, :].rearrange("p a n -> p (a n)")).then_inc(a0_act.sem, 1)
                wait(act, a0_pe, "tq2", trip)
                act.copy(qtb[:, :], PS[:, 4:6, :].rearrange("p a n -> p (a n)")).then_inc(a0_act.sem, 1)
                for n, (c, j) in enumerate(SWEEP_B):
                    w = 512 * (c + 1) - max(512 * c, P * j)
                    for h in range(HG):
                        wait(act, a0_pe, ("st", n, h), trip)
                        if n >= 2:
                            wait(act, a0_pe, ("pv", n - 2), trip)
                        act.activation(pe_[:, h, n % 2, 0:w], PS[:, h, 0:w], ACT.Exp, scale=HD0 ** -0.5)\
                            .then_inc(a0_act.sem, 1)

            for c in range(NC):
                act.wait_ge(z0_ps, c + 1)
                act.copy(Z0T[:, c * 512:(c + 1) * 512], PS[:, c, :]).then_inc(z0_cp, 1)
            act.wait_ge(rms_ss[1], NT)
            act.activation(rms_sd[:, :], ssq[:, :], ACT.Sqrt, bias=eps[:, 1:2], scale=1.0 / D)\
                .then_inc(rms_sq[1], 1)
            for c in range(NC):
                act.wait_ge(xf_ps, c + 1)
                act.activation(XT[:, c * 512:(c + 1) * 512], PS[:, c, :], ACT.Copy, scale=w0("n2"))\
                    .then_inc(xf_cp, 1)

            def gate(layer, experts):
                act.wait_ge(gl_sub[layer], 1)
                act.activation(ge[:, :, 0:experts], lg[:, :, 0:experts], ACT.Exp).then_inc(gl_exp[layer], 1)

            gate(0, E0)

            with act.Fori(0, NC) as c:
                for u, (name, _, _, then, dst) in enumerate(units):
                    if then not in ("gelu", "silu"):
                        continue
                    wait(act, m0_pe, ("u", u), c)
                    if then == "gelu":
                        act.activation(hid[:, dst, :], PS[:, u % 6, :], ACT.Gelu).then_inc(m0_act.sem, 1)
                    else:
                        act.activation(e1t[:, name[1], :], PS[:, u % 6, :], ACT.Tanh, scale=0.5)\
                            .then_inc(m0_act.sem, 1)

            norm(1)
            gate(1, E1)

            with act.Fori(0, H1 // 2) as hp:
                for b in range(B):
                    for h in range(2):
                        wait(act, a1_pe, ("qp", b), hp)
                        act.copy(QH[0:HD1, h, :], PS[h * HD1:(h + 1) * HD1, 4:6, :].rearrange("p a n -> p (a n)"))\
                            .then_inc(a1_act.sem, 1)
                    wait(act, a1_pe, ("vp", b), hp)
                    for half in range(2):
                        act.copy(VH[:, :, 4 * half:4 * half + 4, 0:HD1],
                                 PS[:, half, :].rearrange("p (t h n) -> p h t n", t=4, h=2))\
                            .then_inc(a1_act.sem, 1)
                    for h in range(2):
                        wait(act, a1_pe, ("mr", b, h), hp)
                        act.copy(QH[HD1:HD1 + 1, h, :],
                                 PS[0:1, 4 + 2 * h:6 + 2 * h, :].rearrange("p a n -> p (a n)"))\
                            .then_inc(a1_act.sem, 1)
                    for n, (c, j) in enumerate(SWEEP_B):
                        w = 512 * (c + 1) - max(512 * c, P * j)
                        for h in range(2):
                            wait(act, a1_pe, ("st", b, n, h), hp)
                            if n >= 2:
                                wait(act, a1_pe, ("pv", b, n - 2, h), hp)
                            act.activation(pe_[:, h, n % 2, 0:w], PS[:, (2 * n + h) % 4, 0:w], ACT.Exp,
                                           scale=HD1 ** -0.5).then_inc(a1_act.sem, 1)

            with act.Fori(0, E1 // 2) as ep:
                for u in range(2 * NM1):
                    wait(act, m1_pe, ("u", u), ep)
                    if u >= 3:
                        wait(act, m1_dve, ("mu", u - 3), ep)
                    else:
                        wait(act, m1_dve, ("mu", max(v for v in range(2 * NM1) if v % 3 == u)), ep, 1)
                    act.activation(GS[:, u % 3, :], PS[:, 2 * (u % 3), :], ACT.Silu).then_inc(m1_act.sem, 1)

        @block.vector
        def _(dve):
            count = [0]

            def link(ins):
                count[0] += 1
                ins.then_inc(dve_chain, 1)
                dve.wait_ge(dve_chain, count[0])

            for s in (a0_dve, m0_dve, a1_dve, m1_dve):
                dve.sem_inc(s.sem, s.per_trip)
            dve.sem_inc(ttt_fast.ew, 1)
            dve.sem_inc(ttt_full.ew, 1)
            dve.wait_ge(const_ready, N_CONST)

            def norm(layer):
                for t in range(NT):
                    if layer == 0:
                        dve.wait_ge(x_loaded, 32)
                    link(dve.bn_stats(stats[:, t, :], X[:, t, :]))
                    dve.bn_aggr(mv[:, t, :], stats[:, t, :]).then_inc(ln_var[layer], 1)
                dve.wait_ge(ln_sd[layer], 1)
                link(dve.reciprocal(rstd[:, :], sd[:, :]))
                for t in range(NT):
                    dve.tensor_scalar(XN[:, t, :], X[:, t, :], mv[:, t, 0:1], rstd[:, t:t + 1], ALU.subtract,
                                      ALU.mult).then_inc(ln_done[layer], 1)
                dve.wait_ge(ln_done[layer], NT)

            def rms(which):
                for t in range(NT):
                    if t:
                        dve.wait_ge(rms_ss[which], t)
                    dve.tensor_tensor_reduce(junk[:, :], XN[:, t, :], XN[:, t, :], 1.0, 0.0, ALU.mult, ALU.add,
                                             ssq[:, t:t + 1]).then_inc(rms_ss[which], 1)
                dve.wait_ge(rms_sq[which], 1)

            norm(0)
            rms(0)
            dve.reciprocal(rms_r[:, :], rms_sd[:, :]).then_inc(ln_done[0], 1)
            dve.wait_ge(w0_loaded, 16)
            dve.tensor_scalar(wqkv_n[:, :], w0("wqkv"), w0("n1"), None, ALU.mult).then_inc(qkv_w, 1)
            a, b_ = W0_AT["w1"][0], W0_AT["w2t"][1]
            dve.tensor_copy(st0[:, 0:3 * P], W0[:, a:b_])
            dve.tensor_scalar(st0[:, 3 * P:4 * P], w0("b1_rows"), 0.5, None, ALU.mult)
            dve.tensor_scalar(st0[:, 4 * P:5 * P], w0("b2_rows"), 1.0 / D, None, ALU.mult)
            dve.tensor_copy(st0[:, 5 * P:5 * P + 1], w0("b1_col"))
            link(dve.tensor_scalar(st0[:, 5 * P + 1:5 * P + 2], w0("b2_col"), 1.0 / D, None, ALU.mult))
            link(dve.tensor_copy(st[:, :], st0[:, :]))
            dve.wait_ge(hsq, 1)
            dve.tensor_reduce(hss.rearrange("p (t h) -> p t h", t=NT),
                              LO.rearrange("p t (h e) -> p t h e", e=HD0), AX.X, ALU.add).then_inc(hsum, 1)
            dve.wait_ge(hroot, 1)
            link(dve.reciprocal(hss, hsd))
            qk4 = QKV[:, :, 0:2 * D].rearrange("p t (h e) -> p t h e", e=HD0)
            link(dve.tensor_tensor(qk4, qk4, hss.rearrange("p (t h) -> p t h", t=NT).unsqueeze(3)
                                   .broadcast_to([P, NT, 32, HD0]), ALU.mult))
            for a, name in enumerate(("qn", "kn")):
                part = QKV[:, :, a * D:(a + 1) * D].rearrange("p t (h e) -> p t h e", e=HD0)
                ins = dve.tensor_tensor(part, part, w0(name).unsqueeze(1).unsqueeze(1)
                                        .broadcast_to([P, NT, H0, HD0]), ALU.mult)
                if a == 0:
                    link(ins)
            ins.then_inc(hnorm, 1)
            dve.wait_ge(hhi, 1)
            dve.tensor_tensor(LO, QKV[:, :, 0:2 * D], HI, ALU.subtract).then_inc(hlo, 1)

            def ttt(run):
                n = P // 2
                with dve.Fori(0, CHUNKS) as c:
                    dve.wait_ge(run.th, run.ac(c))
                    dve.tensor_scalar(vb[:, 0, :], kv[:, 2, :], 1.0 / D, ST_B2C, ALU.mult, ALU.subtract)\
                        .then_inc(run.ew, 1)
                    dve.scalar_tensor_tensor(vb[:, 1, :], kv[:, 3, :], 1.0 / D, ST_B2, ALU.mult,
                                             ALU.subtract).then_inc(run.ew, 1)
                    dve.wait_ge(run.mm, run.pe(c, "base"))
                    dve.scalar_tensor_tensor(g1[:, :], PS[:, 1, 0:P], 1.0, lr_mask_h[:, :], ALU.add, ALU.mult)\
                        .then_inc(run.ew, 1)
                    dve.tensor_scalar(zb[:, 0, :], PS[:, 1, P:2 * P], ST_B1C, 0.5, ALU.add, ALU.mult)\
                        .then_inc(run.ew, 1)
                    dve.scalar_tensor_tensor(zb[:, 1, :], PS[:, 1, 2 * P:3 * P], 0.5, ST_B1, ALU.mult, ALU.add)\
                        .then_inc(run.ew, 1)
                    dve.memset(gr[:, 1, :, :], 0.0).then_inc(run.ew, 1)
                    with dve.Fori(0, run.trips) as trip:
                        for par in range(2):
                            sweep = trip * 2 + par
                            dve.wait_ge(run.mm, run.pe(c, "zc", sweep))
                            dve.wait_ge(run.ew, run.dv_before(c, sweep))
                            dve.tensor_tensor(zh[:, :, :], PS[:, 0, 0:2 * P].rearrange("p (a n) -> p a n", a=2),
                                              zb[:, :, :], ALU.add).then_inc(run.ew, 1)
                            dve.wait_ge(run.th, run.ac(c, sweep))
                            dve.scalar_tensor_tensor(sl[:, :, :], th[:, :, :], 1.0, zh[:, :, :], ALU.add, ALU.mult)\
                                .then_inc(run.ew, 1)
                            dve.wait_ge(run.mm, run.pe(c, "ys", sweep))
                            dve.scalar_tensor_tensor(g2[:, :], PS[:, 0, 2 * P:3 * P], 1.0, lr_mask[:, :], ALU.add,
                                                     ALU.mult).then_inc(run.ew, 1)
                            dve.wait_ge(run.ew, run.dv(c, "s", sweep))
                            dve.scalar_tensor_tensor(du[:, :], th[:, 1, :], 1.0, sl[:, 1, :], ALU.subtract,
                                                     ALU.mult).then_inc(run.ew, 1)
                            dve.wait_ge(run.ew, run.dv(c, "u", sweep))
                            dve.scalar_tensor_tensor(dd[:, :], th[:, 1, :], 1.0, du[:, :], ALU.add,
                                                     ALU.subtract).then_inc(run.ew, 1)
                            dve.wait_ge(run.mm, run.pe(c, "yc", sweep))
                            dve.scalar_tensor_tensor(gr[:, par, 0:2, :],
                                                     PS[:, 1, 0:2 * P].rearrange("p (a n) -> p a n", a=2),
                                                     1.0 / D, vb[:, :, :], ALU.mult, ALU.subtract)\
                                .then_inc(run.ew, 1)
                            dve.wait_ge(run.mm, run.pe(c, "ds", sweep))
                            dve.tensor_tensor(g3[:, :], PS[:, 0, 3 * P:4 * P], lr_mask[:, :], ALU.mult)\
                                .then_inc(run.ew, 1)
                            dve.wait_ge(run.mm, run.pe(c, "dc", sweep))
                            dve.wait_ge(run.ew, run.dv(c, "d", sweep))
                            dve.scalar_tensor_tensor(gr[:, par, 2, :], PS[:, 1, 2 * P:3 * P], 0.5, dd[:, :],
                                                     ALU.mult, ALU.mult).then_inc(run.ew, 1)
                    if run.checked:
                        dve.wait_ge(run.ew, run.dv_before(c, run.sweeps))
                        dve.tensor_tensor(cdiff[:, :, :], gr[:, 1, 1:3, :], gr[:, 0, 1:3, :], ALU.subtract)\
                            .then_inc(run.ew, 1)
                        dve.tensor_reduce(cmax[:, :], gr[:, 1, 1:3, :], AX.X, ALU.max, apply_absolute_value=True)\
                            .then_inc(run.ew, 1)
                        dve.wait_ge(run.ew, run.dv(c, "cm"))
                        dve.tensor_scalar(cmax[:, :], cmax[:, :], CONVERGED, 1e-30, ALU.mult, ALU.add)\
                            .then_inc(run.ew, 1)
                        dve.wait_ge(run.ew, run.dv(c, "ct"))
                        for k, sign in enumerate((1.0, -1.0)):
                            dve.scalar_tensor_tensor(cin[:, k, :, :], cdiff[:, :, :], sign,
                                                     cmax[:, :].unsqueeze(2).broadcast_to([P, 2, P]), ALU.mult,
                                                     ALU.is_lt).then_inc(run.ew, 1)
                        dve.wait_ge(run.ew, run.dv(c, "cn"))
                        dve.tensor_reduce(cok[:, :], cin[:, :, :, :], AX.XYZ, ALU.min).then_inc(run.ew, 1)
                        dve.wait_ge(run.ew, run.dv(c, "cr"))
                        dve.tensor_tensor(okay[:, :], okay[:, :], cok[:, :], ALU.min).then_inc(run.ew, 1)
                    dve.wait_ge(run.mm, run.pe(c, "up"))
                    dve.scalar_tensor_tensor(st[:, 0:3 * P], PS[:, 0, 0:3 * P], -LR, st[:, 0:3 * P], ALU.mult,
                                             ALU.add).then_inc(run.ew, 1)
                    dve.scalar_tensor_tensor(ST_B1, PS[:, 0, 3 * P:4 * P], -LR / 2, ST_B1, ALU.mult, ALU.add)\
                        .then_inc(run.ew, 1)
                    dve.scalar_tensor_tensor(ST_B2, PS[:, 1, 0:P], -LR / D, ST_B2, ALU.mult, ALU.add)\
                        .then_inc(run.ew, 1)
                    dve.scalar_tensor_tensor(ST_B1C, PS[:, 1, P:P + 1], -LR, ST_B1C, ALU.mult, ALU.add)\
                        .then_inc(run.ew, 1)
                    dve.scalar_tensor_tensor(ST_B2C, PS[:, 1, P + 1:P + 2], -LR / D, ST_B2C, ALU.mult, ALU.add)\
                        .then_inc(run.ew, 1)
                dve.wait_ge(run.ew, CHUNKS * run.td + 1)

            ttt(ttt_fast)
            dve.tensor_copy(cok[:, :], okay[:, :]).then_inc(ttt_okay, 1)
            dve.wait_ge(ttt_sum, 1)
            link(dve.tensor_scalar(flag_f[0:1, 0:1], PS[0:1, 2, 0:1], P - 0.5, None, ALU.is_ge))
            dve.tensor_copy(flag_i[0:1, 0:1], flag_f[0:1, 0:1]).then_inc(ttt_flag, 1)
            dve.wait_ge(ttt_flag, 1)
            settled = dve.value_load(flag_i[0:1, 0:1], min_val=0, max_val=1)
            with dve.If(settled == 0):
                dve.tensor_copy(st[:, :], st0[:, :]).then_inc(ttt_reset, 1)
                dve.wait_ge(ttt_reset, 1)
                ttt(ttt_full)
            with dve.Else():
                dve.nop()
            dve.scalar_tensor_tensor(X[:, :, :], ST_B2.unsqueeze(1).broadcast_to([P, NT, D]), float(D), X[:, :, :],
                                     ALU.mult, ALU.add).then_inc(ttt_settled, 1)
            for c in range(NC):
                dve.wait_ge(tq_th, 2 * c + 2)
                if c:
                    dve.wait_ge(tq_y, c)
                link(dve.scalar_tensor_tensor(QZT[:, 1, :], hq[:, 1, :], 1.0, hq[:, 0, :], ALU.add, ALU.mult))
                dve.tensor_scalar(QZT[:, 1, :], QZT[:, 1, :], 0.5, None, ALU.mult).then_inc(tq_s, 1)
                dve.wait_ge(tq_y, c + 1)
                dve.wait_ge(ttt_settled, 1)
                xs = X[:, 4 * c:4 * c + 4, :]
                dve.tensor_tensor(xs, PS[:, 2, :].rearrange("p (t n) -> p t n", t=4), xs, ALU.add)\
                    .then_inc(tq_acc, 1)

            with dve.Fori(0, B) as b:
                with dve.Fori(0, H0 // HG) as g:
                    trip = b * (H0 // HG) + g

                    wait(dve, a0_pe, "tk", trip)
                    dve.tensor_copy(kta[:, :], PS[:, 6:8, :].rearrange("p a n -> p (a n)")).then_inc(a0_dve.sem, 1)
                    for h in range(HG):
                        for i in range(TB):
                            r = 2 * ((h * TB + i) % 2)
                            wait(dve, a0_pe, ("a", h, i), trip)
                            src = PS[:, r:r + 2, :].rearrange("p a n -> p (a n)")[:, 0:(i + 1) * P]
                            dve.tensor_reduce(tmq[:, i, 32 * h + QM:32 * h + QM + 1], src, AX.X, ALU.max,
                                              negate=True).then_inc(a0_dve.sem, 1)
                    for c in range(2):
                        wait(dve, a0_pe, ("pv", LAST[c]), trip)
                        dve.tensor_copy(ots[:, c, :], PS[:, 6 + c, :]).then_inc(a0_dve.sem, 1)
                        wait(dve, a0_pe, ("to", c), trip)
                        ov = PS[:, 4 + c, :].rearrange("p (i h n) -> p (i h) n", i=4, h=HG)
                        dve.reciprocal(rz[:, c, :], ov[:, :, HD0]).then_inc(a0_dve.sem, 1)
                        wait(dve, a0_dve, ("rc", c), trip)
                        dst = Z0[:, bass.ds(b * TB + 4 * c, 4), bass.ds(g * (HG * HD0), HG * HD0)]
                        dve.tensor_tensor(dst.rearrange("p t (h e) -> p t h e", h=HG),
                                          ov[:, :, 0:HD0].rearrange("p (i h) n -> p i h n", i=4),
                                          rz[:, c, :].rearrange("p (i h) -> p i h", i=4).unsqueeze(3)
                                          .broadcast_to([P, 4, HG, HD0]), ALU.mult).then_inc(a0_dve.sem, 1)

            for c in range(NC):
                dve.wait_ge(ao_ps, c + 1)
                xs = XN[:, 4 * c:4 * c + 4, M_ZERO:D]
                dve.tensor_tensor(xs, PS[:, 4 + c, :].rearrange("p (t n) -> p t n", t=4)[:, :, 0:D - M_ZERO], xs,
                                  ALU.add).then_inc(ao_add, 1)
            dve.wait_ge(ao_add, NC)
            rms(1)
            link(dve.reciprocal(rms_r[:, :], rms_sd[:, :]))
            for t in range(NT):
                dve.tensor_scalar(Z0[:, t, :], XN[:, t, :], rms_r[:, t:t + 1], None, ALU.mult).then_inc(xf_tile, 1)
            dve.wait_ge(tq_acc, NC)
            dve.tensor_tensor(X[:, :, :], X[:, :, :], XN[:, :, :], ALU.add).then_inc(x_plus, 1)

            def gate(layer, experts, wts):
                n = experts
                l, e_, p_ = lg[:, :, 0:n], ge[:, :, 0:n], gp[:, :, 0:n]
                dve.wait_ge(gl_ps[layer], 1)
                ps = PS[:, 6, 0:NT * n].rearrange("p (t e) -> p t e", e=n)
                if layer == 0:
                    link(dve.tensor_copy(p_, ps))
                    link(dve.memset(l, 0.0))
                    link(dve.tensor_tensor(lgm[:, :, 0:n], p_, p_, ALU.is_equal))
                    link(dve.copy_predicated(l, lgm[:, :, 0:n], p_))
                    big = float(np.finfo(np.float32).max)
                    link(dve.tensor_scalar(l, l, big, -big, ALU.min, ALU.max))
                else:
                    link(dve.tensor_copy(l, ps))

                def rows(v):
                    return v.unsqueeze(2).broadcast_to([P, NT, n])

                link(dve.tensor_reduce(lgx[:, :], l, AX.X, ALU.max))
                dve.tensor_tensor(l, l, rows(lgx[:, :]), ALU.subtract).then_inc(gl_sub[layer], 1)
                dve.wait_ge(gl_exp[layer], 1)
                link(dve.tensor_reduce(lgx[:, :], e_, AX.X, ALU.add))
                link(dve.reciprocal(wsum[:, :], lgx[:, :]))
                link(dve.tensor_tensor(p_, e_, rows(wsum[:, :]), ALU.mult))
                cmp = gc[:, 0:n, 0:NT * n].rearrange("p f (t e) -> p f t e", e=n)
                link(dve.memset(gc[:, 0:n, 0:NT * n], 0.0))
                for f in range(n):
                    def other(k):
                        return p_[:, :, f:f + 1].broadcast_to([P, NT, k])
                    if f + 1 < n:
                        ins = dve.tensor_tensor(cmp[:, f, :, f + 1:n], other(n - 1 - f), p_[:, :, f + 1:n],
                                                ALU.is_ge)
                    if f:
                        ins = dve.tensor_tensor(cmp[:, f, :, 0:f], other(f), p_[:, :, 0:f], ALU.is_gt)
                link(ins)
                link(dve.tensor_reduce(rank[:, :, 0:n].rearrange("p t e -> p t e"),
                                       gc[:, 0:n, 0:NT * n].rearrange("p f (t e) -> p t e f", e=n), AX.X, ALU.add))
                link(dve.scalar_tensor_tensor(e_, rank[:, :, 0:n], 1.5, p_, ALU.is_lt, ALU.mult))
                link(dve.tensor_reduce(lgx[:, :], e_, AX.X, ALU.add))
                link(dve.tensor_scalar(lgx[:, :], lgx[:, :], 1e-8, None, ALU.add))
                link(dve.reciprocal(wsum[:, :], lgx[:, :]))
                dve.tensor_tensor(wts[:, :, :].rearrange("p e t -> p t e"), e_, rows(wsum[:, :]), ALU.mult)\
                    .then_inc(gl_done[layer], 1)
                dve.wait_ge(gl_done[layer], 1)

            gate(0, E0, wt0)

            dve.wait_ge(x_plus, 1)
            with dve.Fori(0, NC) as c:
                for kind, u in seq0:
                    if kind == "dn":
                        bank = 6 + dn_order.index(u) % 2
                        wait(dve, m0_pe, ("dn", u), c)
                        for i in range(4):
                            if u != dn_order[0]:
                                wait(dve, m0_dve, ("ac", dn_order[dn_order.index(u) - 1], i), c)
                            xs = X[:, bass.ds(c * 4 + i, 1), M_ZERO:D]
                            dve.scalar_tensor_tensor(
                                xs, PS[:, bank, i * P:i * P + D - M_ZERO].unsqueeze(1),
                                wt0[:, u, bass.ds(c * 4 + i, 1)], xs, ALU.mult, ALU.add).then_inc(m0_dve.sem, 1)
                        continue
                    then = units[u][3]
                    m = units[u][0][1]
                    if then == "silu":
                        wait(dve, m0_act, ("u", u), c)
                        dve.scalar_tensor_tensor(hid[:, HU[("e1g", m)], :], e1t[:, m, :], 1.0, PS[:, u % 6, :],
                                                 ALU.add, ALU.mult).then_inc(m0_dve.sem, 1)
                    elif then == "times":
                        wait(dve, m0_pe, ("u", u), c)
                        wait(dve, m0_dve, ("sg", 2 + m), c)
                        dve.scalar_tensor_tensor(hid[:, HU[("e1v", m)], :], hid[:, HU[("e1g", m)], :], 0.5,
                                                 PS[:, u % 6, :], ALU.mult, ALU.mult).then_inc(m0_dve.sem, 1)
            dve.wait_ge(m0_dve.sem, m0_dve.at(dve0[-1], NC - 1))

            norm(1)
            gate(1, E1, wt1)

            with dve.Fori(0, H1 // 2) as hp:
                def add_out(b):
                    wait(dve, a1_pe, ("wo", b), hp)
                    for half in range(2):
                        xs = X[:, TB * b + 4 * half:TB * b + 4 * half + 4, :]
                        dve.tensor_tensor(xs, PS[:, 2 + half, :].rearrange("p (t n) -> p t n", t=4), xs, ALU.add)\
                            .then_inc(a1_dve.sem, 1)

                for b in range(B):
                    for h in range(2):
                        wait(dve, a1_pe, ("kp", b), hp)
                        dve.tensor_copy(KH[0:HD1, h, :],
                                        PS[h * HD1:(h + 1) * HD1, 6:8, :].rearrange("p a n -> p (a n)"))\
                            .then_inc(a1_dve.sem, 1)
                    if b:
                        add_out(0)
                    for h in range(2):
                        for i in range(TB):
                            r = 2 * ((h * TB + i) % 2)
                            wait(dve, a1_pe, ("a", b, h, i), hp)
                            src = PS[:, r:r + 2, :].rearrange("p a n -> p (a n)")[:, 0:(i + 1) * P]
                            dve.tensor_reduce(NM[:, h, i:i + 1], src, AX.X, ALU.max, negate=True)\
                                .then_inc(a1_dve.sem, 1)
                    for c in range(2):
                        for h in range(2):
                            bank = 4 + 2 * c + h
                            wait(dve, a1_pe, ("pv", b, LAST[c], h), hp)
                            if c:
                                wait(dve, a1_dve, ("zt", b, 0, h), hp)
                            dve.reciprocal(RC[0:HD1, h, :], PS[HD1:P, bank, :]).then_inc(a1_dve.sem, 1)
                            wait(dve, a1_dve, ("rc", b, c, h), hp)
                            dve.tensor_tensor(ZT[h * HD1:(h + 1) * HD1, b, c * 512:(c + 1) * 512],
                                              PS[0:HD1, bank, :], RC[0:HD1, h, :], ALU.mult)\
                                .then_inc(a1_dve.sem, 1)
                add_out(1)
            dve.wait_ge(a1_dve.sem, a1_dve.at(("xa", 1, 1), H1 // 2 - 1))

            with dve.Fori(0, E1 // 2) as ep:
                for m in range(NM1 + 1):
                    if m < NM1:
                        for u in (2 * m, 2 * m + 1):
                            wait(dve, m1_act, ("u", u), ep)
                            if m >= 2:
                                wait(dve, m1_pe, ("dn", m - 2), ep)
                            dve.tensor_tensor(HB[:, m % 2, u % 2, :], GS[:, u % 3, :], PS[:, 2 * (u % 3) + 1, :],
                                              ALU.mult).then_inc(m1_dve.sem, 1)
                    if m >= 1:
                        k = m - 1
                        wait(dve, m1_pe, ("dn", k), ep)
                        for i in range(4):
                            t = (k % NC) * 4 + i
                            if k >= NC:
                                wait(dve, m1_dve, ("ac", k - NC, i), ep)
                            else:
                                wait(dve, m1_dve, ("ac", k + NC, i), ep, 1)
                            dve.scalar_tensor_tensor(
                                X[:, t, :], PS[:, 6 + k % 2, i * P:(i + 1) * P],
                                wt1[:, bass.ds(ep * 2 + k // NC, 1), t], X[:, t, :], ALU.mult, ALU.add)\
                                .then_inc(m1_dve.sem, 1)

        @block.tensor
        def _(pe):
            for s in (a0_pe, m0_pe, a1_pe, m1_pe):
                pe.sem_inc(s.sem, s.per_trip)
            pe.sem_inc(ttt_fast.mm, 1)
            pe.sem_inc(ttt_full.mm, 1)
            pe.wait_ge(const_ready, N_CONST)

            def turn(layer, src, ready, done, first_bank=0):
                for t in range(NT):
                    if ready is not None:
                        pe.wait_ge(ready, t + 1)
                    ins = pe.transpose(PS[:, first_bank + t // 4, (t % 4) * P:(t % 4 + 1) * P], src[:, t, :],
                                       ident[:, :])
                    if t % 4 == 3:
                        ins.then_inc(done, 1)

            turn(0, XN, ln_done[0], xt_ps[0])
            pe.wait_ge(qkv_w, 1)
            for t in range(NT):
                pe.wait_ge(xt_done[0], t // 4 + 1)
                if t >= 4:
                    pe.wait_ge(qkv_done, t - 3)
                pe.matmul(PS[:, 4 + t % 4, 0:3 * D], XT[:, t * P:(t + 1) * P], wqkv_n[:, :], start=True, stop=True)\
                    .then_inc(qkv_ps, 1)

            def mm(*args, **kw):
                return pe.matmul(*args, skip_group_check=True, **kw)

            def ttt(run):
                def ps(bank, k):
                    return PS[:, bank, k * P:(k + 1) * P]

                xcv = xc[:, :, :].rearrange("p b s -> p (b s)")
                with pe.Fori(0, CHUNKS) as c:
                    pe.wait_ge(run.staged, c + 1)
                    pe.wait_ge(run.ew, c * run.td + 1)
                    wk, wv = w0("wk_ttt"), w0("wv_ttt")
                    mm(ps(0, 0), wk, xcv, start=True, stop=True)
                    mm(ps(0, 1), xcv, wk, start=True, stop=True)
                    mm(ps(0, 2), wv, xcv, start=True, stop=True)
                    mm(ps(0, 3), xcv, wv, start=True, stop=True).then_inc(run.mm, 1)
                    pe.wait_ge(run.th, run.ac(c))
                    mm(ps(1, 0), kv[:, 0, :], kv[:, 0, :], start=True, stop=True)
                    mm(ps(1, 1), ST_W1, kv[:, 0, :], start=True, stop=True)
                    mm(ps(1, 2), kv[:, 0, :], ST_W1, start=True, stop=True).then_inc(run.mm, 1)
                    with pe.Fori(0, run.trips) as trip:
                        for par in range(2):
                            sweep = trip * 2 + par
                            dyo, dzo = gr[:, 1 - par, 1, :], gr[:, 1 - par, 2, :]
                            dyt = gr[:, par, 0, :]
                            s_t, s_tm = sl[:, 0, :], sl[:, 1, :]
                            pe.wait_ge(run.ew, run.dv_before(c, sweep))
                            mm(ps(0, 0), dzo, g1[:, :], start=True, stop=True)
                            mm(ps(0, 1), g1[:, :], dzo, start=True, stop=True).then_inc(run.mm, 1)
                            pe.wait_ge(run.ew, run.dv(c, "s", sweep))
                            mm(ps(0, 2), s_t, s_t, start=True, stop=True)
                            mm(ps(1, 0), ST_W2, s_t, start=True, stop=False)
                            mm(ps(1, 1), s_t, ST_W2, start=False, stop=False).then_inc(run.mm, 1)
                            pe.wait_ge(run.ew, run.dv(c, "g2", sweep))
                            mm(ps(1, 0), dyo, g2[:, :], start=False, stop=False)
                            mm(ps(1, 1), g2[:, :], dyo, start=False, stop=True).then_inc(run.mm, 1)
                            pe.wait_ge(run.ew, run.dv(c, "dy", sweep))
                            mm(ps(0, 3), dyt, dyt, start=True, stop=True)
                            mm(ps(1, 2), dyt, ST_W2T, start=True, stop=False).then_inc(run.mm, 1)
                            pe.wait_ge(run.ew, run.dv(c, "g3", sweep))
                            mm(ps(1, 2), g3[:, :], s_tm, start=False, stop=True).then_inc(run.mm, 1)
                    pe.wait_ge(run.ew, run.dv_before(c, run.sweeps))
                    dy, dz, s_tm = gr[:, 1, 1, :], gr[:, 1, 2, :], sl[:, 1, :]
                    mm(ps(0, 0), kv[:, 1, :], dz, start=True, stop=True)
                    mm(ps(0, 1), s_tm, dy, start=True, stop=True)
                    mm(ps(0, 2), dy, s_tm, start=True, stop=True)
                    mm(ps(0, 3), ones[:, :], dz, start=True, stop=True)
                    mm(ps(1, 0), ones[:, :], dy, start=True, stop=True)
                    mm(PS[:, 1, P:P + 1], dz, ones[:, 0:1], start=True, stop=True)
                    mm(PS[:, 1, P + 1:P + 2], dy, ones[:, 0:1], start=True, stop=True).then_inc(run.mm, 1)

            ttt(ttt_fast)
            pe.wait_ge(ttt_okay, 1)
            pe.matmul(PS[0:1, 2, 0:1], cok[:, :], ones[:, 0:1], start=True, stop=True).then_inc(ttt_sum, 1)
            pe.wait_ge(ttt_flag, 1)
            settled = pe.value_load(flag_i[0:1, 0:1], min_val=0, max_val=1)
            with pe.If(settled == 0):
                pe.wait_ge(ttt_reset, 1)
                ttt(ttt_full)
            with pe.Else():
                pe.nop()

            pe.wait_ge(ttt_settled, 1)
            for c in range(NC):
                if c:
                    pe.wait_ge(tq_qc, c)
                pe.matmul(PS[:, 0, :], w0("wq_ttt"), XT[:, c * 512:(c + 1) * 512], start=True, stop=True)\
                    .then_inc(tq_q, 1)
                pe.wait_ge(tq_qc, c + 1)
                if c:
                    pe.wait_ge(tq_th, 2 * c)
                pe.matmul(PS[:, 1, :], ST_W1, QZT[:, 0, :], start=True, stop=True).then_inc(tq_z, 1)
                pe.wait_ge(tq_s, c + 1)
                if c:
                    pe.wait_ge(tq_acc, c)
                for i in range(4):
                    ins = pe.matmul(PS[:, 2, i * P:(i + 1) * P], QZT[:, 1, i * P:(i + 1) * P], ST_W2, start=True,
                                    stop=True)
                ins.then_inc(tq_y, 1)
            pe.wait_ge(tq_acc, NC)

            with pe.Fori(0, B * H0 // HG) as trip:
                pe.wait_ge(a0_pool.sem, trip * 3 + 2)
                wait(pe, a0_dve, ("zt", 1), trip, 1)
                for i in range(TB):
                    ins = pe.transpose(PS[:, 4 + i // 4, (i % 4) * P:(i % 4 + 1) * P], tmq[:, i, :], ident[:, :])
                ins.then_inc(a0_pe.sem, 1)
                for i in range(TB):
                    ins = pe.transpose(PS[:, 6 + i // 4, (i % 4) * P:(i % 4 + 1) * P], tmk[:, i, :], ident[:, :])
                ins.then_inc(a0_pe.sem, 1)
                wait(pe, a0_act, "qa", trip)
                wait(pe, a0_dve, "ka", trip)
                wait(pe, a0_act, ("ex", NB - 1, HG - 1), trip, 1)
                for h in range(HG):
                    rows = slice(32 * h, 32 * h + 32)
                    for i in range(TB):
                        n = h * TB + i
                        r = 2 * (n % 2)
                        if n >= 2:
                            wait(pe, a0_dve, ("mx", (n - 2) // TB, (n - 2) % TB), trip)
                        for k0 in range(0, (i + 1) * P, 512):
                            k1 = min(k0 + 512, (i + 1) * P)
                            pe.matmul(PS[:, r + k0 // 512, 0:k1 - k0], qta[rows, i * P:(i + 1) * P],
                                      kta[rows, k0:k1], start=True, stop=True)
                        pe.matmul(PS[:, r + i // 4, (i % 4) * P:(i % 4 + 1) * P], ident_b[:, :], mask_qk[:, :],
                                  start=False, stop=True, skip_group_check=True).then_inc(a0_pe.sem, 1)
                wait(pe, a0_dve, ("mx", HG - 1, TB - 1), trip)
                for i in range(TB):
                    ins = pe.transpose(PS[:, 4 + i // 4, (i % 4) * P:(i % 4 + 1) * P], tmq[:, i, :], ident[:, :])
                ins.then_inc(a0_pe.sem, 1)
                wait(pe, a0_act, "qb", trip)
                pe.wait_ge(a0_pool.sem, trip * 3 + 3)

                def pv(n):
                    c, j = SWEEP_B[n]
                    q0 = max(512 * c, P * j)
                    for h in range(HG):
                        wait(pe, a0_act, ("ex", n, h), trip)
                        ins = pe.matmul(PS[32 * h:32 * h + 32, 6 + c, q0 - 512 * c:512],
                                        tmv[:, j, 32 * h:32 * h + 32], pe_[:, h, n % 2, 0:512 * (c + 1) - q0],
                                        start=(j == 0), stop=(j == 4 * c + 3), skip_group_check=True)
                    ins.then_inc(a0_pe.sem, 1)

                def out_turned(c):
                    wait(pe, a0_dve, ("oc", c), trip)
                    for i in range(4):
                        ins = pe.transpose(PS[:, 4 + c, i * P:(i + 1) * P], ots[:, c, i * P:(i + 1) * P],
                                           ident[:, :])
                    ins.then_inc(a0_pe.sem, 1)

                for n in range(NB + 1):
                    if n < NB:
                        c, j = SWEEP_B[n]
                        q0 = max(512 * c, P * j)
                        w = 512 * (c + 1) - q0
                        diag = j >= 4 * c
                        for h in range(HG):
                            rows = slice(32 * h, 32 * h + 32)
                            if n:
                                wait(pe, a0_act, ("ex", n - 1, h), trip)
                            ins = pe.matmul(PS[:, h, 0:w], kta[rows, j * P:(j + 1) * P], qtb[rows, q0:q0 + w],
                                            start=True, stop=True)
                            if diag:
                                ins = pe.matmul(PS[:, h, 0:P], ident_b[:, :], mask_kq[:, :], start=False, stop=True,
                                                skip_group_check=True)
                            ins.then_inc(a0_pe.sem, 1)
                    if n >= 1:
                        pv(n - 1)
                    if n == 7:
                        out_turned(0)
                out_turned(1)

            pe.wait_ge(a0_dve.sem, a0_dve.at(("zt", 1), B * H0 // HG - 1))
            turn(0, Z0, None, z0_ps)
            for t in range(NT):
                pe.wait_ge(z0_cp, t // 4 + 1)
                ins = pe.matmul(PS[:, 4 + t // 4, (t % 4) * P:(t % 4) * P + D - M_ZERO], Z0T[:, t * P:(t + 1) * P],
                                w0("wo", M_ZERO), start=True, stop=True)
                if t % 4 == 3:
                    ins.then_inc(ao_ps, 1)
            turn(0, Z0, xf_tile, xf_ps)
            pe.wait_ge(ao_add, NC)
            pe.wait_ge(xf_cp, NC)

            def gate(layer, weights, experts):
                for t in range(NT):
                    ins = pe.matmul(PS[:, 6, t * experts:(t + 1) * experts], XT[:, t * P:(t + 1) * P], weights,
                                    start=True, stop=True)
                ins.then_inc(gl_ps[layer], 1)

            gate(0, w0("gate"), E0)
            pe.wait_ge(gl_sub[0], 1)

            with pe.Fori(0, NC) as c:
                for kind, u in seq0:
                    if kind == "u":
                        name, blocks, rhs, then, dst = units[u]
                        if u >= 6:
                            s, step = unit_freed(u - 6)
                            wait(pe, s, step, c)
                        else:
                            s, step = unit_freed(max(v for v in range(15) if v % 6 == u))
                            wait(pe, s, step, c, 1)
                        for k, (lhs, r) in enumerate(zip(blocks, rhs)):
                            if r is None:
                                src = XT[:, bass.ts(c, 512)]
                            else:
                                made = next(v for v, s_ in enumerate(units) if s_[4] == r)
                                wait(pe, m0_act, ("u", made), c)
                                src = hid[:, r, :]
                            ins = pe.matmul(PS[:, u % 6, :], lhs, src, start=(k == 0), stop=(k == len(blocks) - 1))
                        ins.then_inc(m0_pe.sem, 1)
                    else:
                        wname, src = DOWN[u]
                        place = dn_order.index(u)
                        bank = 6 + place % 2
                        for k in range(2):
                            if u == 1:
                                wait(pe, m0_dve, ("tm", 4 + k), c)
                            else:
                                made = next(v for v, s_ in enumerate(units) if s_[4] == HU[(src, k)])
                                wait(pe, m0_act, ("u", made), c)
                        if place >= 2:
                            wait(pe, m0_dve, ("ac", dn_order[place - 2], 3), c)
                        else:
                            wait(pe, m0_dve, ("ac", dn_order[place + 2], 3), c, 1)
                        for i in range(4):
                            for k in range(2):
                                ins = pe.matmul(PS[:, bank, i * P:i * P + D - M_ZERO],
                                                hid[:, HU[(src, k)], i * P:(i + 1) * P],
                                                w0(wname, k * D + M_ZERO, (k + 1) * D), start=(k == 0), stop=(k == 1))
                        ins.then_inc(m0_pe.sem, 1)

            pe.wait_ge(m0_act.sem, m0_act.at(m0_act.names[-1], NC - 1))
            pe.wait_ge(m0_dve.sem, m0_dve.at(dve0[-1], NC - 1))
            turn(1, XN, ln_done[1], xt_ps[1])
            pe.wait_ge(xt_done[1], NC)
            pe.wait_ge(w1_loaded, 16)
            gate(1, w1("gate"), E1)
            pe.wait_ge(gl_sub[1], 1)
            pe.wait_ge(a1_ones, 1)

            with pe.Fori(0, H1 // 2) as hp:
                def out_product(b):
                    wait(pe, a1_dve, ("zt", b, 1, 1), hp)
                    wait(pe, a1_act, ("ex", b, NB - 1, 1), hp)
                    for t in range(TB):
                        ins = pe.matmul(PS[:, 2 + t // 4, (t % 4) * P:(t % 4 + 1) * P],
                                        ZT[:, b, t * P:(t + 1) * P],
                                        W1[:, bass.ds(hp * P + W1_AT["wo"][0], P)], start=True, stop=True)
                    ins.then_inc(a1_pe.sem, 1)

                for b in range(B):
                    before = (("zt", 1, 1, 1), hp, 1) if b == 0 else (("zt", 0, 1, 1), hp, 0)
                    pe.wait_ge(a1_pool.sem, hp + 1)
                    wait(pe, a1_dve, *before)
                    for a in range(2):
                        for c in range(2):
                            x0 = b * S + c * 512
                            ins = pe.matmul(PS[:, 4 + 2 * a + c, :], wqk_s[:, a, :], XT[:, x0:x0 + 512], start=True,
                                            stop=True)
                        ins.then_inc(a1_pe.sem, 1)
                    before = (("ex", 1, NB - 1, 1), hp, 1) if b == 0 else (("ex", 0, NB - 1, 1), hp, 0)
                    wait(pe, a1_act, *before)
                    for t in range(TB):
                        x0 = b * S + t * P
                        ins = pe.matmul(PS[:, t // 4, (t % 4) * P:(t % 4 + 1) * P], XT[:, x0:x0 + P],
                                        W1[:, bass.ds(hp * P + W1_AT["wv"][0], P)], start=True, stop=True)
                    ins.then_inc(a1_pe.sem, 1)
                    if b:
                        out_product(0)
                    wait(pe, a1_act, ("ve", b, 1), hp)
                    if b:
                        wait(pe, a1_dve, ("xa", 0, 1), hp)
                    else:
                        wait(pe, a1_dve, ("xa", 1, 1), hp, 1)
                    for h in range(2):
                        wait(pe, a1_act, ("qe", b, h), hp)
                        wait(pe, a1_dve, ("ke", b, h), hp)
                        for i in range(TB):
                            n = h * TB + i
                            r = 2 * (n % 2)
                            if n >= 2:
                                wait(pe, a1_dve, ("mx", b, (n - 2) // TB, (n - 2) % TB), hp)
                            for k0 in range(0, (i + 1) * P, 512):
                                k1 = min(k0 + 512, (i + 1) * P)
                                pe.matmul(PS[:, r + k0 // 512, 0:k1 - k0], QH[0:HD1, h, i * P:(i + 1) * P],
                                          KH[0:HD1, h, k0:k1], start=True, stop=True)
                            pe.matmul(PS[:, r + i // 4, (i % 4) * P:(i % 4 + 1) * P], ident_b[:, :], mask_qk[:, :],
                                      start=False, stop=True, skip_group_check=True).then_inc(a1_pe.sem, 1)
                    for h in range(2):
                        wait(pe, a1_dve, ("mx", b, h, TB - 1), hp)
                        for i in range(TB):
                            ins = pe.transpose(PS[0:1, 4 + 2 * h + i // 4, (i % 4) * P:(i % 4 + 1) * P],
                                               NM[:, h, i:i + 1], ident[:, :])
                        ins.then_inc(a1_pe.sem, 1)
                    wait(pe, a1_act, ("me", b, 1), hp)

                    def pv(n, h):
                        c, j = SWEEP_B[n]
                        q0 = max(512 * c, P * j)
                        wait(pe, a1_act, ("ex", b, n, h), hp)
                        pe.matmul(PS[:, 4 + 2 * c + h, q0 - 512 * c:512], VH[:, h, j, :],
                                  pe_[:, h, n % 2, 0:512 * (c + 1) - q0], start=(j == 0),
                                  stop=(j == 4 * c + 3)).then_inc(a1_pe.sem, 1)

                    for n in range(NB + 1):
                        if n < NB:
                            c, j = SWEEP_B[n]
                            q0 = max(512 * c, P * j)
                            w = 512 * (c + 1) - q0
                            diag = j >= 4 * c
                            for h in range(2):
                                bank = (2 * n + h) % 4
                                if n >= 2:
                                    wait(pe, a1_act, ("ex", b, n - 2, h), hp)
                                ins = pe.matmul(PS[:, bank, 0:w], KH[0:HD1 + 1, h, j * P:(j + 1) * P],
                                                QH[0:HD1 + 1, h, q0:q0 + w], start=True, stop=True)
                                if diag:
                                    ins = pe.matmul(PS[:, bank, 0:P], ident_b[:, :], mask_kq[:, :], start=False,
                                                    stop=True, skip_group_check=True)
                                ins.then_inc(a1_pe.sem, 1)
                        if n >= 1:
                            for h in range(2):
                                pv(n - 1, h)
                out_product(1)

            pe.wait_ge(a1_dve.sem, a1_dve.at(("xa", 1, 1), H1 // 2 - 1))

            with pe.Fori(0, E1 // 2) as ep:
                for m in range(NM1 + 1):
                    if m < NM1:
                        k = m // NC
                        if m % NC == 0:
                            pe.wait_ge(m1_pool.sem, ep * 2 + k + 1)
                        for u in (2 * m, 2 * m + 1):
                            half = u % 2
                            if u >= 3:
                                wait(pe, m1_dve, ("mu", u - 3), ep)
                            else:
                                wait(pe, m1_dve, ("mu", max(v for v in range(2 * NM1) if v % 3 == u)), ep, 1)
                            xs = XT[:, (m % NC) * 512:(m % NC + 1) * 512]
                            pe.matmul(PS[:, 2 * (u % 3), :], w11_s[:, k, half * P:(half + 1) * P], xs, start=True,
                                      stop=True)
                            pe.matmul(PS[:, 2 * (u % 3) + 1, :], w12_s[:, k, half * P:(half + 1) * P], xs,
                                      start=True, stop=True).then_inc(m1_pe.sem, 1)
                    if m >= 1:
                        d = m - 1
                        wait(pe, m1_dve, ("mu", 2 * d + 1), ep)
                        if d >= 2:
                            wait(pe, m1_dve, ("ac", d - 2, 3), ep)
                        else:
                            wait(pe, m1_dve, ("ac", NM1 - 2 + d, 3), ep, 1)
                        for i in range(4):
                            for half in range(2):
                                at = W1_AT["w2"][0] + (d // NC) * 2 * D + half * D
                                ins = pe.matmul(PS[:, 6 + d % 2, i * P:(i + 1) * P],
                                                HB[:, d % 2, half, i * P:(i + 1) * P],
                                                W1[:, bass.ds(ep * (4 * D) + at, D)], start=(half == 0),
                                                stop=(half == 1))
                        ins.then_inc(m1_pe.sem, 1)


def pack(parts, made):
    cols = []
    for name, n in parts:
        a = np.asarray(made[name], np.float32).reshape(P, n)
        cols.append(a)
    return np.ascontiguousarray(np.concatenate(cols, axis=1))


def blocks_of(wt):
    k, n = wt.shape
    return wt.reshape(k // P, P, n).transpose(1, 0, 2).reshape(P, -1)


def layout(i):
    g = {k: np.asarray(v) for k, v in i.items()}
    a, f = "L0_attn_", "L0_ffn_"
    rows = lambda v: np.broadcast_to(v[None, :], (P, v.shape[0]))
    w0 = {
        "wq_ttt": g[a + "W_Q"], "wk_ttt": g[a + "W_KV"][:, :D], "wv_ttt": g[a + "W_KV"][:, D:],
        "w1": g[a + "W1"], "w2": g[a + "W2"], "w2t": g[a + "W2"].T,
        "b1_rows": rows(g[a + "b1"]), "b2_rows": rows(g[a + "b2"]), "b1_col": g[a + "b1"], "b2_col": g[a + "b2"],
        "n1": g[f + "n1_w"], "n2": g[f + "n2_w"], "qn": rows(g[f + "qn_w"]), "kn": rows(g[f + "kn_w"]),
        "wqkv": np.concatenate([g[f + "wq"].T, g[f + "wk"].T, g[f + "wv"].T], axis=1), "wo": g[f + "wo"].T,
        "gate": g[f + "gate_w"].T,
    }
    for n in ("e0_up", "e0_down", "e1_w1", "e1_w2", "e1_down", "e2_l1", "e2_l2", "e2_l3", "e2_l4", "e3_down",
              "e3_up", "e3_out"):
        w0[n] = blocks_of(g[f + n].T)
    heads = lambda w: w.transpose(2, 0, 1).reshape(D, H1 * HD1)
    w1 = {
        "wq": heads(g["L1_attn_W_Q"]), "wk": heads(g["L1_attn_W_K"]), "wv": heads(g["L1_attn_W_V"]),
        "wo": blocks_of(g["L1_attn_W_O"].T), "gate": g["L1_ffn_Wg"],
        "w11": g["L1_ffn_W11"].transpose(1, 0, 2), "w12": g["L1_ffn_W12"].transpose(1, 0, 2),
        "w2": g["L1_ffn_W2"].reshape(E1, 2, P, D).transpose(2, 0, 1, 3),
    }
    return g["L0_attn_x"].reshape(B * S, D), pack(W0_PARTS, w0), pack(W1_PARTS, w1)


def kernel(**inputs):
    from concourse import bacc
    from concourse.bass_utils import run_bass_kernel_spmd

    x, w0, w1 = layout(inputs)
    nc = bacc.Bacc("TRN2", target_bir_lowering=False, num_devices=1)
    args = [nc.dram_tensor(n, a.shape, F32, kind="ExternalInput").ap()
            for n, a in (("x", x), ("w0", w0), ("w1", w1))]
    out = nc.dram_tensor("out", (B * S, D), F32, kind="ExternalOutput").ap()
    program(nc, *args, out)
    r = run_bass_kernel_spmd(nc, [{"x": x, "w0": w0, "w1": w1}], core_ids=[0])
    return r.results[0]["out"].reshape(B, S, D)
```

```python
from contextlib import ExitStack

import numpy as np

import concourse.bass as bass
from concourse import mybir

F32 = mybir.dt.float32
F32R = mybir.dt.float32r
BF16 = mybir.dt.bfloat16
I32 = mybir.dt.int32
ALU = mybir.AluOpType
ACT = mybir.ActivationFunctionType
AX = mybir.AxisListType

P = 128
B, S, D = 2, 1024, 128
NT = B * S // P
TB = S // P
NC = B * S // 512
LN_EPS = 1e-5
RMS_EPS = 1.1920929e-07
MASKED = -1e30

LR = 1e-3
CS = 64
CHUNKS = S // CS
SWEEPS = 6
CONVERGED = 2.0 ** -15

H0, HD0 = 16, 8
HG = 4
QM = 24
M_ZERO = 32

H1, HD1 = 16, 64
E0, E1, HID = 4, 8, 256

W0_PARTS = [("wq_ttt", 128), ("wk_ttt", 128), ("wv_ttt", 128), ("w1", 128), ("w2", 128), ("w2t", 128),
            ("b1_rows", 128), ("b2_rows", 128), ("b1_col", 1), ("b2_col", 1), ("n1", 1), ("n2", 1),
            ("qn", 8), ("kn", 8), ("wqkv", 384), ("wo", 128), ("gate", 4),
            ("e0_up", 256), ("e0_down", 256), ("e1_w1", 256), ("e1_w2", 256), ("e1_down", 256),
            ("e2_l1", 256), ("e2_l2", 512), ("e2_l3", 512), ("e2_l4", 256),
            ("e3_down", 128), ("e3_up", 256), ("e3_out", 256)]
W1_PARTS = [("wq", H1 * HD1), ("wk", H1 * HD1), ("wv", H1 * HD1), ("wo", H1 * HD1), ("gate", E1),
            ("w11", E1 * HID), ("w12", E1 * HID), ("w2", E1 * HID)]


def offsets(parts):
    at, out = 0, {}
    for name, n in parts:
        out[name] = (at, at + n)
        at += n
    return out, at


W0_AT, W0_N = offsets(W0_PARTS)
W1_AT, W1_N = offsets(W1_PARTS)


class Steps:

    def __init__(self, sem, names):
        self.sem, self.names = sem, list(names)
        self.per_trip = len(self.names)
        self.index = {n: i + 1 for i, n in enumerate(self.names)}

    def at(self, name, trip, back=0):
        return trip * self.per_trip + (self.index[name] + self.per_trip * (1 - back))


def program(nc, x_in, w0_in, w1_in, out):
    with ExitStack() as ctx:
        def sb(name, shape, dt=F32):
            return ctx.enter_context(nc.sbuf_tensor(name, shape, dt))

        def sem(name):
            return ctx.enter_context(nc.semaphore(name))

        PS = ctx.enter_context(nc.psum_tensor("PS", [P, 8, 512], F32))
        X = sb("X", [P, NT, D])
        XN = sb("XN", [P, NT, D])
        XT = sb("XT", [P, B * S])
        W0 = sb("W0", [P, W0_N])
        W1 = sb("W1", [P, W1_N])
        ident = sb("ident", [P, P])
        ident_b = sb("ident_b", [P, P], BF16)
        mask_qk = sb("mask_qk", [P, P], BF16)
        mask_kq = sb("mask_kq", [P, P], BF16)
        lr_mask = sb("lr_mask", [P, P])
        lr_mask_h = sb("lr_mask_h", [P, P])
        ones = sb("ones", [P, P])
        eps = sb("eps", [P, 2])
        stats = sb("stats", [P, NT, 6])
        mv = sb("mv", [P, NT, 2])
        sd = sb("sd", [P, NT])
        rstd = sb("rstd", [P, NT])
        ssq = sb("ssq", [P, NT])
        rms_sd = sb("rms_sd", [P, NT])
        rms_r = sb("rms_r", [P, NT])
        junk = sb("junk", [P, D])

        xc = sb("xc", [P, 2, CS])
        kv = sb("kv", [P, 4, P])
        vb = sb("vb", [P, 2, P])
        g1 = sb("g1", [P, P])
        g2 = sb("g2", [P, P])
        g3 = sb("g3", [P, P])
        zb = sb("zb", [P, 2, P])
        zh = sb("zh", [P, 2, P])
        th = sb("th", [P, 2, P])
        sl = sb("sl", [P, 2, P])
        du = sb("du", [P, P])
        dd = sb("dd", [P, P])
        gr = sb("gr", [P, 2, 3, P])
        STN = 3 * P + 2 * P + 2
        st = sb("st", [P, STN])
        st0 = sb("st0", [P, STN])
        cdiff = sb("cdiff", [P, 2, P])
        cin = sb("cin", [P, 2, 2, P])
        cmax = sb("cmax", [P, 2])
        cok = sb("cok", [P, 1])
        okay = sb("okay", [P, 1])
        flag_f = sb("flag_f", [1, 1])
        flag_i = sb("flag_i", [1, 1], I32)
        ST_W1, ST_W2, ST_W2T = st[:, 0:P], st[:, P:2 * P], st[:, 2 * P:3 * P]
        ST_B1, ST_B2 = st[:, 3 * P:4 * P], st[:, 4 * P:5 * P]
        ST_B1C, ST_B2C = st[:, 5 * P:5 * P + 1], st[:, 5 * P + 1:5 * P + 2]

        arena = sb("arena", [P, 15360])
        taken = [0]

        def area(n):
            taken[0] += n
            assert taken[0] <= 15360, taken
            return arena[:, taken[0] - n:taken[0]]

        QKV = area(NT * 3 * D).rearrange("p (t n) -> p t n", t=NT)
        LO = area(NT * 2 * D).rearrange("p (t n) -> p t n", t=NT)
        tmq = area(TB * P).rearrange("p (t n) -> p t n", t=TB)
        tmk = area(TB * P).rearrange("p (t n) -> p t n", t=TB)
        tmv = area(TB * P).rearrange("p (t n) -> p t n", t=TB)
        Z0 = area(NT * D).rearrange("p (t n) -> p t n", t=NT)
        taken[0] = 0
        Z0T = area(B * S)
        taken[0] = 0
        hid = area(15 * 512).rearrange("p (u n) -> p u n", u=15)
        e1t = area(2 * 512).rearrange("p (u n) -> p u n", u=2)
        taken[0] = 0
        QH = area(B * 2 * S).rearrange("p (b h n) -> p b h n", b=B, h=2)
        KH = area(B * 2 * S).rearrange("p (b h n) -> p b h n", b=B, h=2)
        VH = area(B * 2 * TB * (HD1 + 1)).rearrange("p (b h t n) -> p b h t n", b=B, h=2, t=TB)
        WO = area(H1 * (D + 1)).rearrange("p (h n) -> p h n", h=H1)
        wqk_s = area(2 * P).rearrange("p (a n) -> p a n", a=2)
        NM = area(2 * TB).rearrange("p (h t) -> p h t", h=2)
        NMH = area(2 * TB).rearrange("p (h t k) -> p h t k", h=2, k=2)
        RS = area(16).rearrange("p (c q) -> p c q", c=2)
        w11_s = area(2 * HID).rearrange("p (a n) -> p a n", a=2)
        w12_s = area(2 * HID).rearrange("p (a n) -> p a n", a=2)
        taken[0] = 0
        GS = area(3 * 512).rearrange("p (u n) -> p u n", u=3)
        HB = area(4 * 512).rearrange("p (m u n) -> p m u n", m=2, u=2)

        qta = sb("qta", [P, S], F32R)
        qtb = sb("qtb", [P, S], F32R)
        kta = sb("kta", [P, S], F32R)
        pe_ = sb("pe_", [P, 4, 2, 512])
        HI = pe_[:, :, :, :].rearrange("p h m n -> p (h m n)").rearrange("p (t n) -> p t n", t=NT)
        ZT = pe_[:, 2:4, :, :]
        QZT, hq = pe_[:, 0, :, :], pe_[:, 1, :, :]
        ots = sb("ots", [P, 2, 512])
        NMH0 = sb("NMH0", [P, HG, 4, 2])
        rz = sb("rz", [P, 2, 16])
        hss, hsd = ots[:, 0, :], ots[:, 1, :]
        wqkv_n = sb("wqkv_n", [P, 3 * D])

        lg = sb("lg", [P, NT, 8])
        lgm = sb("lgm", [P, NT, 8], I32)
        lgx = sb("lgx", [P, NT])
        ge = sb("ge", [P, NT, 8])
        gp = sb("gp", [P, NT, 8])
        gc = ots[:, :, :].rearrange("p a n -> p (a n)").rearrange("p (f n) -> p f n", f=8)
        rank = sb("rank", [P, NT, 8])
        wt0 = sb("wt0", [P, E0, NT])
        wt1 = sb("wt1", [P, E1, NT])
        wsum = sb("wsum", [P, NT])

        def w0(name, lo=0, hi=None):
            a, b = W0_AT[name]
            return W0[:, a + lo:(b if hi is None else a + hi)]

        def w1(name, lo=0, hi=None):
            a, b = W1_AT[name]
            return W1[:, a + lo:(b if hi is None else a + hi)]

        x_loaded, w0_loaded, w1_loaded = sem("x_loaded"), sem("w0_loaded"), sem("w1_loaded")
        const_ready = sem("const_ready")
        stored = sem("stored")
        dve_chain, act_chain, pool_chain = sem("dve_chain"), sem("act_chain"), sem("pool_chain")
        N_CONST = 1


        class Ttt:
            def __init__(self, tag, sweeps):
                self.trips, self.sweeps = sweeps // 2, sweeps
                self.staged = sem(f"ttt_{tag}_chunk_staged")
                self.mm = sem(f"ttt_{tag}_products")
                self.ew = sem(f"ttt_{tag}_elementwise")
                self.th = sem(f"ttt_{tag}_tanh")
                self.pe0, self.pes, self.pe1 = ["kv", "base"], ["zc", "ys", "yc", "ds", "dc"], ["up"]
                self.dv0 = ["vbt", "vb", "g1", "zbt", "zb", "zero"]
                self.dvs = ["z", "s", "g2", "u", "d", "dy", "g3", "dz"]
                self.dv1 = ["w", "b1", "b2", "b1c", "b2c"]
                self.tm = len(self.pe0) + sweeps * len(self.pes) + len(self.pe1)
                self.td = len(self.dv0) + sweeps * len(self.dvs) + len(self.dv1)
                self.ta = 1 + sweeps

            def pe(self, chunk, name, sweep=None):
                if name in self.pe0:
                    return chunk * self.tm + (2 + self.pe0.index(name))
                if name in self.pes:
                    return chunk * self.tm + sweep * len(self.pes) + (2 + len(self.pe0) + self.pes.index(name))
                return (chunk + 1) * self.tm + 1

            def dv(self, chunk, name, sweep=None):
                if name in self.dv0:
                    return chunk * self.td + (2 + self.dv0.index(name))
                if name in self.dvs:
                    return chunk * self.td + sweep * len(self.dvs) + (2 + len(self.dv0) + self.dvs.index(name))
                return chunk * self.td + (2 + len(self.dv0) + self.sweeps * len(self.dvs) + self.dv1.index(name))

            def dv_before(self, chunk, sweep):
                return chunk * self.td + sweep * len(self.dvs) + (1 + len(self.dv0))

            def ac(self, chunk, sweep=None):
                return chunk * self.ta + (2 if sweep is None else sweep + 3)

        ttt_full = Ttt("full", CS)
        ttt_okay, ttt_sum, ttt_flag, ttt_reset, ttt_settled = (
            sem("ttt_okay"), sem("ttt_okay_summed"), sem("ttt_flag_ready"), sem("ttt_state_reset"),
            sem("ttt_settled"))

        SWEEP_B = [(c, j) for c in range(2) for j in range(4 * c + 4)]
        NB = len(SWEEP_B)
        LAST = [3, NB - 1]
        TRIPS = B * H0 // HG
        assert CHUNKS == 2 * TRIPS
        PIECES0 = [(c, h, i, k) for c in range(2) for h in range(HG) for i in range(4 * c, 4 * c + 4)
                   for k in range(c + 1)]
        NP0 = len(PIECES0)
        P0_HALF = NP0 // 3
        attn = [("tq", 0), ("tk", 0), ("tq", 1), ("tk", 1)]
        for p in range(NP0):
            attn.append(("a", p))
            if p == P0_HALF + 4:
                attn.append(("tq2", 0))
        attn.append(("tq2", 1))
        for n in range(NB + 1):
            if n < NB:
                attn += [("st", n, h) for h in range(HG)]
            if n >= 1:
                attn += [("pv", n - 1)]
            if n == 7:
                attn += [("to", 0)]
        attn += [("to", 1)]

        def share(item):
            if item[0] == "a":
                c, h, i, k = PIECES0[item[1]]
                return min(4, i + 1 - 4 * k) + 1
            if item[0] in ("st", "pv"):
                c, j = SWEEP_B[item[1]]
                return (4 * (c + 1) - max(4 * c, j)) * (1 if item[0] == "st" else 2) + 1
            return 5

        train = []
        for q in range(2):
            train += [((q, "kv"), 1.0), ((q, "base"), 1.0)]
            for k in range(SWEEPS):
                train += [((q, "zc", k), 1.8), ((q, "y", k), 1.0), ((q, "ds", k), 0.9), ((q, "dc", k), 0.9)]
            train += [((q, "up"), 1.0)]
        room, total = sum(r for _, r in train), sum(share(a) for a in attn)
        TRIP, used, due = [], 0, 0.0
        rest = list(attn)
        for step, r in train:
            TRIP.append(("t",) + step)
            due += r * total / room
            while rest and used + share(rest[0]) / 2 < due:
                used += share(rest[0])
                TRIP.append(rest.pop(0))
        TRIP += rest

        a0_pe = Steps(sem("a0_products"), attn)
        a0_act = Steps(sem("a0_scalar"), [x for r in attn if r[0] in ("tq", "tq2", "st")
                                          for x in [({"tq": "qa", "tq2": "qb", "st": "ex"}[r[0]],) + r[1:]]])
        vec = []
        for r in attn:
            if r[0] == "tk":
                vec.append(("ka", r[1]))
            elif r[0] == "a":
                vec.append(("mx", r[1]))
                c, h, i, k = PIECES0[r[1]]
                if (c, i, k) == (1, TB - 1, 1):
                    vec.append(("cb", h))
            elif r[0] == "pv" and r[1] in LAST:
                vec.append(("oc", LAST.index(r[1])))
            elif r[0] == "to":
                vec += [("rc", r[1]), ("zt", r[1])]
        a0_dve = Steps(sem("a0_vector"), vec)
        a0_pool = Steps(sem("a0_staged"), ["k", "q", "v"])
        CHECK = ["cd", "cm", "ct", "cp", "cn", "cr", "ck"]
        UPDATE = ["w", "b1", "b2", "b1c", "b2c"]
        tpe, tact, tdve = [], [], []
        for q in range(2):
            tpe += [(q, "kv"), (q, "base")]
            tact += [(q, "kv")]
            tdve += [(q, n) for n in ("vbt", "vb", "g1", "zbt", "zb")]
            for k in range(SWEEPS):
                tpe += ([(q, "zc", k)] if k else []) + [(q, n, k) for n in ("y", "ds", "dc")]
                tpe += [(q, "ss", k)] if k + 1 < SWEEPS else []
                tact += [(q, "th", k)]
                tdve += ([(q, "z", k)] if k else []) + [(q, n, k) for n in ("s", "u", "d", "dy", "g3", "dz")]
                tdve += [(q, "g2", k)] if k + 1 < SWEEPS else []
            tpe += [(q, "up")]
            tdve += [(q, n) for n in UPDATE + CHECK]
        t_pe, t_act, t_dve = Steps(sem("ttt_products"), tpe), Steps(sem("ttt_scalar"), tact), \
            Steps(sem("ttt_vector"), tdve)
        t_pool = Steps(sem("ttt_chunk_staged"), [(0, "xc"), (1, "xc")])

        units = []

        def unit(name, blocks, rhs, then, dst):
            units.append((name, blocks, rhs, then, dst))

        HU = {}

        def slot(name):
            HU.setdefault(name, len(HU))
            return HU[name]

        def layer(tag, wname, k_blocks, m_blocks, src, then):
            for m in range(m_blocks):
                blocks = [w0(wname, kb * 128 * m_blocks + m * 128, kb * 128 * m_blocks + m * 128 + 128)
                          for kb in range(k_blocks)]
                rhs = [None] * k_blocks if src is None else [slot((src, kb)) for kb in range(k_blocks)]
                unit((tag, m), blocks, rhs, then, slot((tag, m)) if then != "none" else None)

        order0 = []
        layer("e0h", "e0_up", 1, 2, None, "gelu")
        layer("e1g", "e1_w1", 1, 2, None, "silu")
        layer("e1v", "e1_w2", 1, 2, None, "times")
        layer("e2a", "e2_l1", 1, 2, None, "gelu")
        layer("e3a", "e3_down", 1, 1, None, "gelu")
        layer("e2b", "e2_l2", 2, 2, "e2a", "gelu")
        layer("e3b", "e3_up", 1, 2, "e3a", "gelu")
        layer("e2c", "e2_l3", 2, 2, "e2b", "gelu")
        assert len(units) == 15 and len(HU) == 15
        seq0 = []
        for u, spec in enumerate(units):
            seq0.append(("u", u))
            if spec[0] == ("e2b", 1):
                seq0.append(("dn", 0))
            if spec[0] == ("e3b", 1):
                seq0.append(("dn", 1))
        seq0 += [("dn", 3), ("dn", 2)]
        DOWN = {0: ("e0_down", "e0h"), 1: ("e1_down", "e1v"), 2: ("e2_l4", "e2c"), 3: ("e3_out", "e3b")}
        dn_order = [s[1] for s in seq0 if s[0] == "dn"]
        m0_pe = Steps(sem("m0_products"), seq0)
        m0_act = Steps(sem("m0_scalar"), [("u", u) for u, s in enumerate(units) if s[3] in ("gelu", "silu")])
        dve0 = []
        for kind, u in seq0:
            if kind == "u" and units[u][3] == "silu":
                dve0.append(("sg", u))
            elif kind == "u" and units[u][3] == "times":
                dve0.append(("tm", u))
            elif kind == "dn":
                dve0 += [("ac", u, i) for i in range(4)]
        m0_dve = Steps(sem("m0_vector"), dve0)

        def unit_freed(u):
            then = units[u][3]
            return (m0_act, ("u", u)) if then == "gelu" else (m0_dve, ("sg", u) if then == "silu" else ("tm", u))

        ROUNDS = B * H1 // 2
        PIECES = [(c, h, i, k) for c in range(2) for h in range(2) for i in range(4 * c, 4 * c + 4)
                  for k in range(c + 1)]
        GROUPS = [range(0, 3), range(3, 6), range(6, 8)]
        extra = {0: ["q", "k"], 2: ["v"], 3: [("a", 0), ("a", 1)], 4: [("a", p) for p in (2, 3, 4)],
                 5: [("a", p) for p in (5, 6, 7)], 6: [("a", 8), ("a", 9), ("w", 0, 0)],
                 7: [("a", 10), ("a", 11), ("w", 0, 1)], 8: [("a", 12), ("a", 13), ("w", 0, 2)],
                 9: [("mr", 0, 0), ("a", 14), ("a", 15), ("mr", 0, 1)], 10: [("a", p) for p in (16, 17, 18)],
                 11: [("a", p) for p in (19, 20, 21)],
                 12: [("a", 22), ("a", 23), ("mr", 1, 0), ("mr", 1, 1), ("w", 1, 0), ("w", 1, 1), ("w", 1, 2)]}
        ROUND = []
        for n in range(NB + 1):
            if n < NB:
                ROUND += [("st", n, 0), ("st", n, 1)]
            if n:
                ROUND += [("pv", n - 1, 0), ("pv", n - 1, 1)]
            ROUND += extra.get(n, [])
        FIRST = [r for r in ROUND if r[0] in ("q", "k", "v", "a", "mr")]
        SECOND = [r for r in ROUND if r not in FIRST]

        def made(kinds, react):
            return [x for r in ROUND if r[0] in kinds for x in react(r)]

        f1_pe = Steps(sem("f1_products"), FIRST)
        s1_pe = Steps(sem("s1_products"), [r for r in SECOND if r[0] != "w"])
        w1_pe = Steps(sem("w1_products"), [r for r in SECOND if r[0] == "w"])
        f1_act = Steps(sem("f1_scalar"), made(("q", "v", "mr"), lambda r: [("me",) + r[1:]] if r[0] == "mr"
                                              else [(r[0] + "e", 0), (r[0] + "e", 1)]))
        s1_act = Steps(sem("s1_exp"), made(("st",), lambda r: [("ex",) + r[1:]]))
        f1_dve = Steps(sem("f1_vector"), made(("k", "a"), lambda r: [("ke", 0), ("ke", 1)] if r == "k" else
                                              [("mx", r[1])] + ([("cb", PIECES[r[1]][1])] if r[1] in (15, 23) else [])))
        s1_dve = Steps(sem("s1_vector"), [("oc", c, h) for c in range(2) for h in range(2)])
        w1_dve = Steps(sem("w1_vector"), made(("w",), lambda r: [("rs",) + r[1:]]
                                              + [("x", r[1], q) for q in GROUPS[r[2]]]))
        w1_stage = sem("wqk_staged")
        W_BANK = {(0, 0): 6, (0, 1): 7, (0, 2): 6, (1, 0): 7, (1, 1): 6, (1, 2): 7}

        NM1 = 2 * NC
        m1pe, m1dve = [], []
        for m in range(NM1 + 1):
            if m < NM1:
                m1pe += [("u", 2 * m), ("u", 2 * m + 1)]
                m1dve += [("mu", 2 * m), ("mu", 2 * m + 1)]
            if m >= 1:
                m1pe += [("dn", m - 1)]
                m1dve += [("ac", m - 1, i) for i in range(4)]
        m1_pe = Steps(sem("m1_products"), m1pe)
        m1_act = Steps(sem("m1_silu"), [("u", u) for u in range(2 * NM1)])
        m1_dve = Steps(sem("m1_vector"), m1dve)
        m1_pool = Steps(sem("m1_staged"), ["w0", "w1"])

        def two(name):
            return sem(name + "_0"), sem(name + "_1")

        ln_var, ln_sd, ln_done, xt_ps, xt_done = (two("ln_var"), two("ln_sd"), two("ln_tile"), two("xt_turned"),
                                                  two("xt_copied"))
        rms_ss, rms_sq = two("rms_sum"), two("rms_root")
        qkv_w, qkv_ps, qkv_done, hsq, hsum, hroot, hnorm, hhi, hlo = (
            sem("qkv_weights"), sem("qkv_products"), sem("qkv_copied"), sem("head_squares"), sem("head_sums"),
            sem("head_roots"), sem("head_normed"), sem("head_high"), sem("head_low"))
        tq_q, tq_z, tq_y, tq_qc, tq_th, tq_s, tq_acc = (
            sem("ttt_q_product"), sem("ttt_hidden_product"), sem("ttt_out_product"), sem("ttt_q_copied"),
            sem("ttt_out_tanh"), sem("ttt_out_silu"), sem("ttt_out_added"))
        z0_ps, z0_cp, ao_ps, ao_add, xf_tile, xf_ps, xf_cp = (
            sem("z0_turned"), sem("z0_copied"), sem("ao_products"), sem("ao_added"), sem("xf_tile"),
            sem("xf_turned"), sem("xf_copied"))
        gl_ps, gl_sub, gl_exp, gl_done = two("gate_logits"), two("gate_shifted"), two("gate_exp"), two("gate_done")
        a0_zero, a1_ones = sem("a0_stacks_cleared"), sem("a1_ones_set")
        x_plus = sem("residual_added")
        wo_loaded = sem("wo_loaded")

        def chunk_before(q):
            return (0, 0) if q else (1, 1)

        def wait(e, steps, name, trip, back=0):
            e.wait_ge(steps.sem, steps.at(name, trip, back))

        def tiles(ap, t, n=1):
            return ap[:, bass.ds(t, n), :]

        block = ctx.enter_context(nc.Block())

        @block.sync
        def _(sp):
            xs = x_in.rearrange("(t p) d -> p t d", p=P)
            sp.dma_start(X[:, 0:TB, :], xs[:, 0:TB, :]).then_inc(x_loaded, 16)
            sp.dma_start(X[:, TB:NT, :], xs[:, TB:NT, :]).then_inc(x_loaded, 16)
            sp.dma_start(W0[:, :], w0_in).then_inc(w0_loaded, 16)
            sp.dma_start(W1[:, :], w1_in).then_inc(w1_loaded, 16)
            sp.wait_ge(m0_pe.sem, m0_pe.at(seq0[-1], NC - 1))
            wo_pairs = WO[0:HD1].rearrange("p (m h) n -> p h m n", h=2)
            lo, hi = W1_AT["wo"]
            for h in range(2):
                sp.dma_start(wo_pairs[:, h, :, 0:D],
                             w1_in[h * HD1:(h + 1) * HD1, lo:hi].rearrange("p (m n) -> p m n", n=D))\
                    .then_inc(wo_loaded, 16)
            sp.wait_ge(m1_dve.sem, m1_dve.at(("ac", NM1 - 1, 3), E1 // 2 - 1))
            sp.dma_start(out.rearrange("(t p) d -> p t d", p=P), X[:, :, :]).then_inc(stored, 16)
            sp.wait_ge(stored, 16)

        @block.gpsimd
        def _(pool):
            count = [0]

            def link(ins):
                count[0] += 1
                ins.then_inc(pool_chain, 1)
                pool.wait_ge(pool_chain, count[0])

            pool.sem_inc(t_pool.sem, t_pool.per_trip)
            for m in (ident, ident_b):
                link(pool.memset(m[:, :], 0.0))
                link(pool.affine_select(out=m[:, :], in_=m[:, :], compare_op=ALU.not_equal, fill=1.0, base=0,
                                        pattern=[[-1, P]], channel_multiplier=1))
            for m, sign in ((mask_qk, 1), (mask_kq, -1)):
                link(pool.memset(m[:, :], 0.0))
                link(pool.affine_select(out=m[:, :], in_=m[:, :], compare_op=ALU.is_ge, fill=MASKED, base=0,
                                        pattern=[[-sign, P]], channel_multiplier=sign))
            for m, v in ((lr_mask, -LR), (lr_mask_h, -LR / 2)):
                link(pool.memset(m[:, :], v))
                for half in range(2):
                    rows = m[half * CS:(half + 1) * CS, :].rearrange("p (b s) -> p b s", b=2)
                    link(pool.affine_select(out=rows, in_=rows, compare_op=ALU.is_ge, fill=0.0, base=-1,
                                            pattern=[[0, 2], [1, CS]], channel_multiplier=-1))
            link(pool.memset(ones[:, :], 1.0))
            link(pool.memset(eps[:, 0:1], LN_EPS))
            link(pool.memset(eps[:, 1:2], RMS_EPS))
            link(pool.memset(okay[:, :], 1.0))
            for tm, at in ((tmk, QM), (tmv, HD0)):
                link(pool.memset(tm, 0.0))
                link(pool.memset(tm.rearrange("p t (h n) -> p t h n", h=HG)[:, :, :, at:at + 1], 1.0))
            pool.memset(tmq, 0.0).then_inc(const_ready, 1)
            pool.wait_ge(const_ready, N_CONST)

            def ttt(run):
                with pool.Fori(0, CHUNKS) as c:
                    pool.wait_ge(run.mm, c * run.tm + 1)
                    src = XT[:, :].rearrange("p (b s) -> p b s", b=B)[:, :, bass.ts(c, CS)]
                    pool.tensor_copy(xc[:, :, :], src).then_inc(run.staged, 1)

            pool.wait_ge(xt_done[0], NC)
            pool.wait_ge(hlo, 1)
            with pool.Fori(0, B) as b:
                with pool.Fori(0, H0 // HG) as g:
                    trip = b * (H0 // HG) + g

                    def tokens(q):
                        p, back = chunk_before(q)
                        wait(pool, t_pe, (p, "kv"), trip, back)
                        at = trip * (2 * CS) + q * CS
                        src = XT[:, :].rearrange("p (b s) -> p b s", b=B)[:, :, bass.ds(at, CS)]
                        pool.tensor_copy(xc[:, :, :], src).then_inc(t_pool.sem, 1)

                    def heads(ap, off):
                        v = ap[:, bass.ts(b, TB), bass.ds(g * (HG * HD0) + off, HG * HD0)]
                        return v.rearrange("p t (h e) -> p t h e", h=HG)

                    def put(tm, at):
                        return tm.rearrange("p t (h n) -> p t h n", h=HG)[:, :, :, at:at + HD0]

                    tokens(0)
                    wait(pool, a0_pe, ("tk", 1), trip, 1)
                    pool.tensor_copy(put(tmk, 0), heads(QKV, D))
                    pool.tensor_copy(put(tmk, HD0), heads(LO, D))
                    pool.tensor_copy(put(tmk, 2 * HD0), heads(QKV, D)).then_inc(a0_pool.sem, 1)
                    wait(pool, a0_pe, ("tq2", 1), trip, 1)
                    pool.tensor_copy(put(tmq, 0), heads(QKV, 0))
                    pool.tensor_copy(put(tmq, HD0), heads(QKV, 0))
                    pool.tensor_copy(put(tmq, 2 * HD0), heads(LO, 0))
                    pool.memset(tmq.rearrange("p t (h n) -> p t h n", h=HG)[:, :, :, QM:QM + 1], 0.0)\
                        .then_inc(a0_pool.sem, 1)
                    wait(pool, a0_pe, ("pv", NB - 1), trip, 1)
                    pool.tensor_copy(put(tmv, 0), heads(QKV, 2 * D)).then_inc(a0_pool.sem, 1)
                    tokens(1)

            pool.wait_ge(ttt_flag, 1)
            settled = pool.value_load(flag_i[0:1, 0:1], min_val=0, max_val=1)
            with pool.If(settled == 0):
                ttt(ttt_full)
            with pool.Else():
                pool.nop()

            pool.wait_ge(m0_pe.sem, m0_pe.at(seq0[-1], NC - 1))
            pool.wait_ge(m0_dve.sem, m0_dve.at(dve0[-1], NC - 1))
            link(pool.memset(VH[:, :, :, :, HD1:HD1 + 1], 1.0))
            link(pool.memset(WO[:, :, D:D + 1], 0.0))
            link(pool.memset(WO[HD1:HD1 + 1, :, :], 0.0))
            link(pool.memset(WO[HD1:HD1 + 1, :, D:D + 1], 1.0))
            pool.memset(KH[HD1:HD1 + 1, :, :, :], 1.0).then_inc(a1_ones, 1)
            pool.wait_ge(a1_ones, 1)
            pool.wait_ge(w1_loaded, 16)
            with pool.Fori(0, H1 // 2) as hp:
                wait(pool, f1_pe, "k", hp * 2 + 1, 2)
                for a, name in enumerate(("wq", "wk")):
                    at = W1_AT[name][0]
                    ins = pool.tensor_copy(wqk_s[:, a, :], W1[:, bass.ds(hp * P + at, P)])
                ins.then_inc(w1_stage, 1)
            with pool.Fori(0, E1 // 2) as ep:
                for k in range(2):
                    wait(pool, m1_pe, ("u", NM1 * (k + 1) - 1), ep, 1)
                    for dst, name in ((w11_s, "w11"), (w12_s, "w12")):
                        at = W1_AT[name][0] + k * HID
                        ins = pool.tensor_copy(dst[:, k, :], W1[:, bass.ds(ep * (2 * HID) + at, HID)])
                    ins.then_inc(m1_pool.sem, 1)

        @block.scalar
        def _(act):
            act.sem_inc(a0_act.sem, a0_act.per_trip)
            act.sem_inc(m0_act.sem, m0_act.per_trip)
            act.sem_inc(f1_act.sem, f1_act.per_trip)
            act.sem_inc(s1_act.sem, s1_act.per_trip)
            act.sem_inc(m1_act.sem, m1_act.per_trip)
            act.sem_inc(t_act.sem, t_act.per_trip)
            act.sem_inc(ttt_full.th, 1)
            act.wait_ge(const_ready, N_CONST)

            def norm(layer):
                act.wait_ge(ln_var[layer], NT)
                act.activation(sd[:, :], mv[:, :, 1], ACT.Sqrt, bias=eps[:, 0:1]).then_inc(ln_sd[layer], 1)
                for c in range(NC):
                    act.wait_ge(xt_ps[layer], c + 1)
                    act.copy(XT[:, c * 512:(c + 1) * 512], PS[:, c, :]).then_inc(xt_done[layer], 1)

            norm(0)
            act.wait_ge(rms_ss[0], NT)
            act.activation(rms_sd[:, :], ssq[:, :], ACT.Sqrt, bias=eps[:, 1:2], scale=1.0 / D)\
                .then_inc(rms_sq[0], 1)
            act.wait_ge(ln_done[0], NT + 1)
            for t in range(NT):
                act.wait_ge(qkv_ps, t + 1)
                act.activation(QKV[:, t, :], PS[:, 4 + t % 4, 0:3 * D], ACT.Copy, scale=rms_r[:, t:t + 1])\
                    .then_inc(qkv_done, 1)
            act.wait_ge(qkv_done, NT)
            act.activation(LO, QKV[:, :, 0:2 * D], ACT.Square).then_inc(hsq, 1)
            act.wait_ge(hsum, 1)
            act.activation(hsd, hss, ACT.Sqrt, bias=eps[:, 1:2], scale=1.0 / HD0).then_inc(hroot, 1)
            act.wait_ge(hnorm, 1)
            act.copy(HI.bitcast(F32R), QKV[:, :, 0:2 * D]).then_inc(hhi, 1)

            def ttt(run):
                with act.Fori(0, CHUNKS) as c:
                    act.wait_ge(run.mm, run.pe(c, "kv"))
                    act.copy(kv[:, :, :], PS[:, 0, :].rearrange("p (a n) -> p a n", a=4)).then_inc(run.th, 1)
                    with act.Fori(0, run.trips) as trip:
                        for par in range(2):
                            sweep = trip * 2 + par
                            act.wait_ge(run.ew, run.dv(c, "z", sweep))
                            act.activation(th[:, :, :], zh[:, :, :], ACT.Tanh).then_inc(run.th, 1)

            with act.Fori(0, TRIPS) as trip:
                for r in TRIP:
                    if r[0] == "t" and r[2] == "kv":
                        wait(act, t_pe, r[1:], trip)
                        act.copy(kv[:, :, :], PS[:, 0, :].rearrange("p (a n) -> p a n", a=4)).then_inc(t_act.sem, 1)
                    elif r[0] == "t" and r[2] == "zc":
                        _, q, _, k = r
                        src = zh if k else zb
                        wait(act, t_dve, (q, "z", k) if k else (q, "zb"), trip)
                        act.activation(th[:, :, :], src[:, :, :], ACT.Tanh).then_inc(t_act.sem, 1)
                    elif r[0] in ("tq", "tq2"):
                        dst = qta if r[0] == "tq" else qtb
                        wait(act, a0_pe, r, trip)
                        act.copy(dst[:, 512 * r[1]:512 * (r[1] + 1)], PS[:, 7, :]).then_inc(a0_act.sem, 1)
                    elif r[0] == "st":
                        _, n, h = r
                        c, j = SWEEP_B[n]
                        w = 512 * (c + 1) - max(512 * c, P * j)
                        wait(act, a0_pe, r, trip)
                        if n >= 2:
                            wait(act, a0_pe, ("pv", n - 2), trip)
                        act.activation(pe_[:, h, n % 2, 0:w], PS[:, 2 + h, 0:w], ACT.Exp, scale=HD0 ** -0.5)\
                            .then_inc(a0_act.sem, 1)

            act.wait_ge(ttt_flag, 1)
            settled = act.value_load(flag_i[0:1, 0:1], min_val=0, max_val=1)
            with act.If(settled == 0):
                ttt(ttt_full)
            with act.Else():
                act.nop()

            for c in range(NC):
                act.wait_ge(tq_q, c + 1)
                act.copy(QZT[:, 0, :], PS[:, 0, :]).then_inc(tq_qc, 1)
                if c:
                    act.wait_ge(tq_s, c)
                act.wait_ge(tq_z, c + 1)
                act.activation(hq[:, 0, :], PS[:, 1, :], ACT.Identity, bias=ST_B1C).then_inc(tq_th, 1)
                act.wait_ge(tq_th, 2 * c + 1)
                act.activation(hq[:, 1, :], hq[:, 0, :], ACT.Tanh, scale=0.5).then_inc(tq_th, 1)

            for c in range(NC):
                act.wait_ge(z0_ps, c + 1)
                act.copy(Z0T[:, c * 512:(c + 1) * 512], PS[:, c, :]).then_inc(z0_cp, 1)
            act.wait_ge(rms_ss[1], NT)
            act.activation(rms_sd[:, :], ssq[:, :], ACT.Sqrt, bias=eps[:, 1:2], scale=1.0 / D)\
                .then_inc(rms_sq[1], 1)
            for c in range(NC):
                act.wait_ge(xf_ps, c + 1)
                act.activation(XT[:, c * 512:(c + 1) * 512], PS[:, c, :], ACT.Copy, scale=w0("n2"))\
                    .then_inc(xf_cp, 1)

            def gate(layer, experts):
                act.wait_ge(gl_sub[layer], 1)
                act.activation(ge[:, :, 0:experts], lg[:, :, 0:experts], ACT.Exp).then_inc(gl_exp[layer], 1)

            gate(0, E0)

            with act.Fori(0, NC) as c:
                for u, (name, _, _, then, dst) in enumerate(units):
                    if then not in ("gelu", "silu"):
                        continue
                    wait(act, m0_pe, ("u", u), c)
                    if then == "gelu":
                        act.activation(hid[:, dst, :], PS[:, u % 6, :], ACT.Gelu).then_inc(m0_act.sem, 1)
                    else:
                        act.activation(e1t[:, name[1], :], PS[:, u % 6, :], ACT.Tanh, scale=0.5)\
                            .then_inc(m0_act.sem, 1)

            norm(1)
            gate(1, E1)

            def do_round(s, b, second=True, first=True):
                nb = 1 - b
                for r in ROUND:
                    if r[0] == "st" and second:
                        _, n, h = r
                        c, j = SWEEP_B[n]
                        w = 512 * (c + 1) - max(512 * c, P * j)
                        wait(act, s1_pe, r, s)
                        if n >= 2:
                            wait(act, s1_pe, ("pv", n - 2, h), s)
                        act.activation(pe_[:, h, n % 2, 0:w], PS[:, h, 0:w], ACT.Exp, scale=HD1 ** -0.5)\
                            .then_inc(s1_act.sem, 1)
                    elif r == "q" and first:
                        wait(act, f1_pe, "q", s + 1)
                        for h in range(2):
                            act.copy(QH[0:HD1, nb, h, :],
                                     PS[h * HD1:(h + 1) * HD1, 4:6, :].rearrange("p a n -> p (a n)"))\
                                .then_inc(f1_act.sem, 1)
                    elif r == "v" and first:
                        wait(act, f1_pe, "v", s + 1)
                        for half in range(2):
                            act.copy(VH[:, nb, :, 4 * half:4 * half + 4, 0:HD1],
                                     PS[:, 4 + half, :].rearrange("p (t h n) -> p h t n", t=4, h=2))\
                                .then_inc(f1_act.sem, 1)
                    elif r[0] == "mr" and first:
                        _, c, h = r
                        wait(act, f1_pe, r, s + 1)
                        act.copy(QH[HD1:HD1 + 1, nb, h, 512 * c:512 * (c + 1)], PS[0:1, 7 - h, :])\
                            .then_inc(f1_act.sem, 1)

            do_round(-1, 1, second=False)
            with act.Fori(0, H1 // 2 - 1) as hp:
                do_round(hp * 2, 0)
                do_round(hp * 2 + 1, 1)
            do_round(ROUNDS - 2, 0)
            do_round(ROUNDS - 1, 1, first=False)

            with act.Fori(0, E1 // 2) as ep:
                for u in range(2 * NM1):
                    wait(act, m1_pe, ("u", u), ep)
                    if u >= 3:
                        wait(act, m1_dve, ("mu", u - 3), ep)
                    else:
                        wait(act, m1_dve, ("mu", max(v for v in range(2 * NM1) if v % 3 == u)), ep, 1)
                    act.activation(GS[:, u % 3, :], PS[:, 2 * (u % 3), :], ACT.Silu).then_inc(m1_act.sem, 1)

        @block.vector
        def _(dve):
            count = [0]

            def link(ins):
                count[0] += 1
                ins.then_inc(dve_chain, 1)
                dve.wait_ge(dve_chain, count[0])

            for s in (t_dve, a0_dve, m0_dve, f1_dve, s1_dve, w1_dve, m1_dve):
                dve.sem_inc(s.sem, s.per_trip)
            dve.sem_inc(ttt_full.ew, 1)
            dve.wait_ge(const_ready, N_CONST)

            def norm(layer):
                for t in range(NT):
                    if layer == 0:
                        dve.wait_ge(x_loaded, 32)
                    link(dve.bn_stats(stats[:, t, :], X[:, t, :]))
                    dve.bn_aggr(mv[:, t, :], stats[:, t, :]).then_inc(ln_var[layer], 1)
                dve.wait_ge(ln_sd[layer], 1)
                link(dve.reciprocal(rstd[:, :], sd[:, :]))
                for t in range(NT):
                    dve.tensor_scalar(XN[:, t, :], X[:, t, :], mv[:, t, 0:1], rstd[:, t:t + 1], ALU.subtract,
                                      ALU.mult).then_inc(ln_done[layer], 1)
                dve.wait_ge(ln_done[layer], NT)

            def rms(which):
                for t in range(NT):
                    if t:
                        dve.wait_ge(rms_ss[which], t)
                    dve.tensor_tensor_reduce(junk[:, :], XN[:, t, :], XN[:, t, :], 1.0, 0.0, ALU.mult, ALU.add,
                                             ssq[:, t:t + 1]).then_inc(rms_ss[which], 1)
                dve.wait_ge(rms_sq[which], 1)

            norm(0)
            rms(0)
            dve.reciprocal(rms_r[:, :], rms_sd[:, :]).then_inc(ln_done[0], 1)
            dve.wait_ge(w0_loaded, 16)
            dve.tensor_scalar(wqkv_n[:, :], w0("wqkv"), w0("n1"), None, ALU.mult).then_inc(qkv_w, 1)
            a, b_ = W0_AT["w1"][0], W0_AT["w2t"][1]
            dve.tensor_copy(st0[:, 0:3 * P], W0[:, a:b_])
            dve.tensor_scalar(st0[:, 3 * P:4 * P], w0("b1_rows"), 0.5, None, ALU.mult)
            dve.tensor_scalar(st0[:, 4 * P:5 * P], w0("b2_rows"), 1.0 / D, None, ALU.mult)
            dve.tensor_copy(st0[:, 5 * P:5 * P + 1], w0("b1_col"))
            link(dve.tensor_scalar(st0[:, 5 * P + 1:5 * P + 2], w0("b2_col"), 1.0 / D, None, ALU.mult))
            link(dve.tensor_copy(st[:, :], st0[:, :]))
            dve.wait_ge(hsq, 1)
            dve.tensor_reduce(hss.rearrange("p (t h) -> p t h", t=NT),
                              LO.rearrange("p t (h e) -> p t h e", e=HD0), AX.X, ALU.add).then_inc(hsum, 1)
            dve.wait_ge(hroot, 1)
            link(dve.reciprocal(hss, hsd))
            qk4 = QKV[:, :, 0:2 * D].rearrange("p t (h e) -> p t h e", e=HD0)
            link(dve.tensor_tensor(qk4, qk4, hss.rearrange("p (t h) -> p t h", t=NT).unsqueeze(3)
                                   .broadcast_to([P, NT, 32, HD0]), ALU.mult))
            for a, name in enumerate(("qn", "kn")):
                part = QKV[:, :, a * D:(a + 1) * D].rearrange("p t (h e) -> p t h e", e=HD0)
                ins = dve.tensor_tensor(part, part, w0(name).unsqueeze(1).unsqueeze(1)
                                        .broadcast_to([P, NT, H0, HD0]), ALU.mult)
                if a == 0:
                    link(ins)
            ins.then_inc(hnorm, 1)
            dve.wait_ge(hhi, 1)
            dve.tensor_tensor(LO, QKV[:, :, 0:2 * D], HI, ALU.subtract).then_inc(hlo, 1)

            def ttt(run):
                n = P // 2
                with dve.Fori(0, CHUNKS) as c:
                    dve.wait_ge(run.th, run.ac(c))
                    dve.tensor_scalar(vb[:, 0, :], kv[:, 2, :], 1.0 / D, ST_B2C, ALU.mult, ALU.subtract)\
                        .then_inc(run.ew, 1)
                    dve.scalar_tensor_tensor(vb[:, 1, :], kv[:, 3, :], 1.0 / D, ST_B2, ALU.mult,
                                             ALU.subtract).then_inc(run.ew, 1)
                    dve.wait_ge(run.mm, run.pe(c, "base"))
                    dve.scalar_tensor_tensor(g1[:, :], PS[:, 1, 0:P], 1.0, lr_mask_h[:, :], ALU.add, ALU.mult)\
                        .then_inc(run.ew, 1)
                    dve.tensor_scalar(zb[:, 0, :], PS[:, 1, P:2 * P], ST_B1C, 0.5, ALU.add, ALU.mult)\
                        .then_inc(run.ew, 1)
                    dve.scalar_tensor_tensor(zb[:, 1, :], PS[:, 1, 2 * P:3 * P], 0.5, ST_B1, ALU.mult, ALU.add)\
                        .then_inc(run.ew, 1)
                    dve.memset(gr[:, 1, :, :], 0.0).then_inc(run.ew, 1)
                    with dve.Fori(0, run.trips) as trip:
                        for par in range(2):
                            sweep = trip * 2 + par
                            dve.wait_ge(run.mm, run.pe(c, "zc", sweep))
                            dve.wait_ge(run.ew, run.dv_before(c, sweep))
                            dve.tensor_tensor(zh[:, :, :], PS[:, 0, 0:2 * P].rearrange("p (a n) -> p a n", a=2),
                                              zb[:, :, :], ALU.add).then_inc(run.ew, 1)
                            dve.wait_ge(run.th, run.ac(c, sweep))
                            dve.scalar_tensor_tensor(sl[:, :, :], th[:, :, :], 1.0, zh[:, :, :], ALU.add, ALU.mult)\
                                .then_inc(run.ew, 1)
                            dve.wait_ge(run.mm, run.pe(c, "ys", sweep))
                            dve.scalar_tensor_tensor(g2[:, :], PS[:, 0, 2 * P:3 * P], 1.0, lr_mask[:, :], ALU.add,
                                                     ALU.mult).then_inc(run.ew, 1)
                            dve.wait_ge(run.ew, run.dv(c, "s", sweep))
                            dve.scalar_tensor_tensor(du[:, :], th[:, 1, :], 1.0, sl[:, 1, :], ALU.subtract,
                                                     ALU.mult).then_inc(run.ew, 1)
                            dve.wait_ge(run.ew, run.dv(c, "u", sweep))
                            dve.scalar_tensor_tensor(dd[:, :], th[:, 1, :], 1.0, du[:, :], ALU.add,
                                                     ALU.subtract).then_inc(run.ew, 1)
                            dve.wait_ge(run.mm, run.pe(c, "yc", sweep))
                            dve.scalar_tensor_tensor(gr[:, par, 0:2, :],
                                                     PS[:, 1, 0:2 * P].rearrange("p (a n) -> p a n", a=2),
                                                     1.0 / D, vb[:, :, :], ALU.mult, ALU.subtract)\
                                .then_inc(run.ew, 1)
                            dve.wait_ge(run.mm, run.pe(c, "ds", sweep))
                            dve.tensor_tensor(g3[:, :], PS[:, 0, 3 * P:4 * P], lr_mask[:, :], ALU.mult)\
                                .then_inc(run.ew, 1)
                            dve.wait_ge(run.mm, run.pe(c, "dc", sweep))
                            dve.wait_ge(run.ew, run.dv(c, "d", sweep))
                            dve.scalar_tensor_tensor(gr[:, par, 2, :], PS[:, 1, 2 * P:3 * P], 0.5, dd[:, :],
                                                     ALU.mult, ALU.mult).then_inc(run.ew, 1)
                    dve.wait_ge(run.mm, run.pe(c, "up"))
                    dve.scalar_tensor_tensor(st[:, 0:3 * P], PS[:, 0, 0:3 * P], -LR, st[:, 0:3 * P], ALU.mult,
                                             ALU.add).then_inc(run.ew, 1)
                    dve.scalar_tensor_tensor(ST_B1, PS[:, 0, 3 * P:4 * P], -LR / 2, ST_B1, ALU.mult, ALU.add)\
                        .then_inc(run.ew, 1)
                    dve.scalar_tensor_tensor(ST_B2, PS[:, 1, 0:P], -LR / D, ST_B2, ALU.mult, ALU.add)\
                        .then_inc(run.ew, 1)
                    dve.scalar_tensor_tensor(ST_B1C, PS[:, 1, P:P + 1], -LR, ST_B1C, ALU.mult, ALU.add)\
                        .then_inc(run.ew, 1)
                    dve.scalar_tensor_tensor(ST_B2C, PS[:, 1, P + 1:P + 2], -LR / D, ST_B2C, ALU.mult, ALU.add)\
                        .then_inc(run.ew, 1)
                dve.wait_ge(run.ew, CHUNKS * run.td + 1)

            def train_step(trip, q, name, k=None):
                def on(dep, *a):
                    wait(dve, t_dve, (q, dep) + a, trip)

                def done(ins):
                    ins.then_inc(t_dve.sem, 1)

                gd = None if k is None else gr[:, k % 2, :, :]
                src = zh if k else zb
                if name == "kv":
                    p, back = chunk_before(q)
                    wait(dve, t_dve, (p, CHECK[-1]), trip, back)
                    wait(dve, t_act, (q, "kv"), trip)
                    done(dve.tensor_scalar(vb[:, 0, :], kv[:, 2, :], 1.0 / D, ST_B2C, ALU.mult, ALU.subtract))
                    done(dve.scalar_tensor_tensor(vb[:, 1, :], kv[:, 3, :], 1.0 / D, ST_B2, ALU.mult, ALU.subtract))
                elif name == "base":
                    wait(dve, t_pe, (q, "base"), trip)
                    done(dve.scalar_tensor_tensor(g1[:, :], PS[:, 1, 0:P], 1.0, lr_mask_h[:, :], ALU.add, ALU.mult))
                    done(dve.tensor_scalar(zb[:, 0, :], PS[:, 1, P:2 * P], ST_B1C, 0.5, ALU.add, ALU.mult))
                    done(dve.scalar_tensor_tensor(zb[:, 1, :], PS[:, 1, 2 * P:3 * P], 0.5, ST_B1, ALU.mult, ALU.add))
                elif name == "zc":
                    if k:
                        wait(dve, t_pe, (q, "zc", k), trip)
                        on("s", k - 1)
                        done(dve.tensor_tensor(zh[:, :, :], PS[:, 1, 0:2 * P].rearrange("p (a n) -> p a n", a=2),
                                               zb[:, :, :], ALU.add))
                    wait(dve, t_act, (q, "th", k), trip)
                    on("z", k) if k else on("zb")
                    done(dve.scalar_tensor_tensor(sl[:, :, :], th[:, :, :], 1.0, src[:, :, :], ALU.add, ALU.mult))
                    on("s", k)
                    done(dve.scalar_tensor_tensor(du[:, :], th[:, 1, :], 1.0, sl[:, 1, :], ALU.subtract, ALU.mult))
                    on("u", k)
                    done(dve.scalar_tensor_tensor(dd[:, :], th[:, 1, :], 1.0, du[:, :], ALU.add, ALU.subtract))
                elif name == "y":
                    wait(dve, t_pe, (q, "y", k), trip)
                    done(dve.scalar_tensor_tensor(gd[:, 0:2, :], PS[:, 1, 0:2 * P].rearrange("p (a n) -> p a n", a=2),
                                                  1.0 / D, vb[:, :, :], ALU.mult, ALU.subtract))
                elif name == "ds":
                    wait(dve, t_pe, (q, "ds", k), trip)
                    done(dve.tensor_tensor(g3[:, :], PS[:, 0, 3 * P:4 * P], lr_mask[:, :], ALU.mult))
                elif name == "dc":
                    wait(dve, t_pe, (q, "dc", k), trip)
                    on("d", k)
                    done(dve.scalar_tensor_tensor(gd[:, 2, :], PS[:, 1, 2 * P:3 * P], 0.5, dd[:, :], ALU.mult,
                                                  ALU.mult))
                    if k + 1 < SWEEPS:
                        wait(dve, t_pe, (q, "ss", k), trip)
                        done(dve.scalar_tensor_tensor(g2[:, :], PS[:, 0, 2 * P:3 * P], 1.0, lr_mask[:, :], ALU.add,
                                                      ALU.mult))
                elif name == "up":
                    wait(dve, t_pe, (q, "up"), trip)
                    for dst, bank, lo, hi, by in ((st[:, 0:3 * P], 0, 0, 3 * P, -LR), (ST_B1, 0, 3 * P, 4 * P, -LR / 2),
                                                  (ST_B2, 1, 0, P, -LR / D), (ST_B1C, 1, P, P + 1, -LR),
                                                  (ST_B2C, 1, P + 1, P + 2, -LR / D)):
                        done(dve.scalar_tensor_tensor(dst, PS[:, bank, lo:hi], by, dst, ALU.mult, ALU.add))
                    on("dz", SWEEPS - 1)
                    done(dve.tensor_tensor(cdiff[:, :, :], gr[:, 1, 1:3, :], gr[:, 0, 1:3, :], ALU.subtract))
                    done(dve.tensor_reduce(cmax[:, :], gr[:, 1, 1:3, :], AX.X, ALU.max, apply_absolute_value=True))
                    on("cm")
                    done(dve.tensor_scalar(cmax[:, :], cmax[:, :], CONVERGED, 1e-30, ALU.mult, ALU.add))
                    on("ct")
                    for i, sign in enumerate((1.0, -1.0)):
                        done(dve.scalar_tensor_tensor(cin[:, i, :, :], cdiff[:, :, :], sign,
                                                      cmax[:, :].unsqueeze(2).broadcast_to([P, 2, P]), ALU.mult,
                                                      ALU.is_lt))
                    on("cn")
                    done(dve.tensor_reduce(cok[:, :], cin[:, :, :, :], AX.XYZ, ALU.min))
                    on("cr")
                    done(dve.tensor_tensor(okay[:, :], okay[:, :], cok[:, :], ALU.min))

            with dve.Fori(0, B) as b:
                with dve.Fori(0, H0 // HG) as g:
                    trip = b * (H0 // HG) + g
                    for r in TRIP:
                        if r[0] == "t":
                            train_step(trip, *r[1:])
                        elif r[0] == "tk":
                            wait(dve, a0_pe, r, trip)
                            dve.tensor_copy(kta[:, 512 * r[1]:512 * (r[1] + 1)], PS[:, 6, :]).then_inc(a0_dve.sem, 1)
                        elif r[0] == "a":
                            c, h, i, k = PIECES0[r[1]]
                            wait(dve, a0_pe, r, trip)
                            col = 32 * h + QM
                            if c == 0:
                                dst = tmq[:, i, col:col + 1]
                            else:
                                dst = NMH0[:, h, i - 4, k:k + 1]
                            dve.tensor_reduce(dst, PS[:, 2 + r[1] % 4, 0:min(512, (i + 1) * P - 512 * k)], AX.X,
                                              ALU.max, negate=True).then_inc(a0_dve.sem, 1)
                            if (c, i, k) == (1, TB - 1, 1):
                                wait(dve, a0_dve, ("mx", r[1]), trip)
                                dve.tensor_tensor(tmq[:, 4:8, col], NMH0[:, h, :, 0], NMH0[:, h, :, 1], ALU.min)\
                                    .then_inc(a0_dve.sem, 1)
                        elif r[0] == "pv" and r[1] in LAST:
                            wait(dve, a0_pe, r, trip)
                            dve.tensor_copy(ots[:, LAST.index(r[1]), :], PS[:, 6, :]).then_inc(a0_dve.sem, 1)
                        elif r[0] == "to":
                            c = r[1]
                            wait(dve, a0_pe, r, trip)
                            ov = PS[:, 7, :].rearrange("p (i h n) -> p (i h) n", i=4, h=HG)
                            dve.reciprocal(rz[:, c, :], ov[:, :, HD0]).then_inc(a0_dve.sem, 1)
                            wait(dve, a0_dve, ("rc", c), trip)
                            dst = Z0[:, bass.ds(b * TB + 4 * c, 4), bass.ds(g * (HG * HD0), HG * HD0)]
                            dve.tensor_tensor(dst.rearrange("p t (h e) -> p t h e", h=HG),
                                              ov[:, :, 0:HD0].rearrange("p (i h) n -> p i h n", i=4),
                                              rz[:, c, :].rearrange("p (i h) -> p i h", i=4).unsqueeze(3)
                                              .broadcast_to([P, 4, HG, HD0]), ALU.mult).then_inc(a0_dve.sem, 1)
            dve.wait_ge(t_dve.sem, t_dve.at((1, CHECK[-1]), TRIPS - 1))

            dve.tensor_copy(cok[:, :], okay[:, :]).then_inc(ttt_okay, 1)
            dve.wait_ge(ttt_sum, 1)
            link(dve.tensor_scalar(flag_f[0:1, 0:1], PS[0:1, 2, 0:1], P - 0.5, None, ALU.is_ge))
            dve.tensor_copy(flag_i[0:1, 0:1], flag_f[0:1, 0:1]).then_inc(ttt_flag, 1)
            dve.wait_ge(ttt_flag, 1)
            settled = dve.value_load(flag_i[0:1, 0:1], min_val=0, max_val=1)
            with dve.If(settled == 0):
                dve.tensor_copy(st[:, :], st0[:, :]).then_inc(ttt_reset, 1)
                dve.wait_ge(ttt_reset, 1)
                ttt(ttt_full)
            with dve.Else():
                dve.nop()
            dve.scalar_tensor_tensor(X[:, :, :], ST_B2.unsqueeze(1).broadcast_to([P, NT, D]), float(D), X[:, :, :],
                                     ALU.mult, ALU.add).then_inc(ttt_settled, 1)
            for c in range(NC):
                dve.wait_ge(tq_th, 2 * c + 2)
                if c:
                    dve.wait_ge(tq_y, c)
                link(dve.scalar_tensor_tensor(QZT[:, 1, :], hq[:, 1, :], 1.0, hq[:, 0, :], ALU.add, ALU.mult))
                dve.tensor_scalar(QZT[:, 1, :], QZT[:, 1, :], 0.5, None, ALU.mult).then_inc(tq_s, 1)
                dve.wait_ge(tq_y, c + 1)
                dve.wait_ge(ttt_settled, 1)
                xs = X[:, 4 * c:4 * c + 4, :]
                dve.tensor_tensor(xs, PS[:, 2, :].rearrange("p (t n) -> p t n", t=4), xs, ALU.add)\
                    .then_inc(tq_acc, 1)

            for c in range(NC):
                dve.wait_ge(ao_ps, c + 1)
                xs = XN[:, 4 * c:4 * c + 4, M_ZERO:D]
                dve.tensor_tensor(xs, PS[:, 4 + c, :].rearrange("p (t n) -> p t n", t=4)[:, :, 0:D - M_ZERO], xs,
                                  ALU.add).then_inc(ao_add, 1)
            dve.wait_ge(ao_add, NC)
            rms(1)
            link(dve.reciprocal(rms_r[:, :], rms_sd[:, :]))
            for t in range(NT):
                dve.tensor_scalar(Z0[:, t, :], XN[:, t, :], rms_r[:, t:t + 1], None, ALU.mult).then_inc(xf_tile, 1)
            dve.wait_ge(tq_acc, NC)
            dve.tensor_tensor(X[:, :, :], X[:, :, :], XN[:, :, :], ALU.add).then_inc(x_plus, 1)

            def gate(layer, experts, wts):
                n = experts
                l, e_, p_ = lg[:, :, 0:n], ge[:, :, 0:n], gp[:, :, 0:n]
                dve.wait_ge(gl_ps[layer], 1)
                ps = PS[:, 6, 0:NT * n].rearrange("p (t e) -> p t e", e=n)
                if layer == 0:
                    link(dve.tensor_copy(p_, ps))
                    link(dve.memset(l, 0.0))
                    link(dve.tensor_tensor(lgm[:, :, 0:n], p_, p_, ALU.is_equal))
                    link(dve.copy_predicated(l, lgm[:, :, 0:n], p_))
                    big = float(np.finfo(np.float32).max)
                    link(dve.tensor_scalar(l, l, big, -big, ALU.min, ALU.max))
                else:
                    link(dve.tensor_copy(l, ps))

                def rows(v):
                    return v.unsqueeze(2).broadcast_to([P, NT, n])

                link(dve.tensor_reduce(lgx[:, :], l, AX.X, ALU.max))
                dve.tensor_tensor(l, l, rows(lgx[:, :]), ALU.subtract).then_inc(gl_sub[layer], 1)
                dve.wait_ge(gl_exp[layer], 1)
                link(dve.tensor_reduce(lgx[:, :], e_, AX.X, ALU.add))
                link(dve.reciprocal(wsum[:, :], lgx[:, :]))
                link(dve.tensor_tensor(p_, e_, rows(wsum[:, :]), ALU.mult))
                cmp = gc[:, 0:n, 0:NT * n].rearrange("p f (t e) -> p f t e", e=n)
                link(dve.memset(gc[:, 0:n, 0:NT * n], 0.0))
                for f in range(n):
                    def other(k):
                        return p_[:, :, f:f + 1].broadcast_to([P, NT, k])
                    if f + 1 < n:
                        ins = dve.tensor_tensor(cmp[:, f, :, f + 1:n], other(n - 1 - f), p_[:, :, f + 1:n],
                                                ALU.is_ge)
                    if f:
                        ins = dve.tensor_tensor(cmp[:, f, :, 0:f], other(f), p_[:, :, 0:f], ALU.is_gt)
                link(ins)
                link(dve.tensor_reduce(rank[:, :, 0:n].rearrange("p t e -> p t e"),
                                       gc[:, 0:n, 0:NT * n].rearrange("p f (t e) -> p t e f", e=n), AX.X, ALU.add))
                link(dve.scalar_tensor_tensor(e_, rank[:, :, 0:n], 1.5, p_, ALU.is_lt, ALU.mult))
                link(dve.tensor_reduce(lgx[:, :], e_, AX.X, ALU.add))
                link(dve.tensor_scalar(lgx[:, :], lgx[:, :], 1e-8, None, ALU.add))
                link(dve.reciprocal(wsum[:, :], lgx[:, :]))
                dve.tensor_tensor(wts[:, :, :].rearrange("p e t -> p t e"), e_, rows(wsum[:, :]), ALU.mult)\
                    .then_inc(gl_done[layer], 1)
                dve.wait_ge(gl_done[layer], 1)

            gate(0, E0, wt0)

            dve.wait_ge(x_plus, 1)
            with dve.Fori(0, NC) as c:
                for kind, u in seq0:
                    if kind == "dn":
                        bank = 6 + dn_order.index(u) % 2
                        wait(dve, m0_pe, ("dn", u), c)
                        for i in range(4):
                            if u != dn_order[0]:
                                wait(dve, m0_dve, ("ac", dn_order[dn_order.index(u) - 1], i), c)
                            xs = X[:, bass.ds(c * 4 + i, 1), M_ZERO:D]
                            dve.scalar_tensor_tensor(
                                xs, PS[:, bank, i * P:i * P + D - M_ZERO].unsqueeze(1),
                                wt0[:, u, bass.ds(c * 4 + i, 1)], xs, ALU.mult, ALU.add).then_inc(m0_dve.sem, 1)
                        continue
                    then = units[u][3]
                    m = units[u][0][1]
                    if then == "silu":
                        wait(dve, m0_act, ("u", u), c)
                        dve.scalar_tensor_tensor(hid[:, HU[("e1g", m)], :], e1t[:, m, :], 1.0, PS[:, u % 6, :],
                                                 ALU.add, ALU.mult).then_inc(m0_dve.sem, 1)
                    elif then == "times":
                        wait(dve, m0_pe, ("u", u), c)
                        wait(dve, m0_dve, ("sg", 2 + m), c)
                        dve.scalar_tensor_tensor(hid[:, HU[("e1v", m)], :], hid[:, HU[("e1g", m)], :], 0.5,
                                                 PS[:, u % 6, :], ALU.mult, ALU.mult).then_inc(m0_dve.sem, 1)
            dve.wait_ge(m0_dve.sem, m0_dve.at(dve0[-1], NC - 1))

            norm(1)
            gate(1, E1, wt1)

            def do_round(s, b, second=True, first=True):
                for r in ROUND:
                    if r[0] == "pv" and r[1] in LAST and second:
                        _, n, h = r
                        c = LAST.index(n)
                        wait(dve, s1_pe, r, s)
                        wait(dve, w1_pe, ("w", c, 2), s, 1)
                        dve.tensor_copy(ZT[0:HD1 + 1, h, c, :], PS[0:HD1 + 1, 2 + h, :]).then_inc(s1_dve.sem, 1)
                    elif r[0] == "w" and second:
                        _, c, g = r
                        bank = W_BANK[(c, g)]
                        lo, n = GROUPS[g][0], len(GROUPS[g])
                        wait(dve, w1_pe, r, s)
                        if (c, g) == (0, 0):
                            wait(dve, w1_dve, ("x", 1, 7), s, 1)
                        view = PS[:, bank, 0:n * (D + 1)].rearrange("p (q n) -> p q n", q=n)
                        dve.reciprocal(RS[:, c, lo:lo + n], view[:, :, D]).then_inc(w1_dve.sem, 1)
                        wait(dve, w1_dve, ("rs", c, g), s)
                        for q in GROUPS[g]:
                            t = TB * b + 4 * c + q // 2
                            if q % 2:
                                wait(dve, w1_dve, ("x", c, q - 1), s)
                            dve.scalar_tensor_tensor(X[:, t, :], view[:, q - lo, 0:D], RS[:, c, q:q + 1], X[:, t, :],
                                                     ALU.mult, ALU.add).then_inc(w1_dve.sem, 1)
                    elif r == "k" and first:
                        wait(dve, f1_pe, "k", s + 1)
                        for h in range(2):
                            dve.tensor_copy(KH[0:HD1, 1 - b, h, :],
                                            PS[h * HD1:(h + 1) * HD1, 6:8, :].rearrange("p a n -> p (a n)"))\
                                .then_inc(f1_dve.sem, 1)
                    elif r[0] == "a" and first:
                        p = r[1]
                        c, h, i, k = PIECES[p]
                        w = min(512, (i + 1) * P - 512 * k)
                        wait(dve, f1_pe, r, s + 1)
                        dst = NMH[:, h, i - 4, k:k + 1] if c else NM[:, h, i:i + 1]
                        if p == 8:
                            wait(dve, f1_dve, ("cb", 1), s + 1, 1)
                        dve.tensor_reduce(dst, PS[:, 4 + p % 2, 0:w], AX.X, ALU.max, negate=True)\
                            .then_inc(f1_dve.sem, 1)
                        if p in (15, 23):
                            wait(dve, f1_dve, ("mx", p), s + 1)
                            dve.tensor_tensor(NM[:, h, 4:8], NMH[:, h, :, 0], NMH[:, h, :, 1], ALU.min)\
                                .then_inc(f1_dve.sem, 1)

            do_round(-1, 1, second=False)
            with dve.Fori(0, H1 // 2 - 1) as hp:
                do_round(hp * 2, 0)
                do_round(hp * 2 + 1, 1)
            do_round(ROUNDS - 2, 0)
            do_round(ROUNDS - 1, 1, first=False)
            dve.wait_ge(w1_dve.sem, w1_dve.at(("x", 1, 7), ROUNDS - 1))

            with dve.Fori(0, E1 // 2) as ep:
                for m in range(NM1 + 1):
                    if m < NM1:
                        for u in (2 * m, 2 * m + 1):
                            wait(dve, m1_act, ("u", u), ep)
                            if m >= 2:
                                wait(dve, m1_pe, ("dn", m - 2), ep)
                            dve.tensor_tensor(HB[:, m % 2, u % 2, :], GS[:, u % 3, :], PS[:, 2 * (u % 3) + 1, :],
                                              ALU.mult).then_inc(m1_dve.sem, 1)
                    if m >= 1:
                        k = m - 1
                        wait(dve, m1_pe, ("dn", k), ep)
                        for i in range(4):
                            t = (k % NC) * 4 + i
                            if k >= NC:
                                wait(dve, m1_dve, ("ac", k - NC, i), ep)
                            else:
                                wait(dve, m1_dve, ("ac", k + NC, i), ep, 1)
                            dve.scalar_tensor_tensor(
                                X[:, t, :], PS[:, 6 + k % 2, i * P:(i + 1) * P],
                                wt1[:, bass.ds(ep * 2 + k // NC, 1), t], X[:, t, :], ALU.mult, ALU.add)\
                                .then_inc(m1_dve.sem, 1)

        @block.tensor
        def _(pe):
            for s in (t_pe, a0_pe, m0_pe, f1_pe, s1_pe, w1_pe, m1_pe):
                pe.sem_inc(s.sem, s.per_trip)
            pe.sem_inc(ttt_full.mm, 1)
            pe.wait_ge(const_ready, N_CONST)

            def turn(layer, src, ready, done, first_bank=0):
                for t in range(NT):
                    if ready is not None:
                        pe.wait_ge(ready, t + 1)
                    ins = pe.transpose(PS[:, first_bank + t // 4, (t % 4) * P:(t % 4 + 1) * P], src[:, t, :],
                                       ident[:, :])
                    if t % 4 == 3:
                        ins.then_inc(done, 1)

            turn(0, XN, ln_done[0], xt_ps[0])
            pe.wait_ge(qkv_w, 1)
            for t in range(NT):
                pe.wait_ge(xt_done[0], t // 4 + 1)
                if t >= 4:
                    pe.wait_ge(qkv_done, t - 3)
                pe.matmul(PS[:, 4 + t % 4, 0:3 * D], XT[:, t * P:(t + 1) * P], wqkv_n[:, :], start=True, stop=True)\
                    .then_inc(qkv_ps, 1)

            def mm(*args, **kw):
                return pe.matmul(*args, skip_group_check=True, **kw)

            def ttt(run):
                def ps(bank, k):
                    return PS[:, bank, k * P:(k + 1) * P]

                xcv = xc[:, :, :].rearrange("p b s -> p (b s)")
                with pe.Fori(0, CHUNKS) as c:
                    pe.wait_ge(run.staged, c + 1)
                    pe.wait_ge(run.ew, c * run.td + 1)
                    wk, wv = w0("wk_ttt"), w0("wv_ttt")
                    mm(ps(0, 0), wk, xcv, start=True, stop=True)
                    mm(ps(0, 1), xcv, wk, start=True, stop=True)
                    mm(ps(0, 2), wv, xcv, start=True, stop=True)
                    mm(ps(0, 3), xcv, wv, start=True, stop=True).then_inc(run.mm, 1)
                    pe.wait_ge(run.th, run.ac(c))
                    mm(ps(1, 0), kv[:, 0, :], kv[:, 0, :], start=True, stop=True)
                    mm(ps(1, 1), ST_W1, kv[:, 0, :], start=True, stop=True)
                    mm(ps(1, 2), kv[:, 0, :], ST_W1, start=True, stop=True).then_inc(run.mm, 1)
                    with pe.Fori(0, run.trips) as trip:
                        for par in range(2):
                            sweep = trip * 2 + par
                            dyo, dzo = gr[:, 1 - par, 1, :], gr[:, 1 - par, 2, :]
                            dyt = gr[:, par, 0, :]
                            s_t, s_tm = sl[:, 0, :], sl[:, 1, :]
                            pe.wait_ge(run.ew, run.dv_before(c, sweep))
                            mm(ps(0, 0), dzo, g1[:, :], start=True, stop=True)
                            mm(ps(0, 1), g1[:, :], dzo, start=True, stop=True).then_inc(run.mm, 1)
                            pe.wait_ge(run.ew, run.dv(c, "s", sweep))
                            mm(ps(0, 2), s_t, s_t, start=True, stop=True)
                            mm(ps(1, 0), ST_W2, s_t, start=True, stop=False)
                            mm(ps(1, 1), s_t, ST_W2, start=False, stop=False).then_inc(run.mm, 1)
                            pe.wait_ge(run.ew, run.dv(c, "g2", sweep))
                            mm(ps(1, 0), dyo, g2[:, :], start=False, stop=False)
                            mm(ps(1, 1), g2[:, :], dyo, start=False, stop=True).then_inc(run.mm, 1)
                            pe.wait_ge(run.ew, run.dv(c, "dy", sweep))
                            mm(ps(0, 3), dyt, dyt, start=True, stop=True)
                            mm(ps(1, 2), dyt, ST_W2T, start=True, stop=False).then_inc(run.mm, 1)
                            pe.wait_ge(run.ew, run.dv(c, "g3", sweep))
                            mm(ps(1, 2), g3[:, :], s_tm, start=False, stop=True).then_inc(run.mm, 1)
                    pe.wait_ge(run.ew, run.dv_before(c, run.sweeps))
                    dy, dz, s_tm = gr[:, 1, 1, :], gr[:, 1, 2, :], sl[:, 1, :]
                    mm(ps(0, 0), kv[:, 1, :], dz, start=True, stop=True)
                    mm(ps(0, 1), s_tm, dy, start=True, stop=True)
                    mm(ps(0, 2), dy, s_tm, start=True, stop=True)
                    mm(ps(0, 3), ones[:, :], dz, start=True, stop=True)
                    mm(ps(1, 0), ones[:, :], dy, start=True, stop=True)
                    mm(PS[:, 1, P:P + 1], dz, ones[:, 0:1], start=True, stop=True)
                    mm(PS[:, 1, P + 1:P + 2], dy, ones[:, 0:1], start=True, stop=True).then_inc(run.mm, 1)

            def train_step(trip, q, name, k=None):
                def ps(bank, i):
                    return PS[:, bank, i * P:(i + 1) * P]

                def on(dep, *a):
                    wait(pe, t_dve, (q, dep) + a, trip)

                xcv = xc[:, :, :].rearrange("p b s -> p (b s)")
                s_t, s_tm = sl[:, 0, :], sl[:, 1, :]
                if name == "kv":
                    wait(pe, t_pool, (q, "xc"), trip)
                    p, back = chunk_before(q)
                    wait(pe, t_dve, (p, "b1"), trip, back)
                    wk, wv = w0("wk_ttt"), w0("wv_ttt")
                    mm(ps(0, 0), wk, xcv, start=True, stop=True)
                    mm(ps(0, 1), xcv, wk, start=True, stop=True)
                    mm(ps(0, 2), wv, xcv, start=True, stop=True)
                    mm(ps(0, 3), xcv, wv, start=True, stop=True).then_inc(t_pe.sem, 1)
                elif name == "base":
                    p, back = chunk_before(q)
                    wait(pe, t_dve, (p, "b2c"), trip, back)
                    wait(pe, t_act, (q, "kv"), trip)
                    mm(ps(1, 0), kv[:, 0, :], kv[:, 0, :], start=True, stop=True)
                    mm(ps(1, 1), ST_W1, kv[:, 0, :], start=True, stop=True)
                    mm(ps(1, 2), kv[:, 0, :], ST_W1, start=True, stop=True).then_inc(t_pe.sem, 1)
                elif name == "zc" and k:
                    dzo = gr[:, 1 - k % 2, 2, :]
                    on("dz", k - 1)
                    mm(ps(1, 0), dzo, g1[:, :], start=True, stop=True)
                    mm(ps(1, 1), g1[:, :], dzo, start=True, stop=True).then_inc(t_pe.sem, 1)
                elif name == "y":
                    on("s", k)
                    mm(ps(1, 0), ST_W2, s_t, start=True, stop=not k)
                    ins = mm(ps(1, 1), s_t, ST_W2, start=False, stop=not k)
                    if k:
                        dyo = gr[:, 1 - k % 2, 1, :]
                        mm(ps(1, 0), dyo, g2[:, :], start=False, stop=False)
                        ins = mm(ps(1, 1), g2[:, :], dyo, start=False, stop=True)
                    ins.then_inc(t_pe.sem, 1)
                elif name == "ds":
                    dyt = gr[:, k % 2, 0, :]
                    on("dy", k)
                    mm(ps(0, 3), dyt, dyt, start=True, stop=True).then_inc(t_pe.sem, 1)
                    mm(ps(1, 2), dyt, ST_W2T, start=True, stop=False)
                elif name == "dc":
                    on("g3", k)
                    mm(ps(1, 2), g3[:, :], s_tm, start=False, stop=True).then_inc(t_pe.sem, 1)
                    if k + 1 < SWEEPS:
                        mm(ps(0, 2), s_t, s_t, start=True, stop=True).then_inc(t_pe.sem, 1)
                elif name == "up":
                    on("dz", SWEEPS - 1)
                    dy, dz = gr[:, 1, 1, :], gr[:, 1, 2, :]
                    mm(ps(0, 0), kv[:, 1, :], dz, start=True, stop=True)
                    mm(ps(0, 1), s_tm, dy, start=True, stop=True)
                    mm(ps(0, 2), dy, s_tm, start=True, stop=True)
                    mm(ps(0, 3), ones[:, :], dz, start=True, stop=True)
                    mm(ps(1, 0), ones[:, :], dy, start=True, stop=True)
                    mm(PS[:, 1, P:P + 1], dz, ones[:, 0:1], start=True, stop=True)
                    mm(PS[:, 1, P + 1:P + 2], dy, ones[:, 0:1], start=True, stop=True).then_inc(t_pe.sem, 1)

            pe.wait_ge(hlo, 1)
            with pe.Fori(0, TRIPS) as trip:
                for r in TRIP:
                    if r[0] == "t":
                        train_step(trip, *r[1:])
                    elif r[0] in ("tq", "tk", "tq2", "to"):
                        kind, half = r
                        tm, bank = {"tq": (tmq, 7), "tk": (tmk, 6), "tq2": (tmq, 7), "to": (None, 7)}[kind]
                        if kind == "tq":
                            pe.wait_ge(a0_pool.sem, trip * 3 + 2)
                            if half:
                                wait(pe, a0_act, ("qa", 0), trip)
                            else:
                                wait(pe, a0_dve, ("zt", 1), trip, 1)
                        elif kind == "tk":
                            pe.wait_ge(a0_pool.sem, trip * 3 + 1)
                            if half:
                                wait(pe, a0_dve, ("ka", 0), trip)
                            else:
                                wait(pe, a0_dve, ("oc", 1), trip, 1)
                        elif kind == "tq2":
                            wait(pe, a0_dve, ("cb", HG - 1) if half else ("mx", P0_HALF - 1), trip)
                            wait(pe, a0_act, ("qb", 0) if half else ("qa", 1), trip)
                        else:
                            wait(pe, a0_dve, ("oc", half), trip)
                            if half:
                                wait(pe, a0_dve, ("zt", 0), trip)
                            else:
                                wait(pe, a0_act, ("qb", 1), trip)
                        for i in range(4):
                            src = tm[:, 4 * half + i, :] if tm is not None else ots[:, half, i * P:(i + 1) * P]
                            ins = pe.transpose(PS[:, bank, i * P:(i + 1) * P], src, ident[:, :])
                        ins.then_inc(a0_pe.sem, 1)
                    elif r[0] == "a":
                        p = r[1]
                        c, h, i, k = PIECES0[p]
                        w = min(512, (i + 1) * P - 512 * k)
                        bank, rows = 2 + p % 4, slice(32 * h, 32 * h + 32)
                        if p == 0:
                            wait(pe, a0_act, ("qa", 1), trip)
                            wait(pe, a0_dve, ("ka", 1), trip)
                        if p >= 4:
                            wait(pe, a0_dve, ("mx", p - 4), trip)
                        else:
                            wait(pe, a0_act, ("ex", NB - 1, p), trip, 1)
                        ins = pe.matmul(PS[:, bank, 0:w], qta[rows, i * P:(i + 1) * P],
                                        kta[rows, 512 * k:512 * k + w], start=True, stop=True)
                        if k == c:
                            ins = pe.matmul(PS[:, bank, w - P:w], ident_b[:, :], mask_qk[:, :], start=False,
                                            stop=True, skip_group_check=True)
                        ins.then_inc(a0_pe.sem, 1)
                    elif r[0] == "st":
                        _, n, h = r
                        c, j = SWEEP_B[n]
                        q0 = max(512 * c, P * j)
                        w = 512 * (c + 1) - q0
                        rows = slice(32 * h, 32 * h + 32)
                        if n:
                            wait(pe, a0_act, ("ex", n - 1, h), trip)
                        else:
                            wait(pe, a0_act, ("qb", 1), trip)
                        ins = pe.matmul(PS[:, 2 + h, 0:w], kta[rows, j * P:(j + 1) * P], qtb[rows, q0:q0 + w],
                                        start=True, stop=True)
                        if j >= 4 * c:
                            ins = pe.matmul(PS[:, 2 + h, 0:P], ident_b[:, :], mask_kq[:, :], start=False, stop=True,
                                            skip_group_check=True)
                        ins.then_inc(a0_pe.sem, 1)
                    elif r[0] == "pv":
                        n = r[1]
                        c, j = SWEEP_B[n]
                        q0 = max(512 * c, P * j)
                        if n == 0:
                            pe.wait_ge(a0_pool.sem, trip * 3 + 3)
                            wait(pe, a0_dve, ("ka", 1), trip)
                        elif j == 0:
                            wait(pe, a0_dve, ("oc", 0), trip)
                        for h in range(HG):
                            wait(pe, a0_act, ("ex", n, h), trip)
                            ins = pe.matmul(PS[32 * h:32 * h + 32, 6, q0 - 512 * c:512],
                                            tmv[:, j, 32 * h:32 * h + 32], pe_[:, h, n % 2, 0:512 * (c + 1) - q0],
                                            start=(j == 0), stop=(j == 4 * c + 3), skip_group_check=True)
                        ins.then_inc(a0_pe.sem, 1)
            pe.wait_ge(a0_dve.sem, a0_dve.at(("zt", 1), TRIPS - 1))

            pe.wait_ge(ttt_okay, 1)
            pe.matmul(PS[0:1, 2, 0:1], cok[:, :], ones[:, 0:1], start=True, stop=True).then_inc(ttt_sum, 1)
            pe.wait_ge(ttt_flag, 1)
            settled = pe.value_load(flag_i[0:1, 0:1], min_val=0, max_val=1)
            with pe.If(settled == 0):
                pe.wait_ge(ttt_reset, 1)
                ttt(ttt_full)
            with pe.Else():
                pe.nop()

            pe.wait_ge(ttt_settled, 1)
            for c in range(NC):
                if c:
                    pe.wait_ge(tq_qc, c)
                pe.matmul(PS[:, 0, :], w0("wq_ttt"), XT[:, c * 512:(c + 1) * 512], start=True, stop=True)\
                    .then_inc(tq_q, 1)
                pe.wait_ge(tq_qc, c + 1)
                if c:
                    pe.wait_ge(tq_th, 2 * c)
                pe.matmul(PS[:, 1, :], ST_W1, QZT[:, 0, :], start=True, stop=True).then_inc(tq_z, 1)
                pe.wait_ge(tq_s, c + 1)
                if c:
                    pe.wait_ge(tq_acc, c)
                for i in range(4):
                    ins = pe.matmul(PS[:, 2, i * P:(i + 1) * P], QZT[:, 1, i * P:(i + 1) * P], ST_W2, start=True,
                                    stop=True)
                ins.then_inc(tq_y, 1)
            pe.wait_ge(tq_acc, NC)

            turn(0, Z0, None, z0_ps)
            for t in range(NT):
                pe.wait_ge(z0_cp, t // 4 + 1)
                ins = pe.matmul(PS[:, 4 + t // 4, (t % 4) * P:(t % 4) * P + D - M_ZERO], Z0T[:, t * P:(t + 1) * P],
                                w0("wo", M_ZERO), start=True, stop=True)
                if t % 4 == 3:
                    ins.then_inc(ao_ps, 1)
            turn(0, Z0, xf_tile, xf_ps)
            pe.wait_ge(ao_add, NC)
            pe.wait_ge(xf_cp, NC)

            def gate(layer, weights, experts):
                for t in range(NT):
                    ins = pe.matmul(PS[:, 6, t * experts:(t + 1) * experts], XT[:, t * P:(t + 1) * P], weights,
                                    start=True, stop=True)
                ins.then_inc(gl_ps[layer], 1)

            gate(0, w0("gate"), E0)
            pe.wait_ge(gl_sub[0], 1)

            with pe.Fori(0, NC) as c:
                for kind, u in seq0:
                    if kind == "u":
                        name, blocks, rhs, then, dst = units[u]
                        if u >= 6:
                            s, step = unit_freed(u - 6)
                            wait(pe, s, step, c)
                        else:
                            s, step = unit_freed(max(v for v in range(15) if v % 6 == u))
                            wait(pe, s, step, c, 1)
                        for k, (lhs, r) in enumerate(zip(blocks, rhs)):
                            if r is None:
                                src = XT[:, bass.ts(c, 512)]
                            else:
                                made = next(v for v, s_ in enumerate(units) if s_[4] == r)
                                wait(pe, m0_act, ("u", made), c)
                                src = hid[:, r, :]
                            ins = pe.matmul(PS[:, u % 6, :], lhs, src, start=(k == 0), stop=(k == len(blocks) - 1))
                        ins.then_inc(m0_pe.sem, 1)
                    else:
                        wname, src = DOWN[u]
                        place = dn_order.index(u)
                        bank = 6 + place % 2
                        for k in range(2):
                            if u == 1:
                                wait(pe, m0_dve, ("tm", 4 + k), c)
                            else:
                                made = next(v for v, s_ in enumerate(units) if s_[4] == HU[(src, k)])
                                wait(pe, m0_act, ("u", made), c)
                        if place >= 2:
                            wait(pe, m0_dve, ("ac", dn_order[place - 2], 3), c)
                        else:
                            wait(pe, m0_dve, ("ac", dn_order[place + 2], 3), c, 1)
                        for i in range(4):
                            for k in range(2):
                                ins = pe.matmul(PS[:, bank, i * P:i * P + D - M_ZERO],
                                                hid[:, HU[(src, k)], i * P:(i + 1) * P],
                                                w0(wname, k * D + M_ZERO, (k + 1) * D), start=(k == 0), stop=(k == 1))
                        ins.then_inc(m0_pe.sem, 1)

            pe.wait_ge(m0_act.sem, m0_act.at(m0_act.names[-1], NC - 1))
            pe.wait_ge(m0_dve.sem, m0_dve.at(dve0[-1], NC - 1))
            turn(1, XN, ln_done[1], xt_ps[1])
            pe.wait_ge(xt_done[1], NC)
            pe.wait_ge(w1_loaded, 16)
            gate(1, w1("gate"), E1)
            pe.wait_ge(gl_sub[1], 1)
            pe.wait_ge(a1_ones, 1)

            pe.wait_ge(wo_loaded, 32)

            def do_round(s, b, hp, next_hp, second=True, first=True):
                nb = 1 - b
                for r in ROUND:
                    if r[0] == "st" and second:
                        _, n, h = r
                        c, j = SWEEP_B[n]
                        q0 = max(512 * c, P * j)
                        w = 512 * (c + 1) - q0
                        if n in (0, 4):
                            wait(pe, f1_act, ("me", c, h), s)
                        if n:
                            wait(pe, s1_act, ("ex", n - 1, h), s)
                        else:
                            wait(pe, s1_act, ("ex", NB - 1, h), s, 1)
                        ins = pe.matmul(PS[:, h, 0:w], KH[0:HD1 + 1, b, h, j * P:(j + 1) * P],
                                        QH[0:HD1 + 1, b, h, q0:q0 + w], start=True, stop=True)
                        if j >= 4 * c:
                            ins = pe.matmul(PS[:, h, 0:P], ident_b[:, :], mask_kq[:, :], start=False, stop=True,
                                            skip_group_check=True)
                        ins.then_inc(s1_pe.sem, 1)
                    elif r[0] == "pv" and second:
                        _, n, h = r
                        c, j = SWEEP_B[n]
                        q0 = max(512 * c, P * j)
                        if n == 0:
                            wait(pe, s1_dve, ("oc", 1, h), s, 1)
                        elif j == 0:
                            wait(pe, s1_dve, ("oc", 0, h), s)
                        wait(pe, s1_act, ("ex", n, h), s)
                        pe.matmul(PS[0:HD1 + 1, 2 + h, q0 - 512 * c:512], VH[:, b, h, j, :],
                                  pe_[:, h, n % 2, 0:512 * (c + 1) - q0], start=(j == 0), stop=(j == 4 * c + 3))\
                            .then_inc(s1_pe.sem, 1)
                    elif r[0] == "w" and second:
                        _, c, g = r
                        wait(pe, s1_dve, ("oc", c, 1), s)
                        if g == 2:
                            wait(pe, w1_dve, ("x", c, 2), s)
                        elif first and c == 0:
                            wait(pe, f1_dve, ("ke", 1), s + 1)
                        elif first:
                            wait(pe, f1_act, ("me", 1, g), s + 1)
                        elif c == 0:
                            wait(pe, w1_dve, ("x", 1, 7), s, 1)
                        else:
                            wait(pe, w1_dve, ("x", 0, 7), s)
                        lo = GROUPS[g][0]
                        for q in GROUPS[g]:
                            t, h = q // 2, q % 2
                            ins = pe.matmul(PS[:, W_BANK[(c, g)], (q - lo) * (D + 1):(q - lo + 1) * (D + 1)],
                                            ZT[0:HD1 + 1, h, c, t * P:(t + 1) * P],
                                            WO[0:HD1 + 1, bass.ds(hp * 2 + h, 1), :], start=True, stop=True)
                        ins.then_inc(w1_pe.sem, 1)
                    elif r in ("q", "k") and first:
                        a = ("q", "k").index(r)
                        if a == 0:
                            pe.wait_ge(w1_stage, next_hp + 1)
                            wait(pe, f1_dve, ("mx", 23), s + 1, 1)
                        else:
                            wait(pe, f1_act, ("me", 1, 1), s + 1, 1)
                            wait(pe, w1_dve, ("x", 1, 7), s, 1)
                            if not second:
                                pe.wait_ge(gl_sub[1], 1)
                        for c in range(2):
                            x0 = nb * S + c * 512
                            ins = pe.matmul(PS[:, 4 + 2 * a + c, :], wqk_s[:, a, :], XT[:, x0:x0 + 512], start=True,
                                            stop=True)
                        ins.then_inc(f1_pe.sem, 1)
                    elif r == "v" and first:
                        wait(pe, f1_act, ("qe", 1), s + 1)
                        for t in range(TB):
                            x0 = nb * S + t * P
                            ins = pe.matmul(PS[:, 4 + t // 4, (t % 4) * P:(t % 4 + 1) * P], XT[:, x0:x0 + P],
                                            W1[:, bass.ds(next_hp * P + W1_AT["wv"][0], P)], start=True, stop=True)
                        ins.then_inc(f1_pe.sem, 1)
                    elif r[0] == "a" and first:
                        p = r[1]
                        c, h, i, k = PIECES[p]
                        w = min(512, (i + 1) * P - 512 * k)
                        if p == 0:
                            wait(pe, f1_dve, ("ke", 1), s + 1)
                        if p < 2:
                            wait(pe, f1_act, ("ve", p), s + 1)
                        else:
                            wait(pe, f1_dve, ("mx", p - 2), s + 1)
                        ins = pe.matmul(PS[:, 4 + p % 2, 0:w], QH[0:HD1, nb, h, i * P:(i + 1) * P],
                                        KH[0:HD1, nb, h, 512 * k:512 * k + w], start=True, stop=True)
                        if k == c:
                            ins = pe.matmul(PS[:, 4 + p % 2, w - P:w], ident_b[:, :], mask_qk[:, :], start=False,
                                            stop=True, skip_group_check=True)
                        ins.then_inc(f1_pe.sem, 1)
                    elif r[0] == "mr" and first:
                        _, c, h = r
                        wait(pe, f1_dve, ("cb", h) if c else ("mx", 3 + 4 * h), s + 1)
                        if c:
                            wait(pe, f1_act, ("me", 0, h), s + 1)
                        elif second:
                            wait(pe, w1_dve, ("x", 0, 5 if h == 0 else 7), s)
                        for i in range(4):
                            ins = pe.transpose(PS[0:1, 7 - h, i * P:(i + 1) * P], NM[:, h, 4 * c + i:4 * c + i + 1],
                                               ident[:, :])
                        ins.then_inc(f1_pe.sem, 1)

            do_round(-1, 1, None, 0, second=False)
            with pe.Fori(0, H1 // 2 - 1) as hp:
                do_round(hp * 2, 0, hp, hp)
                do_round(hp * 2 + 1, 1, hp, hp + 1)
            do_round(ROUNDS - 2, 0, H1 // 2 - 1, H1 // 2 - 1)
            do_round(ROUNDS - 1, 1, H1 // 2 - 1, None, first=False)
            pe.wait_ge(w1_dve.sem, w1_dve.at(("x", 1, 7), ROUNDS - 1))

            with pe.Fori(0, E1 // 2) as ep:
                for m in range(NM1 + 1):
                    if m < NM1:
                        k = m // NC
                        if m % NC == 0:
                            pe.wait_ge(m1_pool.sem, ep * 2 + k + 1)
                        for u in (2 * m, 2 * m + 1):
                            half = u % 2
                            if u >= 3:
                                wait(pe, m1_dve, ("mu", u - 3), ep)
                            else:
                                wait(pe, m1_dve, ("mu", max(v for v in range(2 * NM1) if v % 3 == u)), ep, 1)
                            xs = XT[:, (m % NC) * 512:(m % NC + 1) * 512]
                            pe.matmul(PS[:, 2 * (u % 3), :], w11_s[:, k, half * P:(half + 1) * P], xs, start=True,
                                      stop=True)
                            pe.matmul(PS[:, 2 * (u % 3) + 1, :], w12_s[:, k, half * P:(half + 1) * P], xs,
                                      start=True, stop=True).then_inc(m1_pe.sem, 1)
                    if m >= 1:
                        d = m - 1
                        wait(pe, m1_dve, ("mu", 2 * d + 1), ep)
                        if d >= 2:
                            wait(pe, m1_dve, ("ac", d - 2, 3), ep)
                        else:
                            wait(pe, m1_dve, ("ac", NM1 - 2 + d, 3), ep, 1)
                        for i in range(4):
                            for half in range(2):
                                at = W1_AT["w2"][0] + (d // NC) * 2 * D + half * D
                                ins = pe.matmul(PS[:, 6 + d % 2, i * P:(i + 1) * P],
                                                HB[:, d % 2, half, i * P:(i + 1) * P],
                                                W1[:, bass.ds(ep * (4 * D) + at, D)], start=(half == 0),
                                                stop=(half == 1))
                        ins.then_inc(m1_pe.sem, 1)


def pack(parts, made):
    cols = []
    for name, n in parts:
        a = np.asarray(made[name], np.float32).reshape(P, n)
        cols.append(a)
    return np.ascontiguousarray(np.concatenate(cols, axis=1))


def blocks_of(wt):
    k, n = wt.shape
    return wt.reshape(k // P, P, n).transpose(1, 0, 2).reshape(P, -1)


def layout(i):
    g = {k: np.asarray(v) for k, v in i.items()}
    a, f = "L0_attn_", "L0_ffn_"
    rows = lambda v: np.broadcast_to(v[None, :], (P, v.shape[0]))
    w0 = {
        "wq_ttt": g[a + "W_Q"], "wk_ttt": g[a + "W_KV"][:, :D], "wv_ttt": g[a + "W_KV"][:, D:],
        "w1": g[a + "W1"], "w2": g[a + "W2"], "w2t": g[a + "W2"].T,
        "b1_rows": rows(g[a + "b1"]), "b2_rows": rows(g[a + "b2"]), "b1_col": g[a + "b1"], "b2_col": g[a + "b2"],
        "n1": g[f + "n1_w"], "n2": g[f + "n2_w"], "qn": rows(g[f + "qn_w"]), "kn": rows(g[f + "kn_w"]),
        "wqkv": np.concatenate([g[f + "wq"].T, g[f + "wk"].T, g[f + "wv"].T], axis=1), "wo": g[f + "wo"].T,
        "gate": g[f + "gate_w"].T,
    }
    for n in ("e0_up", "e0_down", "e1_w1", "e1_w2", "e1_down", "e2_l1", "e2_l2", "e2_l3", "e2_l4", "e3_down",
              "e3_up", "e3_out"):
        w0[n] = blocks_of(g[f + n].T)
    heads = lambda w: w.transpose(2, 0, 1).reshape(D, H1 * HD1)
    w1 = {
        "wq": heads(g["L1_attn_W_Q"]), "wk": heads(g["L1_attn_W_K"]), "wv": heads(g["L1_attn_W_V"]),
        "wo": blocks_of(g["L1_attn_W_O"].T), "gate": g["L1_ffn_Wg"],
        "w11": g["L1_ffn_W11"].transpose(1, 0, 2), "w12": g["L1_ffn_W12"].transpose(1, 0, 2),
        "w2": g["L1_ffn_W2"].reshape(E1, 2, P, D).transpose(2, 0, 1, 3),
    }
    return g["L0_attn_x"].reshape(B * S, D), pack(W0_PARTS, w0), pack(W1_PARTS, w1)


def kernel(**inputs):
    from concourse import bacc
    from concourse.bass_utils import run_bass_kernel_spmd

    x, w0, w1 = layout(inputs)
    nc = bacc.Bacc("TRN2", target_bir_lowering=False, num_devices=1)
    args = [nc.dram_tensor(n, a.shape, F32, kind="ExternalInput").ap()
            for n, a in (("x", x), ("w0", w0), ("w1", w1))]
    out = nc.dram_tensor("out", (B * S, D), F32, kind="ExternalOutput").ap()
    program(nc, *args, out)
    r = run_bass_kernel_spmd(nc, [{"x": x, "w0": w0, "w1": w1}], core_ids=[0])
    return r.results[0]["out"].reshape(B, S, D)
```

```python
from contextlib import ExitStack

import numpy as np

import concourse.bass as bass
from concourse import mybir

F32 = mybir.dt.float32
F32R = mybir.dt.float32r
BF16 = mybir.dt.bfloat16
I32 = mybir.dt.int32
ALU = mybir.AluOpType
ACT = mybir.ActivationFunctionType
AX = mybir.AxisListType

P = 128
B, S, D = 2, 1024, 128
NT = B * S // P
TB = S // P
NC = B * S // 512
LN_EPS = 1e-5
RMS_EPS = 1.1920929e-07
MASKED = -1e30

LR = 1e-3
CS = 64
CHUNKS = S // CS
SWEEPS = 5
CONVERGED = 2.0 ** -11

H0, HD0 = 16, 8
HG = 4
QM = 24
M_ZERO = 32

H1, HD1 = 16, 64
E0, E1, HID = 4, 8, 256

W0_PARTS = [("wq_ttt", 128), ("wk_ttt", 128), ("wv_ttt", 128), ("w1", 128), ("w2", 128), ("w2t", 128),
            ("b1_rows", 128), ("b2_rows", 128), ("b1_col", 1), ("b2_col", 1), ("n1", 1), ("n2", 1),
            ("qn", 8), ("kn", 8), ("wqkv", 384), ("wo", 128), ("gate", 4),
            ("e0_up", 256), ("e0_down", 256), ("e1_w1", 256), ("e1_w2", 256), ("e1_down", 256),
            ("e2_l1", 256), ("e2_l2", 512), ("e2_l3", 512), ("e2_l4", 256),
            ("e3_down", 128), ("e3_up", 256), ("e3_out", 256)]
W1_PARTS = [("wq", H1 * HD1), ("wk", H1 * HD1), ("wv", H1 * HD1), ("wo", H1 * HD1), ("gate", E1),
            ("w11", E1 * HID), ("w12", E1 * HID), ("w2", E1 * HID)]


def offsets(parts):
    at, out = 0, {}
    for name, n in parts:
        out[name] = (at, at + n)
        at += n
    return out, at


W0_AT, W0_N = offsets(W0_PARTS)
W1_AT, W1_N = offsets(W1_PARTS)


class Steps:

    def __init__(self, sem, names):
        self.sem, self.names = sem, list(names)
        self.per_trip = len(self.names)
        self.index = {n: i + 1 for i, n in enumerate(self.names)}

    def at(self, name, trip, back=0):
        return trip * self.per_trip + (self.index[name] + self.per_trip * (1 - back))


def program(nc, x_in, w0_in, w1_in, out):
    with ExitStack() as ctx:
        def sb(name, shape, dt=F32):
            return ctx.enter_context(nc.sbuf_tensor(name, shape, dt))

        def sem(name):
            return ctx.enter_context(nc.semaphore(name))

        PS = ctx.enter_context(nc.psum_tensor("PS", [P, 8, 512], F32))
        X = sb("X", [P, NT, D])
        XT = sb("XT", [P, B * S + CS])
        ident = sb("ident", [P, P])
        ident_b = sb("ident_b", [P, P], BF16)
        mask_qk = sb("mask_qk", [P, P], BF16)
        mask_kq = sb("mask_kq", [P, P], BF16)
        lr_mask = sb("lr_mask", [P, P])
        lr_mask_h = sb("lr_mask_h", [P, P])
        ones = sb("ones", [P, P])
        zero = sb("zero", [P, HG])
        eps = sb("eps", [P, 2])
        stats = sb("stats", [P, NT, 6])
        mv = sb("mv", [P, NT, 2])
        sd = sb("sd", [P, NT])
        rstd = sb("rstd", [P, NT])
        ssq = sb("ssq", [P, NT])
        rms_sd = sb("rms_sd", [P, NT])
        rms_r = sb("rms_r", [P, NT])

        xc = sb("xc", [P, 2, CS])
        kvs = sb("kvs", [P, 2, 4, P])
        kv = kvs[:, 0, :, :]
        vb = sb("vb", [P, 2, P])
        g1 = sb("g1", [P, P])
        g2 = sb("g2", [P, P])
        g3 = sb("g3", [P, P])
        zb = sb("zb", [P, 2, P])
        zh = sb("zh", [P, 2, P])
        th = sb("th", [P, 2, P])
        sl = sb("sl", [P, 2, P])
        du = sb("du", [P, P])
        dd = sb("dd", [P, P])
        grc = sb("grc", [P, 8, P])
        gr = grc[:, 0:6, :].rearrange("p (m a) n -> p m a n", m=2)
        STN = 3 * P + 2 * P + 2
        st = sb("st", [P, STN])
        st0 = sb("st0", [P, STN])
        cmax = sb("cmax", [P, 4])
        cin = sb("cin", [P, 2])
        cok = sb("cok", [P, 2])
        okay = sb("okay", [P, 2])
        flag_f = sb("flag_f", [1, 1])
        flag_i = sb("flag_i", [1, 1], I32)
        ST_W1, ST_W2, ST_W2T = st[:, 0:P], st[:, P:2 * P], st[:, 2 * P:3 * P]
        ST_B1, ST_B2 = st[:, 3 * P:4 * P], st[:, 4 * P:5 * P]
        ST_B1C, ST_B2C = st[:, 5 * P:5 * P + 1], st[:, 5 * P + 1:5 * P + 2]

        pe_ = sb("pe_", [P, 4, 2, 512])
        HI = pe_[:, :, :, :].rearrange("p h m n -> p (h m n)").rearrange("p (t n) -> p t n", t=NT)
        ZT = pe_[:, 2:4, :, :]
        QZ, SZ = (pe_[:, 2 * a:2 * a + 2, :, :].rearrange("p h m n -> p (h m) n") for a in range(2))
        ots = sb("ots", [P, 2, 512])
        NMH0 = sb("NMH0", [P, HG, 4, 2])
        rz = sb("rz", [P, 2, 16])
        hss, hsd = ots[:, 0, :], ots[:, 1, :]
        wqkv_n = sb("wqkv_n", [P, 3 * D])

        lg = sb("lg", [P, NT, 8])
        lgm = sb("lgm", [P, NT, 8], I32)
        lgx = sb("lgx", [P, NT])
        ge = sb("ge", [P, NT, 8])
        gp = sb("gp", [P, NT, 8])
        gc = ots[:, :, :].rearrange("p a n -> p (a n)").rearrange("p (f n) -> p f n", f=8)
        rank = sb("rank", [P, NT, 8])
        wt0 = sb("wt0", [P, E0, NT])
        wt1 = sb("wt1", [P, E1, NT])
        wsum = sb("wsum", [P, NT])

        with nc.sbuf_tensor("qta", [P, HG, S], F32R) as qta, nc.sbuf_tensor("qtb", [P, HG, S], F32R) as qtb:
            pass
        W1 = sb("W1", [P, W1_N])
        assert W1_N >= 2 * HG * S

        with ExitStack() as early:
            def sb0(name, shape, dt=F32):
                return early.enter_context(nc.sbuf_tensor(name, shape, dt))

            XN = sb0("XN", [P, NT, D])
            W0 = sb0("W0", [P, W0_N])
            kta = sb0("kta", [P, S], F32R)
            arena = sb0("arena", [P, 15360])
        taken = [0]

        def area(n):
            taken[0] += n
            assert taken[0] <= 15360, taken
            return arena[:, taken[0] - n:taken[0]]

        QKV = area(NT * 3 * D).rearrange("p (t n) -> p t n", t=NT)
        LO = area(NT * 2 * D).rearrange("p (t n) -> p t n", t=NT)
        tmq = area(TB * P).rearrange("p (t n) -> p t n", t=TB)
        tmk = area(TB * P).rearrange("p (t n) -> p t n", t=TB)
        tmv = area(TB * P).rearrange("p (t n) -> p t n", t=TB)
        Z0 = area(NT * D).rearrange("p (t n) -> p t n", t=NT)
        taken[0] = 0
        Z0T = area(B * S)
        taken[0] = 0
        hid = area(15 * 512).rearrange("p (u n) -> p u n", u=15)
        e1t = area(2 * 512).rearrange("p (u n) -> p u n", u=2)
        def head_parts(name, heads=B * 2):
            return sb(name, [P, heads * S], F32R).rearrange("p (b h n) -> p b h n", b=B, h=2)

        QA, KA, QB, KB = (head_parts(n) for n in ("QA", "KA", "QB", "KB"))
        WO = sb("WO", [P, H1, D + 1])
        VH = sb("VH", [P, B, 2, TB, HD1 + 1])
        wqk_s = sb("wqk_s", [P, 2, P])
        NM = sb("NM", [P, 2, TB])
        NMH = sb("NMH", [P, 2, TB // 2, 2])
        NM2 = sb("NM2", [P, 2, TB, 2])
        RS = sb("RS", [P, 2, 8])
        w11_s, w12_s = (sb(n, [P, 2, 2, HID], F32R) for n in ("w11_s", "w12_s"))
        XH, XL = (m[:, 0:1, :, :].rearrange("p b h n -> p (b h n)") for m in (QA, KA))
        pe_flat = pe_[:, :, :, :].rearrange("p h m n -> p (h m n)")
        GS = pe_flat[:, 0:3 * 512].rearrange("p (u n) -> p u n", u=3)
        HB = pe_flat[:, 3 * 512:7 * 512].rearrange("p (m u n) -> p m u n", m=2, u=2)

        def w0(name, lo=0, hi=None):
            a, b = W0_AT[name]
            return W0[:, a + lo:(b if hi is None else a + hi)]

        def w1(name, lo=0, hi=None):
            a, b = W1_AT[name]
            return W1[:, a + lo:(b if hi is None else a + hi)]

        x_loaded, w0_loaded, w1_loaded = sem("x_loaded"), sem("w0_loaded"), sem("w1_loaded")
        const_ready = sem("const_ready")
        stored = sem("stored")
        dve_chain, pool_chain = sem("dve_chain"), sem("pool_chain")
        N_CONST = 1


        class Ttt:
            def __init__(self, tag, sweeps):
                self.trips, self.sweeps = sweeps // 2, sweeps
                self.staged = sem(f"ttt_{tag}_chunk_staged")
                self.mm = sem(f"ttt_{tag}_products")
                self.ew = sem(f"ttt_{tag}_elementwise")
                self.th = sem(f"ttt_{tag}_tanh")
                self.pe0, self.pes, self.pe1 = ["kv", "base"], ["zc", "ys", "yc", "ds", "dc"], ["up"]
                self.dv0 = ["vbt", "vb", "g1", "zbt", "zb", "zero"]
                self.dvs = ["z", "s", "g2", "u", "d", "dy", "g3", "dz"]
                self.dv1 = ["w", "b1", "b2", "b1c", "b2c"]
                self.tm = len(self.pe0) + sweeps * len(self.pes) + len(self.pe1)
                self.td = len(self.dv0) + sweeps * len(self.dvs) + len(self.dv1)
                self.ta = 1 + sweeps

            def pe(self, chunk, name, sweep=None):
                if name in self.pe0:
                    return chunk * self.tm + (2 + self.pe0.index(name))
                if name in self.pes:
                    return chunk * self.tm + sweep * len(self.pes) + (2 + len(self.pe0) + self.pes.index(name))
                return (chunk + 1) * self.tm + 1

            def dv(self, chunk, name, sweep=None):
                if name in self.dv0:
                    return chunk * self.td + (2 + self.dv0.index(name))
                if name in self.dvs:
                    return chunk * self.td + sweep * len(self.dvs) + (2 + len(self.dv0) + self.dvs.index(name))
                return chunk * self.td + (2 + len(self.dv0) + self.sweeps * len(self.dvs) + self.dv1.index(name))

            def dv_before(self, chunk, sweep):
                return chunk * self.td + sweep * len(self.dvs) + (1 + len(self.dv0))

            def ac(self, chunk, sweep=None):
                return chunk * self.ta + (2 if sweep is None else sweep + 3)

        ttt_full = Ttt("full", CS)
        ttt_okay, ttt_sum, ttt_flag, ttt_reset, ttt_settled = (
            sem("ttt_okay"), sem("ttt_okay_summed"), sem("ttt_flag_ready"), sem("ttt_state_reset"),
            sem("ttt_settled"))

        SWEEP_B = [(c, j) for c in range(2) for j in range(4 * c + 4)]
        NB = len(SWEEP_B)
        LAST = [3, NB - 1]
        TRIPS = B * H0 // HG
        assert CHUNKS == 2 * TRIPS
        PIECES0 = [(c, h, i, k) for c in range(2) for h in range(HG) for i in range(4 * c, 4 * c + 4)
                   for k in range(c + 1)]
        NP0 = len(PIECES0)
        P0_HALF = NP0 // 3
        TURN_BANK = {("tk", 0): 6, ("tq", 0): 7, ("tk", 1): 6, ("tq", 1): 7, ("tq2", 0): 7, ("tq2", 1): 7,
                     ("to", 0): 7, ("to", 1): 7}

        def turned(kind, half):
            return [(kind, half)] + [("copy", kind, half, h) for h in range(HG)]

        attn = [("tk", 0)] + turned("tq", 0) + [("tk", 1)]
        for p in range(NP0):
            attn.append(("a", p))
            if p == 3:
                attn += turned("tq", 1)
            if p == P0_HALF + 4:
                attn += turned("tq2", 0)
        for n in range(NB + 1):
            if n < NB:
                attn += [("st", n, h) for h in range(HG)]
            if n >= 1:
                attn += [("pv", n - 1)]
            if n == 0:
                attn += turned("tq2", 1)
            if n == 7:
                attn += [("to", 0)]
        attn += [("to", 1)]

        def share(item):
            if item[0] == "a":
                c, h, i, k = PIECES0[item[1]]
                return (min(4, i + 1 - 4 * k) + 1) * 1.2
            if item[0] in ("st", "pv"):
                c, j = SWEEP_B[item[1]]
                return (4 * (c + 1) - max(4 * c, j)) * (1 if item[0] == "st" else 1.5) + 1
            return 2 if item[0] == "copy" else 5

        train = []
        for q in range(2):
            train += [((q, "base"), 0.0)]
            for k in range(SWEEPS):
                train += [((q, "zc", k), 0.8 if k + 1 == SWEEPS else 2.6)]
                train += [((q, "kvn"), 0.0)] if k + 1 == SWEEPS else []
                train += [((q, "y", k), 0.8), ((q, "ds", k), 0.5), ((q, "dc", k), 0.9)]
            train += [((q, "up"), 0.0)]
        room, total = sum(r for _, r in train), sum(share(a) for a in attn)
        TRIP, used, due = [], 0, 0.0
        rest = list(attn[:-1])
        for step, r in train:
            TRIP.append(("t",) + step)
            due += r * total / room
            while rest and r and used + share(rest[0]) / 2 < due:
                used += share(rest[0])
                TRIP.append(rest.pop(0))
        TRIP += rest + attn[-1:]

        a0_pe = Steps(sem("a0_products"), [r for r in attn if r[0] != "copy"])
        a0_act = Steps(sem("a0_scalar"), [{"copy": ("qa" if r[1] == "tq" else "qb",) + r[2:],
                                           "st": ("ex",) + r[1:]}[r[0]] for r in attn if r[0] in ("copy", "st")])
        vec = []
        for r in attn:
            if r[0] == "tk":
                vec.append(("ka", r[1]))
            elif r[0] == "a":
                vec.append(("mx", r[1]))
                c, h, i, k = PIECES0[r[1]]
                if (c, i, k) == (1, TB - 1, 1):
                    vec.append(("cb", h))
            elif r[0] == "pv" and r[1] in LAST:
                vec.append(("oc", LAST.index(r[1])))
            elif r[0] == "to":
                vec += [("rc", r[1]), ("zt", r[1])]
        a0_dve = Steps(sem("a0_vector"), vec)
        a0_pool = Steps(sem("a0_staged"), ["k", "q", "v"])
        UPDATE = ["w1", "b1", "b1c", "w2", "b2", "b2c"]
        tpe, tact, tdve = [], [], []
        for q in range(2):
            tpe += [(q, "base")]
            tdve += [(q, n) for n in ("zbt", "zb", "vbt", "vb")]
            for k in range(SWEEPS):
                last = k + 1 == SWEEPS
                tpe += ([(q, "zc", k)] if k else []) + ([(q, "kvn")] if last else [])
                tpe += [(q, n, k) for n in ("yt", "ym", "ds", "dc")] + [(q, "kk") if last else (q, "ss", k)]
                tact += [(q, "th", k)] + ([(q, "kvn")] if last else [])
                tdve += ([(q, "z", k)] if k else []) + [(q, n, k) for n in ("st", "sm")]
                tdve += [] if k else [(q, "cd"), (q, "cm")]
                tdve += [(q, n, k) for n in ("dyt", "u", "dym", "d", "g3", "dz")] + [(q, "g1") if last else (q, "g2", k)]
                tdve += [] if k else [(q, "cc"), (q, "co")]
            tpe += [(q, "up1"), (q, "up2")]
            tdve += [(q, n) for n in UPDATE]
        t_pe, t_act, t_dve = Steps(sem("ttt_products"), tpe), Steps(sem("ttt_scalar"), tact), \
            Steps(sem("ttt_vector"), tdve)
        t_pool = Steps(sem("ttt_chunk_staged"), [(0, "xc"), (1, "xc")])

        units = []

        def unit(name, blocks, rhs, then, dst):
            units.append((name, blocks, rhs, then, dst))

        HU = {}

        def slot(name):
            HU.setdefault(name, len(HU))
            return HU[name]

        def layer(tag, wname, k_blocks, m_blocks, src, then):
            for m in range(m_blocks):
                blocks = [w0(wname, kb * 128 * m_blocks + m * 128, kb * 128 * m_blocks + m * 128 + 128)
                          for kb in range(k_blocks)]
                rhs = [None] * k_blocks if src is None else [slot((src, kb)) for kb in range(k_blocks)]
                unit((tag, m), blocks, rhs, then, slot((tag, m)) if then != "none" else None)

        layer("e0h", "e0_up", 1, 2, None, "gelu")
        layer("e1g", "e1_w1", 1, 2, None, "silu")
        layer("e1v", "e1_w2", 1, 2, None, "times")
        layer("e2a", "e2_l1", 1, 2, None, "gelu")
        layer("e3a", "e3_down", 1, 1, None, "gelu")
        layer("e2b", "e2_l2", 2, 2, "e2a", "gelu")
        layer("e3b", "e3_up", 1, 2, "e3a", "gelu")
        layer("e2c", "e2_l3", 2, 2, "e2b", "gelu")
        assert len(units) == 15 and len(HU) == 15
        seq0 = []
        for u, spec in enumerate(units):
            seq0.append(("u", u))
            if spec[0] == ("e2b", 1):
                seq0.append(("dn", 0))
            if spec[0] == ("e3b", 1):
                seq0.append(("dn", 1))
        seq0 += [("dn", 3), ("dn", 2)]
        DOWN = {0: ("e0_down", "e0h"), 1: ("e1_down", "e1v"), 2: ("e2_l4", "e2c"), 3: ("e3_out", "e3b")}
        dn_order = [s[1] for s in seq0 if s[0] == "dn"]
        m0_pe = Steps(sem("m0_products"), seq0)
        m0_act = Steps(sem("m0_scalar"), [("u", u) for u, s in enumerate(units) if s[3] in ("gelu", "silu")])
        dve0 = []
        for kind, u in seq0:
            if kind == "u" and units[u][3] == "silu":
                dve0.append(("sg", u))
            elif kind == "u" and units[u][3] == "times":
                dve0.append(("tm", u))
            elif kind == "dn":
                dve0 += [("ac", u, i) for i in range(4)]
        m0_dve = Steps(sem("m0_vector"), dve0)

        def unit_freed(u):
            then = units[u][3]
            return (m0_act, ("u", u)) if then == "gelu" else (m0_dve, ("sg", u) if then == "silu" else ("tm", u))

        ROUNDS = B * H1 // 2
        PIECES = [(c, h, i, k) for c in range(2) for h in range(2) for i in range(4 * c, 4 * c + 4)
                  for k in range(c + 1)]
        GROUPS = [range(0, 3), range(3, 6), range(6, 8)]
        between = {0: ["q", "qh"], 1: ["k", "kh"], 2: ["qb", "kd", "v"], 3: [],
                   4: [("a", p) for p in range(0, 3)], 5: [("a", p) for p in range(3, 6)],
                   6: [("a", p) for p in range(6, 9)], 7: [("a", 9), ("a", 10), ("mr", 0, 0), ("a", 11)],
                   8: [("a", 12), ("a", 13), ("mr", 0, 1), ("a", 14)], 9: [("a", 15), ("a", 16), ("w", 0, 0), ("a", 17)],
                   10: [("a", 18), ("a", 19), ("w", 0, 1)], 11: [("a", 20), ("a", 21), ("w", 0, 2)],
                   12: [("a", 22), ("a", 23), ("w", 1, 0), ("w", 1, 1), ("mr", 1, 0), ("mr", 1, 1), ("w", 1, 2)]}
        MR_BANK = {(0, 0): 7, (0, 1): 6, (1, 0): 4, (1, 1): 5}
        ROUND = []
        for n in range(NB + 1):
            rest = list(between[n])
            for h in range(2):
                if n < NB:
                    ROUND.append(("st", n, h))
            for h in range(2):
                if n:
                    ROUND.append(("pv", n - 1, h))
                    if rest:
                        ROUND.append(rest.pop(0))
            ROUND += rest

        def kind_of(r):
            return r if isinstance(r, str) else r[0]

        FIRST = [r for r in ROUND if kind_of(r) in ("q", "k", "v", "a", "mr")]
        SECOND = [r for r in ROUND if r[0] in ("st", "pv", "w")]

        def made(kinds, react):
            return [x for r in ROUND if kind_of(r) in kinds for x in react(r)]

        f1_pe = Steps(sem("f1_products"), FIRST)
        s1_pe = Steps(sem("s1_products"), [r for r in SECOND if r[0] != "w"])
        w1_pe = Steps(sem("w1_products"), [r for r in SECOND if r[0] == "w"])
        f1_act = Steps(sem("f1_scalar"), made(("qh", "kh", "qb", "v", "mr"), lambda r:
                                              [("me",) + r[1:]] if r[0] == "mr" else [(r, 0), (r, 1)]))
        s1_act = Steps(sem("s1_scalar"), made(("st", "pv"), lambda r: [("ex",) + r[1:]] if r[0] == "st" else
                                              [("oc", LAST.index(r[1]), r[2])] if r[1] in LAST else []))
        f1_dve = Steps(sem("f1_vector"), made(
            ("qh", "kh", "kd", "a"), lambda r: [({"qh": "ql", "kh": "kl"}.get(r, r), h) for h in range(2)] if r[0] != "a"
            else [("mx", r[1])] + {3: [("nh", 0, 0), ("nl", 0, 0)], 7: [("nh", 0, 1), ("nl", 0, 1)],
                                   15: [("cb", 0), ("nh", 1, 0), ("nl", 1, 0)],
                                   23: [("cb", 1), ("nh", 1, 1), ("nl", 1, 1)]}.get(r[1], [])))
        w1_dve = Steps(sem("w1_vector"), made(("w",), lambda r: [("rs",) + r[1:]]
                                              + [("x", r[1], q) for q in GROUPS[r[2]]]))
        w1_stage = sem("wqk_staged")
        W_BANK = {(0, 0): 7, (0, 1): 6, (0, 2): 7, (1, 0): 7, (1, 1): 6, (1, 2): 3}

        NM1 = 2 * NC
        m1pe, m1dve = [], []
        for m in range(NM1 + 1):
            if m < NM1:
                m1pe += [("u", 2 * m), ("u", 2 * m + 1)]
                m1dve += [("mu", 2 * m), ("mu", 2 * m + 1)]
            if m >= 1:
                m1pe += [("dn", m - 1)]
                m1dve += [("ac", m - 1, i) for i in range(4)]
        m1_pe = Steps(sem("m1_products"), m1pe)
        m1_act = Steps(sem("m1_silu"), [("u", u) for u in range(2 * NM1)])
        m1_dve = Steps(sem("m1_vector"), m1dve)
        m1_low = Steps(sem("m1_weights_low"), ["w0", "w1"])
        m1_tok_high, m1_tok_low = sem("m1_tokens_high"), sem("m1_tokens_low")
        m1_pool = Steps(sem("m1_staged"), ["w0", "w1"])

        def two(name):
            return sem(name + "_0"), sem(name + "_1")

        ln_var, ln_sd, ln_done, xt_ps, xt_done = (two("ln_var"), two("ln_sd"), two("ln_tile"), two("xt_turned"),
                                                  two("xt_copied"))
        rms_ss, rms_sq = two("rms_sum"), two("rms_root")
        qkv_w, qkv_ps, qkv_done, hsq, hsum, hroot, hnorm, hhi, hlo = (
            sem("qkv_weights"), sem("qkv_products"), sem("qkv_copied"), sem("head_squares"), sem("head_sums"),
            sem("head_roots"), sem("head_normed"), sem("head_high"), sem("head_low"))
        tq_q, tq_z, tq_y, tq_qc, tq_s, tq_acc = (
            sem("ttt_q_product"), sem("ttt_hidden_product"), sem("ttt_out_product"), sem("ttt_q_copied"),
            sem("ttt_out_silu"), sem("ttt_out_added"))
        z0_ps, z0_cp, ao_ps, ao_add, xf_tile, xf_ps, xf_cp = (
            sem("z0_turned"), sem("z0_copied"), sem("ao_products"), sem("ao_added"), sem("xf_tile"),
            sem("xf_turned"), sem("xf_copied"))
        gl_ps, gl_sub, gl_exp, gl_done = two("gate_logits"), two("gate_shifted"), two("gate_exp"), two("gate_done")
        a0_zero, a1_ones = sem("a0_stacks_cleared"), sem("a1_ones_set")
        x_plus = sem("residual_added")
        wo_loaded = sem("wo_loaded")
        first_xc, first_kv, first_copy, first_kk = (sem("ttt_first_chunk_staged"), sem("ttt_first_kv"),
                                                    sem("ttt_first_kv_copied"), sem("ttt_first_gram"))

        def parity(sweep):
            return (sweep + SWEEPS) % 2

        def chunk_before(q):
            return (0, 0) if q else (1, 1)

        def wait(e, steps, name, trip, back=0):
            e.wait_ge(steps.sem, steps.at(name, trip, back))

        def tiles(ap, t, n=1):
            return ap[:, bass.ds(t, n), :]

        block = ctx.enter_context(nc.Block())

        @block.sync
        def _(sp):
            xs = x_in.rearrange("(t p) d -> p t d", p=P)
            sp.dma_start(X[:, 0:TB, :], xs[:, 0:TB, :]).then_inc(x_loaded, 16)
            sp.dma_start(X[:, TB:NT, :], xs[:, TB:NT, :]).then_inc(x_loaded, 16)
            sp.dma_start(W0[:, :], w0_in).then_inc(w0_loaded, 16)
            sp.wait_ge(a0_dve.sem, a0_dve.at(("zt", 1), TRIPS - 1))
            sp.wait_ge(a0_pe.sem, a0_pe.at(("to", 1), TRIPS - 1))
            sp.dma_start(W1[:, :], w1_in).then_inc(w1_loaded, 16)
            sp.wait_ge(m0_pe.sem, m0_pe.at(seq0[-1], NC - 1))
            sp.wait_ge(xt_ps[1], NC)
            wo_pairs = WO[0:HD1, :, :].rearrange("p (m h) n -> p h m n", h=2)
            lo, hi = W1_AT["wo"]
            for h in range(2):
                sp.dma_start(wo_pairs[:, h, :, 0:D],
                             w1_in[h * HD1:(h + 1) * HD1, lo:hi].rearrange("p (m n) -> p m n", n=D))\
                    .then_inc(wo_loaded, 16)
            sp.wait_ge(m1_dve.sem, m1_dve.at(("ac", NM1 - 1, 3), E1 // 2 - 1))
            sp.dma_start(out.rearrange("(t p) d -> p t d", p=P), X[:, :, :]).then_inc(stored, 16)
            sp.wait_ge(stored, 16)

        @block.gpsimd
        def _(pool):
            count = [0]

            def link(ins):
                count[0] += 1
                ins.then_inc(pool_chain, 1)
                pool.wait_ge(pool_chain, count[0])

            pool.sem_inc(t_pool.sem, t_pool.per_trip)
            for m in (ident, ident_b):
                link(pool.memset(m[:, :], 0.0))
                link(pool.affine_select(out=m[:, :], in_=m[:, :], compare_op=ALU.not_equal, fill=1.0, base=0,
                                        pattern=[[-1, P]], channel_multiplier=1))
            for m, sign in ((mask_qk, 1), (mask_kq, -1)):
                link(pool.memset(m[:, :], 0.0))
                link(pool.affine_select(out=m[:, :], in_=m[:, :], compare_op=ALU.is_ge, fill=MASKED, base=0,
                                        pattern=[[-sign, P]], channel_multiplier=sign))
            for m, v in ((lr_mask, -LR), (lr_mask_h, -LR / 2)):
                link(pool.memset(m[:, :], v))
                for half in range(2):
                    rows = m[half * CS:(half + 1) * CS, :].rearrange("p (b s) -> p b s", b=2)
                    link(pool.affine_select(out=rows, in_=rows, compare_op=ALU.is_ge, fill=0.0, base=-1,
                                            pattern=[[0, 2], [1, CS]], channel_multiplier=-1))
            link(pool.memset(ones[:, :], 1.0))
            link(pool.memset(zero[:, :], 0.0))
            link(pool.memset(eps[:, 0:1], LN_EPS))
            link(pool.memset(eps[:, 1:2], RMS_EPS))
            link(pool.memset(okay[:, :], 1.0))
            for tm, at in ((tmk, QM), (tmv, HD0)):
                link(pool.memset(tm, 0.0))
                link(pool.memset(tm.rearrange("p t (h n) -> p t h n", h=HG)[:, :, :, at:at + 1], 1.0))
            pool.memset(tmq, 0.0).then_inc(const_ready, 1)
            pool.wait_ge(const_ready, N_CONST)
            for stack in (qta, qtb):
                ins = pool.tensor_copy(stack[:, :, :], zero[:, :].unsqueeze(2).broadcast_to([P, HG, S]))
            ins.then_inc(a0_zero, 1)

            def ttt(run):
                with pool.Fori(0, CHUNKS) as c:
                    pool.wait_ge(run.mm, c * run.tm + 1)
                    src = XT[:, 0:B * S].rearrange("p (b s) -> p b s", b=B)[:, :, bass.ts(c, CS)]
                    pool.tensor_copy(xc[:, :, :], src).then_inc(run.staged, 1)

            pool.wait_ge(xt_done[0], NC)
            link(pool.memset(XT[:, B * S:B * S + CS], 0.0))
            first = XT[:, 0:B * S].rearrange("p (b s) -> p b s", b=B)[:, :, 0:CS]
            pool.tensor_copy(xc[:, :, :], first).then_inc(first_xc, 1)
            pool.wait_ge(first_kv, 1)
            pool.wait_ge(hlo, 1)
            with pool.Fori(0, B) as b:
                with pool.Fori(0, H0 // HG) as g:
                    trip = b * (H0 // HG) + g

                    def tokens(q):
                        p, back = chunk_before(q)
                        wait(pool, t_pe, (p, "kvn"), trip, back)
                        at = trip * (2 * CS) + (q + 1) * CS
                        for e in range(B):
                            ins = pool.tensor_copy(xc[:, e, :], XT[:, bass.ds(at + e * S, CS)])
                        ins.then_inc(t_pool.sem, 1)

                    def heads(ap, off):
                        v = ap[:, bass.ts(b, TB), bass.ds(g * (HG * HD0) + off, HG * HD0)]
                        return v.rearrange("p t (h e) -> p t h e", h=HG)

                    def put(tm, at):
                        return tm.rearrange("p t (h n) -> p t h n", h=HG)[:, :, :, at:at + HD0]

                    tokens(0)
                    wait(pool, a0_pe, ("tk", 1), trip, 1)
                    pool.tensor_copy(put(tmk, 0), heads(QKV, D))
                    pool.tensor_copy(put(tmk, HD0), heads(LO, D))
                    pool.tensor_copy(put(tmk, 2 * HD0), heads(QKV, D)).then_inc(a0_pool.sem, 1)
                    wait(pool, a0_pe, ("tq2", 1), trip, 1)
                    pool.tensor_copy(put(tmq, 0), heads(QKV, 0))
                    pool.tensor_copy(put(tmq, HD0), heads(QKV, 0))
                    pool.tensor_copy(put(tmq, 2 * HD0), heads(LO, 0))
                    pool.memset(tmq.rearrange("p t (h n) -> p t h n", h=HG)[:, :, :, QM:QM + 1], 0.0)\
                        .then_inc(a0_pool.sem, 1)
                    wait(pool, a0_pe, ("pv", NB - 1), trip, 1)
                    pool.tensor_copy(put(tmv, 0), heads(QKV, 2 * D)).then_inc(a0_pool.sem, 1)
                    tokens(1)

            pool.wait_ge(ttt_flag, 1)
            settled = pool.value_load(flag_i[0:1, 0:1], min_val=0, max_val=1)
            with pool.If(settled == 0):
                ttt(ttt_full)
            with pool.Else():
                pool.nop()

            pool.wait_ge(m0_pe.sem, m0_pe.at(seq0[-1], NC - 1))
            pool.wait_ge(m0_dve.sem, m0_dve.at(dve0[-1], NC - 1))
            pool.wait_ge(xt_ps[1], NC)

            def stage_pair(hp):
                for a, name in enumerate(("wq", "wk")):
                    at = W1_AT[name][0]
                    ins = pool.tensor_copy(wqk_s[:, a, :], W1[:, bass.ds(hp * P + at, P)])
                ins.then_inc(w1_stage, 1)

            pool.wait_ge(w1_loaded, 16)
            stage_pair(0)
            link(pool.memset(VH[:, :, :, :, HD1:HD1 + 1], 1.0))
            link(pool.memset(WO[:, :, D:D + 1], 0.0))
            link(pool.memset(WO[HD1:HD1 + 1, :, :], 0.0))
            link(pool.memset(WO[HD1:HD1 + 1, :, D:D + 1], 1.0))
            rows = KB[HD1:HD1 + 2].rearrange("p b h (t n) -> p (b h t) n", n=P)
            pool.tensor_copy(rows, ones[HD1:HD1 + 2, :].unsqueeze(1).broadcast_to([2, 4 * TB, P])).then_inc(a1_ones, 1)
            with pool.Fori(1, H1 // 2) as hp:
                wait(pool, f1_pe, "k", hp * 2 + 1, 2)
                stage_pair(hp)
            with pool.Fori(0, E1 // 2 + 1) as ep:
                for k in range(2):
                    wait(pool, m1_pe, ("u", NM1 * (k + 1) - 1), ep, 1)
                    for dst, name in ((w11_s, "w11"), (w12_s, "w12")):
                        at = W1_AT[name][0] + k * HID
                        ins = pool.tensor_copy(dst[:, k, 0, :], W1[:, bass.ds(ep * (2 * HID) + at, HID)])
                    ins.then_inc(m1_pool.sem, 1)

        @block.scalar
        def _(act):
            act.sem_inc(a0_act.sem, a0_act.per_trip)
            act.sem_inc(m0_act.sem, m0_act.per_trip)
            act.sem_inc(f1_act.sem, f1_act.per_trip)
            act.sem_inc(s1_act.sem, s1_act.per_trip)
            act.sem_inc(m1_act.sem, m1_act.per_trip)
            act.sem_inc(t_act.sem, t_act.per_trip)
            act.sem_inc(ttt_full.th, 1)
            act.wait_ge(const_ready, N_CONST)

            def norm(layer):
                act.wait_ge(ln_var[layer], NT)
                act.activation(sd[:, :], mv[:, :, 1], ACT.Sqrt, bias=eps[:, 0:1]).then_inc(ln_sd[layer], 1)
                for c in range(NC):
                    act.wait_ge(xt_ps[layer], c + 1)
                    act.copy(XT[:, c * 512:(c + 1) * 512], PS[:, c, :]).then_inc(xt_done[layer], 1)

            norm(0)
            act.wait_ge(rms_ss[0], NT)
            act.activation(rms_sd[:, :], ssq[:, :], ACT.Sqrt, bias=eps[:, 1:2], scale=1.0 / D)\
                .then_inc(rms_sq[0], 1)
            act.wait_ge(ln_done[0], NT + 1)
            for t in range(NT):
                act.wait_ge(qkv_ps, t + 1)
                act.activation(QKV[:, t, :], PS[:, 4 + t % 4, 0:3 * D], ACT.Copy, scale=rms_r[:, t:t + 1])\
                    .then_inc(qkv_done, 1)
            act.wait_ge(qkv_done, NT)
            act.activation(LO, QKV[:, :, 0:2 * D], ACT.Square).then_inc(hsq, 1)
            act.wait_ge(hsum, 1)
            act.activation(hsd, hss, ACT.Sqrt, bias=eps[:, 1:2], scale=1.0 / HD0).then_inc(hroot, 1)
            act.wait_ge(hnorm, 1)
            act.copy(HI.bitcast(F32R), QKV[:, :, 0:2 * D]).then_inc(hhi, 1)

            def ttt(run):
                with act.Fori(0, CHUNKS) as c:
                    act.wait_ge(run.mm, run.pe(c, "kv"))
                    act.copy(kv[:, :, :], PS[:, 0, :].rearrange("p (a n) -> p a n", a=4)).then_inc(run.th, 1)
                    with act.Fori(0, run.trips) as trip:
                        for par in range(2):
                            sweep = trip * 2 + par
                            act.wait_ge(run.ew, run.dv(c, "z", sweep))
                            act.activation(th[:, :, :], zh[:, :, :], ACT.Tanh).then_inc(run.th, 1)

            act.wait_ge(a0_zero, 1)
            act.wait_ge(first_kv, 1)
            act.copy(kvs[:, 0, :, :], PS[:, 1, :].rearrange("p (a n) -> p a n", a=4)).then_inc(first_copy, 1)
            with act.Fori(0, TRIPS) as trip:
                for r in TRIP:
                    if r[0] == "t" and r[2] == "kvn":
                        wait(act, t_pe, r[1:], trip)
                        act.copy(kvs[:, 1 - r[1], :, :], PS[:, 1, :].rearrange("p (a n) -> p a n", a=4))\
                            .then_inc(t_act.sem, 1)
                    elif r[0] == "t" and r[2] == "zc":
                        _, q, _, k = r
                        src = zh if k else zb
                        wait(act, t_dve, (q, "z", k) if k else (q, "zb"), trip)
                        act.activation(th[:, :, :], src[:, :, :], ACT.Tanh).then_inc(t_act.sem, 1)
                    elif r[0] == "copy":
                        _, kind, half, h = r
                        dst = qta if kind == "tq" else qtb
                        rows = slice(32 * h, 32 * h + 32)
                        wait(act, a0_pe, (kind, half), trip)
                        act.copy(dst[rows, h, 512 * half:512 * (half + 1)], PS[rows, TURN_BANK[(kind, half)], :])\
                            .then_inc(a0_act.sem, 1)
                    elif r[0] == "st":
                        _, n, h = r
                        c, j = SWEEP_B[n]
                        w = 512 * (c + 1) - max(512 * c, P * j)
                        wait(act, a0_pe, r, trip)
                        if n >= 2:
                            wait(act, a0_pe, ("pv", n - 2), trip)
                        act.activation(pe_[:, h, n % 2, 0:w], PS[:, 2 + h, 0:w], ACT.Exp, scale=HD0 ** -0.5)\
                            .then_inc(a0_act.sem, 1)

            for c in range(NC):
                act.wait_ge(z0_ps, c + 1)
                act.copy(Z0T[:, c * 512:(c + 1) * 512], PS[:, 4 + c, :]).then_inc(z0_cp, 1)
            act.wait_ge(ttt_flag, 1)
            settled = act.value_load(flag_i[0:1, 0:1], min_val=0, max_val=1)
            with act.If(settled == 0):
                ttt(ttt_full)
            with act.Else():
                act.nop()

            for c in range(NC):
                act.wait_ge(tq_q, c + 1)
                act.copy(QZ[:, c, :], PS[:, c, :]).then_inc(tq_qc, 1)
            act.wait_ge(rms_ss[1], NT)
            act.activation(rms_sd[:, :], ssq[:, :], ACT.Sqrt, bias=eps[:, 1:2], scale=1.0 / D)\
                .then_inc(rms_sq[1], 1)
            for c in range(NC):
                act.wait_ge(tq_z, c + 1)
                act.activation(SZ[:, c, :], PS[:, 4 + c, :], ACT.Silu, bias=ST_B1C).then_inc(tq_s, 1)

            for c in range(NC):
                act.wait_ge(xf_ps, c + 1)
                act.activation(XT[:, c * 512:(c + 1) * 512], PS[:, c, :], ACT.Copy, scale=w0("n2"))\
                    .then_inc(xf_cp, 1)

            def gate(layer, experts):
                act.wait_ge(gl_sub[layer], 1)
                act.activation(ge[:, :, 0:experts], lg[:, :, 0:experts], ACT.Exp).then_inc(gl_exp[layer], 1)

            gate(0, E0)

            with act.Fori(0, NC) as c:
                for u, (name, _, _, then, dst) in enumerate(units):
                    if then not in ("gelu", "silu"):
                        continue
                    wait(act, m0_pe, ("u", u), c)
                    if then == "gelu":
                        act.activation(hid[:, dst, :], PS[:, u % 6, :], ACT.Gelu).then_inc(m0_act.sem, 1)
                    else:
                        act.activation(e1t[:, name[1], :], PS[:, u % 6, :], ACT.Tanh, scale=0.5)\
                            .then_inc(m0_act.sem, 1)

            norm(1)

            def do_round(s, b, second=True, first=True):
                nb = 1 - b
                for r in ROUND:
                    if r[0] == "st" and second:
                        _, n, h = r
                        c, j = SWEEP_B[n]
                        w = 512 * (c + 1) - max(512 * c, P * j)
                        wait(act, s1_pe, r, s)
                        if n >= 2:
                            wait(act, s1_pe, ("pv", n - 2, h), s)
                        act.activation(pe_[:, h, n % 2, 0:w], PS[:, h, 0:w], ACT.Exp, scale=HD1 ** -0.5)\
                            .then_inc(s1_act.sem, 1)
                    elif r[0] == "pv" and r[1] in LAST and second:
                        _, n, h = r
                        c = LAST.index(n)
                        wait(act, s1_pe, r, s)
                        wait(act, w1_pe, ("w", c, 2), s, 1)
                        act.copy(ZT[0:HD1 + 1, h, c, :], PS[0:HD1 + 1, 2 + h, :]).then_inc(s1_act.sem, 1)
                    elif r in ("qh", "kh") and first:
                        dst, bank = (QA, 4) if r == "qh" else (KA, 6)
                        wait(act, f1_pe, r[0], s + 1)
                        for h in range(2):
                            rows = slice(h * HD1, (h + 1) * HD1)
                            act.copy(dst[rows, nb, h, :], PS[rows, bank:bank + 2, :].rearrange("p a n -> p (a n)"))\
                                .then_inc(f1_act.sem, 1)
                    elif r == "qb" and first:
                        wait(act, f1_act, ("qh", 1), s + 1)
                        for h in range(2):
                            act.copy(QB[0:HD1, nb, h, :], QA[h * HD1:(h + 1) * HD1, nb, h, :]).then_inc(f1_act.sem, 1)
                    elif r == "v" and first:
                        wait(act, f1_pe, "v", s + 1)
                        for half in range(2):
                            act.copy(VH[:, nb, :, 4 * half:4 * half + 4, 0:HD1],
                                     PS[:, 4 + half, :].rearrange("p (t h n) -> p h t n", t=4, h=2))\
                                .then_inc(f1_act.sem, 1)
                    elif r[0] == "mr" and first:
                        _, c, h = r
                        wait(act, f1_pe, r, s + 1)
                        act.copy(QB[HD1:HD1 + 2, nb, h, 512 * c:512 * (c + 1)], PS[0:2, MR_BANK[(c, h)], :])\
                            .then_inc(f1_act.sem, 1)

            do_round(-1, 1, second=False)
            gate(1, E1)
            with act.Fori(0, H1 // 2 - 1) as hp:
                do_round(hp * 2, 0)
                do_round(hp * 2 + 1, 1)
            do_round(ROUNDS - 2, 0)
            do_round(ROUNDS - 1, 1, first=False)

            act.wait_ge(f1_pe.sem, f1_pe.at(FIRST[-1], ROUNDS - 1))
            act.wait_ge(s1_pe.sem, s1_pe.at(("pv", NB - 1, 1), ROUNDS - 1))
            for c in range(NC):
                cols = slice(c * 512, (c + 1) * 512)
                act.copy(XH[:, cols], XT[:, cols]).then_inc(m1_tok_high, 1)
            with act.Fori(0, E1 // 2) as ep:
                for u in range(2 * NM1):
                    wait(act, m1_pe, ("u", u), ep)
                    if u >= 3:
                        wait(act, m1_dve, ("mu", u - 3), ep)
                    else:
                        wait(act, m1_dve, ("mu", max(v for v in range(2 * NM1) if v % 3 == u)), ep, 1)
                    act.activation(GS[:, u % 3, :], PS[:, 2 * (u % 3), :], ACT.Silu).then_inc(m1_act.sem, 1)

        @block.vector
        def _(dve):
            count = [0]

            def link(ins):
                count[0] += 1
                ins.then_inc(dve_chain, 1)
                dve.wait_ge(dve_chain, count[0])

            for s in (t_dve, a0_dve, m0_dve, f1_dve, w1_dve, m1_dve):
                dve.sem_inc(s.sem, s.per_trip)
            dve.sem_inc(ttt_full.ew, 1)
            dve.wait_ge(const_ready, N_CONST)

            def norm(layer):
                for t in range(NT):
                    if layer == 0:
                        dve.wait_ge(x_loaded, 32)
                    ins = dve.bn_stats(stats[:, t, :], X[:, t, :])
                link(ins)
                for t in range(NT):
                    dve.bn_aggr(mv[:, t, :], stats[:, t, :]).then_inc(ln_var[layer], 1)
                dve.wait_ge(ln_sd[layer], 1)
                link(dve.reciprocal(rstd[:, :], sd[:, :]))
                for t in range(NT):
                    dve.tensor_scalar(XN[:, t, :], X[:, t, :], mv[:, t, 0:1], rstd[:, t:t + 1], ALU.subtract,
                                      ALU.mult).then_inc(ln_done[layer], 1)
                dve.wait_ge(ln_done[layer], NT)

            def rms(which):
                squares = LO[:, :, 0:D]
                for t in range(NT):
                    dve.tensor_tensor_reduce(squares[:, t, :], XN[:, t, :], XN[:, t, :], 1.0, 0.0, ALU.mult, ALU.add,
                                             ssq[:, t:t + 1]).then_inc(rms_ss[which], 1)

            norm(0)
            rms(0)
            dve.wait_ge(rms_sq[0], 1)
            dve.reciprocal(rms_r[:, :], rms_sd[:, :]).then_inc(ln_done[0], 1)
            dve.wait_ge(w0_loaded, 16)
            dve.tensor_scalar(wqkv_n[:, :], w0("wqkv"), w0("n1"), None, ALU.mult).then_inc(qkv_w, 1)
            a, b_ = W0_AT["w1"][0], W0_AT["w2t"][1]
            dve.tensor_copy(st0[:, 0:3 * P], W0[:, a:b_])
            dve.tensor_scalar(st0[:, 3 * P:4 * P], w0("b1_rows"), 0.5, None, ALU.mult)
            dve.tensor_scalar(st0[:, 4 * P:5 * P], w0("b2_rows"), 1.0 / D, None, ALU.mult)
            dve.tensor_copy(st0[:, 5 * P:5 * P + 1], w0("b1_col"))
            link(dve.tensor_scalar(st0[:, 5 * P + 1:5 * P + 2], w0("b2_col"), 1.0 / D, None, ALU.mult))
            link(dve.tensor_copy(st[:, :], st0[:, :]))
            dve.wait_ge(hsq, 1)
            dve.tensor_reduce(hss.rearrange("p (t h) -> p t h", t=NT),
                              LO.rearrange("p t (h e) -> p t h e", e=HD0), AX.X, ALU.add).then_inc(hsum, 1)
            dve.wait_ge(hroot, 1)
            link(dve.reciprocal(hss, hsd))
            qk4 = QKV[:, :, 0:2 * D].rearrange("p t (h e) -> p t h e", e=HD0)
            link(dve.tensor_tensor(qk4, qk4, hss.rearrange("p (t h) -> p t h", t=NT).unsqueeze(3)
                                   .broadcast_to([P, NT, 32, HD0]), ALU.mult))
            for a, name in enumerate(("qn", "kn")):
                part = QKV[:, :, a * D:(a + 1) * D].rearrange("p t (h e) -> p t h e", e=HD0)
                ins = dve.tensor_tensor(part, part, w0(name).unsqueeze(1).unsqueeze(1)
                                        .broadcast_to([P, NT, H0, HD0]), ALU.mult)
                if a == 0:
                    link(ins)
            ins.then_inc(hnorm, 1)
            dve.wait_ge(hhi, 1)
            dve.tensor_tensor(LO, QKV[:, :, 0:2 * D], HI, ALU.subtract).then_inc(hlo, 1)

            def ttt(run):
                n = P // 2
                with dve.Fori(0, CHUNKS) as c:
                    dve.wait_ge(run.th, run.ac(c))
                    dve.tensor_scalar(vb[:, 0, :], kv[:, 2, :], 1.0 / D, ST_B2C, ALU.mult, ALU.subtract)\
                        .then_inc(run.ew, 1)
                    dve.scalar_tensor_tensor(vb[:, 1, :], kv[:, 3, :], 1.0 / D, ST_B2, ALU.mult,
                                             ALU.subtract).then_inc(run.ew, 1)
                    dve.wait_ge(run.mm, run.pe(c, "base"))
                    dve.scalar_tensor_tensor(g1[:, :], PS[:, 1, 0:P], 1.0, lr_mask_h[:, :], ALU.add, ALU.mult)\
                        .then_inc(run.ew, 1)
                    dve.tensor_scalar(zb[:, 0, :], PS[:, 1, P:2 * P], ST_B1C, 0.5, ALU.add, ALU.mult)\
                        .then_inc(run.ew, 1)
                    dve.scalar_tensor_tensor(zb[:, 1, :], PS[:, 1, 2 * P:3 * P], 0.5, ST_B1, ALU.mult, ALU.add)\
                        .then_inc(run.ew, 1)
                    dve.memset(gr[:, 1, :, :], 0.0).then_inc(run.ew, 1)
                    with dve.Fori(0, run.trips) as trip:
                        for par in range(2):
                            sweep = trip * 2 + par
                            dve.wait_ge(run.mm, run.pe(c, "zc", sweep))
                            dve.wait_ge(run.ew, run.dv_before(c, sweep))
                            dve.tensor_tensor(zh[:, :, :], PS[:, 0, 0:2 * P].rearrange("p (a n) -> p a n", a=2),
                                              zb[:, :, :], ALU.add).then_inc(run.ew, 1)
                            dve.wait_ge(run.th, run.ac(c, sweep))
                            dve.scalar_tensor_tensor(sl[:, :, :], th[:, :, :], 1.0, zh[:, :, :], ALU.add, ALU.mult)\
                                .then_inc(run.ew, 1)
                            dve.wait_ge(run.mm, run.pe(c, "ys", sweep))
                            dve.scalar_tensor_tensor(g2[:, :], PS[:, 0, 2 * P:3 * P], 1.0, lr_mask[:, :], ALU.add,
                                                     ALU.mult).then_inc(run.ew, 1)
                            dve.wait_ge(run.ew, run.dv(c, "s", sweep))
                            dve.scalar_tensor_tensor(du[:, :], th[:, 1, :], 1.0, sl[:, 1, :], ALU.subtract,
                                                     ALU.mult).then_inc(run.ew, 1)
                            dve.wait_ge(run.ew, run.dv(c, "u", sweep))
                            dve.scalar_tensor_tensor(dd[:, :], th[:, 1, :], 1.0, du[:, :], ALU.add,
                                                     ALU.subtract).then_inc(run.ew, 1)
                            dve.wait_ge(run.mm, run.pe(c, "yc", sweep))
                            dve.scalar_tensor_tensor(gr[:, par, 0:2, :],
                                                     PS[:, 1, 0:2 * P].rearrange("p (a n) -> p a n", a=2),
                                                     1.0 / D, vb[:, :, :], ALU.mult, ALU.subtract)\
                                .then_inc(run.ew, 1)
                            dve.wait_ge(run.mm, run.pe(c, "ds", sweep))
                            dve.tensor_tensor(g3[:, :], PS[:, 0, 3 * P:4 * P], lr_mask[:, :], ALU.mult)\
                                .then_inc(run.ew, 1)
                            dve.wait_ge(run.mm, run.pe(c, "dc", sweep))
                            dve.wait_ge(run.ew, run.dv(c, "d", sweep))
                            dve.scalar_tensor_tensor(gr[:, par, 2, :], PS[:, 1, 2 * P:3 * P], 0.5, dd[:, :],
                                                     ALU.mult, ALU.mult).then_inc(run.ew, 1)
                    dve.wait_ge(run.mm, run.pe(c, "up"))
                    dve.scalar_tensor_tensor(st[:, 0:3 * P], PS[:, 0, 0:3 * P], -LR, st[:, 0:3 * P], ALU.mult,
                                             ALU.add).then_inc(run.ew, 1)
                    dve.scalar_tensor_tensor(ST_B1, PS[:, 0, 3 * P:4 * P], -LR / 2, ST_B1, ALU.mult, ALU.add)\
                        .then_inc(run.ew, 1)
                    dve.scalar_tensor_tensor(ST_B2, PS[:, 1, 0:P], -LR / D, ST_B2, ALU.mult, ALU.add)\
                        .then_inc(run.ew, 1)
                    dve.scalar_tensor_tensor(ST_B1C, PS[:, 1, P:P + 1], -LR, ST_B1C, ALU.mult, ALU.add)\
                        .then_inc(run.ew, 1)
                    dve.scalar_tensor_tensor(ST_B2C, PS[:, 1, P + 1:P + 2], -LR / D, ST_B2C, ALU.mult, ALU.add)\
                        .then_inc(run.ew, 1)
                dve.wait_ge(run.ew, CHUNKS * run.td + 1)

            def train_step(trip, q, name, k=None):
                def on(dep, *a):
                    wait(dve, t_dve, (q, dep) + a, trip)

                def done(ins):
                    ins.then_inc(t_dve.sem, 1)

                gd = None if k is None else gr[:, parity(k), :, :]
                src = zh if k else zb
                if name == "base":
                    wait(dve, t_pe, (q, "base"), trip)
                    p, back = chunk_before(q)
                    wait(dve, t_dve, (p, "b2c"), trip, back)
                    wait(dve, t_act, (p, "kvn"), trip, back)
                    done(dve.tensor_scalar(zb[:, 0, :], PS[:, 0, P:2 * P], ST_B1C, 0.5, ALU.add, ALU.mult))
                    done(dve.scalar_tensor_tensor(zb[:, 1, :], PS[:, 0, 2 * P:3 * P], 0.5, ST_B1, ALU.mult, ALU.add))
                    done(dve.tensor_scalar(vb[:, 0, :], kvs[:, q, 2, :], 1.0 / D, ST_B2C, ALU.mult, ALU.subtract))
                    done(dve.scalar_tensor_tensor(vb[:, 1, :], kvs[:, q, 3, :], 1.0 / D, ST_B2, ALU.mult,
                                                  ALU.subtract))
                elif name == "zc":
                    if k:
                        wait(dve, t_pe, (q, "zc", k), trip)
                        on("sm", k - 1)
                        done(dve.tensor_tensor(zh[:, :, :], PS[:, 0, 0:2 * P].rearrange("p (a n) -> p a n", a=2),
                                               zb[:, :, :], ALU.add))
                    wait(dve, t_act, (q, "th", k), trip)
                    on("z", k) if k else on("zb")
                    for i in range(2):
                        done(dve.scalar_tensor_tensor(sl[:, i, :], th[:, i, :], 1.0, src[:, i, :], ALU.add, ALU.mult))
                    if k == 0:
                        check_difference()
                        on("cd")
                        done(check_maxima())
                elif name == "y":
                    wait(dve, t_pe, (q, "yt", k), trip)
                    if k == 0:
                        on("cm")
                    done(dve.scalar_tensor_tensor(gd[:, 0, :], PS[:, 1, 0:P], 1.0 / D, vb[:, 0, :], ALU.mult,
                                                  ALU.subtract))
                    on("sm", k)
                    done(dve.scalar_tensor_tensor(du[:, :], th[:, 1, :], 1.0, sl[:, 1, :], ALU.subtract, ALU.mult))
                    wait(dve, t_pe, (q, "ym", k), trip)
                    done(dve.scalar_tensor_tensor(gd[:, 1, :], PS[:, 0, 2 * P:3 * P], 1.0 / D, vb[:, 1, :], ALU.mult,
                                                  ALU.subtract))
                    on("u", k)
                    done(dve.scalar_tensor_tensor(dd[:, :], th[:, 1, :], 1.0, du[:, :], ALU.add, ALU.subtract))
                elif name == "ds":
                    wait(dve, t_pe, (q, "ds", k), trip)
                    done(dve.tensor_tensor(g3[:, :], PS[:, 1, 3 * P:4 * P], lr_mask[:, :], ALU.mult))
                elif name == "dc":
                    wait(dve, t_pe, (q, "dc", k), trip)
                    on("d", k)
                    done(dve.scalar_tensor_tensor(gd[:, 2, :], PS[:, 0, 3 * P:4 * P], 0.5, dd[:, :], ALU.mult,
                                                  ALU.mult))
                    if k + 1 < SWEEPS:
                        wait(dve, t_pe, (q, "ss", k), trip)
                        done(dve.scalar_tensor_tensor(g2[:, :], PS[:, 1, 2 * P:3 * P], 1.0, lr_mask[:, :], ALU.add,
                                                      ALU.mult))
                    else:
                        wait(dve, t_pe, (q, "kk"), trip)
                        next_g1().then_inc(t_dve.sem, 1)
                    if k == 0:
                        on("cm")
                        done(check_bounds())
                        on("cc")
                        done(check_keep())
                elif name == "up":
                    for dst, bank, lo, hi, by in ((ST_W1, 0, 0, P, -LR), (ST_B1, 0, P, 2 * P, -LR / 2),
                                                  (ST_B1C, 0, 2 * P, 2 * P + 1, -LR),
                                                  (st[:, P:3 * P], 1, 0, 2 * P, -LR), (ST_B2, 1, 2 * P, 3 * P, -LR / D),
                                                  (ST_B2C, 1, 3 * P, 3 * P + 1, -LR / D)):
                        if lo == 0:
                            wait(dve, t_pe, (q, ("up1", "up2")[bank]), trip)
                        done(dve.scalar_tensor_tensor(dst, PS[:, bank, lo:hi], by, dst, ALU.mult, ALU.add))

            def check_difference(last=False):
                ins = dve.tensor_tensor(grc[:, 6:8, :], gr[:, 1, 1:3, :], gr[:, 0, 1:3, :], ALU.subtract)
                if last:
                    return ins
                ins.then_inc(t_dve.sem, 1)

            def check_maxima():
                return dve.tensor_reduce(cmax[:, :], grc[:, 4:8, :], AX.X, ALU.max, apply_absolute_value=True)

            def check_bounds():
                return dve.scalar_tensor_tensor(cin[:, :], cmax[:, 0:2], CONVERGED, cmax[:, 2:4], ALU.mult, ALU.is_ge)

            def check_keep():
                return dve.tensor_tensor(okay[:, :], okay[:, :], cin[:, :], ALU.min)

            def next_g1():
                return dve.scalar_tensor_tensor(g1[:, :], PS[:, 1, 2 * P:3 * P], 1.0, lr_mask_h[:, :], ALU.add,
                                                ALU.mult)

            link(dve.memset(grc[:, :, :], 0.0))
            dve.wait_ge(first_kk, 1)
            link(next_g1())
            dve.wait_ge(first_copy, 1)
            with dve.Fori(0, B) as b:
                with dve.Fori(0, H0 // HG) as g:
                    trip = b * (H0 // HG) + g
                    for r in TRIP:
                        if r[0] == "t":
                            train_step(trip, *r[1:])
                        elif r[0] == "tk":
                            wait(dve, a0_pe, r, trip)
                            dve.tensor_copy(kta[:, 512 * r[1]:512 * (r[1] + 1)], PS[:, TURN_BANK[r], :])\
                                .then_inc(a0_dve.sem, 1)
                        elif r[0] == "a":
                            c, h, i, k = PIECES0[r[1]]
                            wait(dve, a0_pe, r, trip)
                            col = 32 * h + QM
                            if c == 0:
                                dst = tmq[:, i, col:col + 1]
                            else:
                                dst = NMH0[:, h, i - 4, k:k + 1]
                            dve.tensor_reduce(dst, PS[:, 2 + r[1] % 4, 0:min(512, (i + 1) * P - 512 * k)], AX.X,
                                              ALU.max, negate=True).then_inc(a0_dve.sem, 1)
                            if (c, i, k) == (1, TB - 1, 1):
                                wait(dve, a0_dve, ("mx", r[1]), trip)
                                dve.tensor_tensor(tmq[:, 4:8, col], NMH0[:, h, :, 0], NMH0[:, h, :, 1], ALU.min)\
                                    .then_inc(a0_dve.sem, 1)
                        elif r[0] == "pv" and r[1] in LAST:
                            wait(dve, a0_pe, r, trip)
                            dve.tensor_copy(ots[:, LAST.index(r[1]), :], PS[:, 6, :]).then_inc(a0_dve.sem, 1)
                        elif r[0] == "to":
                            c = r[1]
                            wait(dve, a0_pe, r, trip)
                            ov = PS[:, 7, :].rearrange("p (i h n) -> p (i h) n", i=4, h=HG)
                            dve.reciprocal(rz[:, c, :], ov[:, :, HD0]).then_inc(a0_dve.sem, 1)
                            wait(dve, a0_dve, ("rc", c), trip)
                            dst = Z0[:, bass.ds(b * TB + 4 * c, 4), bass.ds(g * (HG * HD0), HG * HD0)]
                            dve.tensor_tensor(dst.rearrange("p t (h e) -> p t h e", h=HG),
                                              ov[:, :, 0:HD0].rearrange("p (i h) n -> p i h n", i=4),
                                              rz[:, c, :].rearrange("p (i h) -> p i h", i=4).unsqueeze(3)
                                              .broadcast_to([P, 4, HG, HD0]), ALU.mult).then_inc(a0_dve.sem, 1)
            dve.wait_ge(t_dve.sem, t_dve.at((1, "b2c"), TRIPS - 1))
            link(check_difference(last=True))
            link(check_maxima())
            link(check_bounds())
            link(check_keep())
            finite = ots[:, :, :].rearrange("p a n -> p (a n)")[:, 0:STN]
            link(dve.tensor_tensor(finite, st[:, :], st[:, :], ALU.subtract))
            link(dve.tensor_scalar(finite, finite, 0.0, None, ALU.is_equal))
            link(dve.tensor_reduce(cin[:, 0:1], finite, AX.X, ALU.min))
            link(dve.tensor_reduce(cin[:, 1:2], okay[:, :], AX.X, ALU.min))
            dve.tensor_tensor(cok[:, 0:1], cin[:, 0:1], cin[:, 1:2], ALU.min).then_inc(ttt_okay, 1)
            dve.wait_ge(ttt_sum, 1)
            link(dve.tensor_scalar(flag_f[0:1, 0:1], PS[0:1, 2, 0:1], P - 0.5, None, ALU.is_ge))
            dve.tensor_copy(flag_i[0:1, 0:1], flag_f[0:1, 0:1]).then_inc(ttt_flag, 1)
            dve.wait_ge(ttt_flag, 1)
            settled = dve.value_load(flag_i[0:1, 0:1], min_val=0, max_val=1)
            with dve.If(settled == 0):
                dve.tensor_copy(st[:, :], st0[:, :]).then_inc(ttt_reset, 1)
                dve.wait_ge(ttt_reset, 1)
                ttt(ttt_full)
            with dve.Else():
                dve.nop()
            dve.tensor_copy(cok[:, 1:2], okay[:, 0:1]).then_inc(ttt_settled, 1)
            for c in range(NC):
                dve.wait_ge(ao_ps, c + 1)
                xs = XN[:, 4 * c:4 * c + 4, M_ZERO:D]
                dve.tensor_tensor(xs, PS[:, 4 + c, :].rearrange("p (t n) -> p t n", t=4)[:, :, 0:D - M_ZERO], xs,
                                  ALU.add).then_inc(ao_add, 1)
            dve.wait_ge(ao_add, NC)
            rms(1)
            dve.wait_ge(rms_sq[1], 1)
            link(dve.reciprocal(rms_r[:, :], rms_sd[:, :]))
            for t in range(NT):
                dve.tensor_scalar(Z0[:, t, :], XN[:, t, :], rms_r[:, t:t + 1], None, ALU.mult).then_inc(xf_tile, 1)
            link(dve.scalar_tensor_tensor(X[:, :, :], ST_B2.unsqueeze(1).broadcast_to([P, NT, D]), float(D),
                                          X[:, :, :], ALU.mult, ALU.add))
            for c in range(NC):
                dve.wait_ge(tq_y, c + 1)
                xs = X[:, 4 * c:4 * c + 4, :]
                dve.tensor_tensor(xs, PS[:, c, :].rearrange("p (t n) -> p t n", t=4), xs, ALU.add)\
                    .then_inc(tq_acc, 1)
            dve.wait_ge(tq_acc, NC)
            dve.tensor_tensor(X[:, :, :], X[:, :, :], XN[:, :, :], ALU.add).then_inc(x_plus, 1)

            def gate(layer, experts, wts):
                n = experts
                l, e_, p_ = lg[:, :, 0:n], ge[:, :, 0:n], gp[:, :, 0:n]
                dve.wait_ge(gl_ps[layer], 1)
                ps = PS[:, 2 if layer else 6, 0:NT * n].rearrange("p (t e) -> p t e", e=n)
                if layer == 0:
                    link(dve.tensor_copy(p_, ps))
                    link(dve.memset(l, 0.0))
                    link(dve.tensor_tensor(lgm[:, :, 0:n], p_, p_, ALU.is_equal))
                    link(dve.copy_predicated(l, lgm[:, :, 0:n], p_))
                    big = float(np.finfo(np.float32).max)
                    link(dve.tensor_scalar(l, l, big, -big, ALU.min, ALU.max))
                else:
                    link(dve.tensor_copy(l, ps))

                def rows(v):
                    return v.unsqueeze(2).broadcast_to([P, NT, n])

                link(dve.tensor_reduce(lgx[:, :], l, AX.X, ALU.max))
                dve.tensor_tensor(l, l, rows(lgx[:, :]), ALU.subtract).then_inc(gl_sub[layer], 1)
                dve.wait_ge(gl_exp[layer], 1)
                link(dve.tensor_reduce(lgx[:, :], e_, AX.X, ALU.add))
                link(dve.reciprocal(wsum[:, :], lgx[:, :]))
                link(dve.tensor_tensor(p_, e_, rows(wsum[:, :]), ALU.mult))
                cmp = gc[:, 0:n, 0:NT * n].rearrange("p f (t e) -> p f t e", e=n)
                link(dve.memset(gc[:, 0:n, 0:NT * n], 0.0))
                for f in range(n):
                    def other(k):
                        return p_[:, :, f:f + 1].broadcast_to([P, NT, k])
                    if f + 1 < n:
                        ins = dve.tensor_tensor(cmp[:, f, :, f + 1:n], other(n - 1 - f), p_[:, :, f + 1:n],
                                                ALU.is_ge)
                    if f:
                        ins = dve.tensor_tensor(cmp[:, f, :, 0:f], other(f), p_[:, :, 0:f], ALU.is_gt)
                link(ins)
                link(dve.tensor_reduce(rank[:, :, 0:n].rearrange("p t e -> p t e"),
                                       gc[:, 0:n, 0:NT * n].rearrange("p f (t e) -> p t e f", e=n), AX.X, ALU.add))
                link(dve.scalar_tensor_tensor(e_, rank[:, :, 0:n], 1.5, p_, ALU.is_lt, ALU.mult))
                link(dve.tensor_reduce(lgx[:, :], e_, AX.X, ALU.add))
                link(dve.tensor_scalar(lgx[:, :], lgx[:, :], 1e-8, None, ALU.add))
                link(dve.reciprocal(wsum[:, :], lgx[:, :]))
                dve.tensor_tensor(wts[:, :, :].rearrange("p e t -> p t e"), e_, rows(wsum[:, :]), ALU.mult)\
                    .then_inc(gl_done[layer], 1)
                dve.wait_ge(gl_done[layer], 1)

            gate(0, E0, wt0)

            dve.wait_ge(x_plus, 1)
            with dve.Fori(0, NC) as c:
                for kind, u in seq0:
                    if kind == "dn":
                        bank = 6 + dn_order.index(u) % 2
                        wait(dve, m0_pe, ("dn", u), c)
                        for i in range(4):
                            if u != dn_order[0]:
                                wait(dve, m0_dve, ("ac", dn_order[dn_order.index(u) - 1], i), c)
                            xs = X[:, bass.ds(c * 4 + i, 1), M_ZERO:D]
                            dve.scalar_tensor_tensor(
                                xs, PS[:, bank, i * P:i * P + D - M_ZERO].unsqueeze(1),
                                wt0[:, u, bass.ds(c * 4 + i, 1)], xs, ALU.mult, ALU.add).then_inc(m0_dve.sem, 1)
                        continue
                    then = units[u][3]
                    m = units[u][0][1]
                    if then == "silu":
                        wait(dve, m0_act, ("u", u), c)
                        dve.scalar_tensor_tensor(hid[:, HU[("e1g", m)], :], e1t[:, m, :], 1.0, PS[:, u % 6, :],
                                                 ALU.add, ALU.mult).then_inc(m0_dve.sem, 1)
                    elif then == "times":
                        wait(dve, m0_pe, ("u", u), c)
                        wait(dve, m0_dve, ("sg", 2 + m), c)
                        dve.scalar_tensor_tensor(hid[:, HU[("e1v", m)], :], hid[:, HU[("e1g", m)], :], 0.5,
                                                 PS[:, u % 6, :], ALU.mult, ALU.mult).then_inc(m0_dve.sem, 1)
            dve.wait_ge(m0_dve.sem, m0_dve.at(dve0[-1], NC - 1))

            norm(1)

            def do_round(s, b, second=True, first=True):
                for r in ROUND:
                    if r[0] == "w" and second:
                        _, c, g = r
                        bank = W_BANK[(c, g)]
                        lo, n = GROUPS[g][0], len(GROUPS[g])
                        wait(dve, w1_pe, r, s)
                        if (c, g) == (0, 0):
                            wait(dve, w1_dve, ("x", 1, 7), s, 1)
                        view = PS[:, bank, 0:n * (D + 1)].rearrange("p (q n) -> p q n", q=n)
                        dve.reciprocal(RS[:, c, lo:lo + n], view[:, :, D]).then_inc(w1_dve.sem, 1)
                        wait(dve, w1_dve, ("rs", c, g), s)
                        for q in GROUPS[g]:
                            t = TB * b + 4 * c + q // 2
                            if q % 2:
                                wait(dve, w1_dve, ("x", c, q - 1), s)
                            dve.scalar_tensor_tensor(X[:, t, :], view[:, q - lo, 0:D], RS[:, c, q:q + 1], X[:, t, :],
                                                     ALU.mult, ALU.add).then_inc(w1_dve.sem, 1)
                    elif r in ("qh", "kh") and first:
                        for h in range(2):
                            rows, others = slice(h * HD1, (h + 1) * HD1), slice((1 - h) * HD1, (2 - h) * HD1)
                            wait(dve, f1_act, (r, 1), s + 1)
                            if r == "qh":
                                dst, high, bank = QA[others, 1 - b, h, :], QA[rows, 1 - b, h, :], 4
                            else:
                                dst, high, bank = KB[0:HD1, 1 - b, h, :], KA[rows, 1 - b, h, :], 6
                            dve.tensor_tensor(dst, PS[rows, bank:bank + 2, :].rearrange("p a n -> p (a n)"),
                                              high.bitcast(F32), ALU.subtract).then_inc(f1_dve.sem, 1)
                    elif r == "kd" and first:
                        for h in range(2):
                            rows, others = slice(h * HD1, (h + 1) * HD1), slice((1 - h) * HD1, (2 - h) * HD1)
                            dve.tensor_copy(KA[others, 1 - b, h, :], KA[rows, 1 - b, h, :]).then_inc(f1_dve.sem, 1)
                    elif r[0] == "a" and first:
                        p = r[1]
                        c, h, i, k = PIECES[p]
                        w = min(512, (i + 1) * P - 512 * k)
                        wait(dve, f1_pe, r, s + 1)
                        dst = NMH[:, h, i - 4, k:k + 1] if c else NM[:, h, i:i + 1]
                        if p == 8:
                            wait(dve, f1_dve, ("cb", 1), s + 1, 1)
                        dve.tensor_reduce(dst, PS[:, 4 + p % 2, 0:w], AX.X, ALU.max, negate=True)\
                            .then_inc(f1_dve.sem, 1)
                        if p in (15, 23):
                            wait(dve, f1_dve, ("mx", p), s + 1)
                            dve.tensor_tensor(NM[:, h, 4:8], NMH[:, h, :, 0], NMH[:, h, :, 1], ALU.min)\
                                .then_inc(f1_dve.sem, 1)
                        if p in (3, 7, 15, 23):
                            wait(dve, f1_dve, ("cb", h) if c else ("mx", p), s + 1)
                            part = NM2[:, h, 4 * c:4 * c + 4, :]
                            dve.tensor_copy(part[:, :, 0].bitcast(F32R), NM[:, h, 4 * c:4 * c + 4])\
                                .then_inc(f1_dve.sem, 1)
                            wait(dve, f1_dve, ("nh", c, h), s + 1)
                            dve.tensor_tensor(part[:, :, 1], NM[:, h, 4 * c:4 * c + 4], part[:, :, 0], ALU.subtract)\
                                .then_inc(f1_dve.sem, 1)

            do_round(-1, 1, second=False)
            gate(1, E1, wt1)
            with dve.Fori(0, H1 // 2 - 1) as hp:
                do_round(hp * 2, 0)
                do_round(hp * 2 + 1, 1)
            do_round(ROUNDS - 2, 0)
            do_round(ROUNDS - 1, 1, first=False)
            dve.wait_ge(w1_dve.sem, w1_dve.at(("x", 1, 7), ROUNDS - 1))

            for c in range(NC):
                cols = slice(c * 512, (c + 1) * 512)
                dve.wait_ge(m1_tok_high, c + 1)
                dve.tensor_tensor(XL[:, cols], XT[:, cols], XH[:, cols].bitcast(F32), ALU.subtract)\
                    .then_inc(m1_tok_low, 1)
            def weights_low(ep, k):
                dve.wait_ge(m1_pool.sem, ep * 2 + k + 1)
                wait(dve, m1_pe, ("u", NM1 * (k + 1) - 1), ep, 1)
                for dst, name in ((w11_s, "w11"), (w12_s, "w12")):
                    at = W1_AT[name][0] + k * HID
                    ins = dve.tensor_tensor(dst[:, k, 1, :], W1[:, bass.ds(ep * (2 * HID) + at, HID)],
                                            dst[:, k, 0, :].bitcast(F32), ALU.subtract)
                ins.then_inc(m1_low.sem, 1)

            weights_low(0, 0)
            with dve.Fori(0, E1 // 2) as ep:
                for m in range(NM1 + 1):
                    if m == NC - 1:
                        weights_low(ep, 1)
                    if m == NM1 - 1:
                        weights_low(ep + 1, 0)
                    if m < NM1:
                        for u in (2 * m, 2 * m + 1):
                            wait(dve, m1_act, ("u", u), ep)
                            if m >= 2:
                                wait(dve, m1_pe, ("dn", m - 2), ep)
                            dve.tensor_tensor(HB[:, m % 2, u % 2, :], GS[:, u % 3, :], PS[:, 2 * (u % 3) + 1, :],
                                              ALU.mult).then_inc(m1_dve.sem, 1)
                    if m >= 1:
                        k = m - 1
                        wait(dve, m1_pe, ("dn", k), ep)
                        for i in range(4):
                            t = (k % NC) * 4 + i
                            if k >= NC:
                                wait(dve, m1_dve, ("ac", k - NC, i), ep)
                            else:
                                wait(dve, m1_dve, ("ac", k + NC, i), ep, 1)
                            dve.scalar_tensor_tensor(
                                X[:, t, :], PS[:, 6 + k % 2, i * P:(i + 1) * P],
                                wt1[:, bass.ds(ep * 2 + k // NC, 1), t], X[:, t, :], ALU.mult, ALU.add)\
                                .then_inc(m1_dve.sem, 1)

        @block.tensor
        def _(pe):
            for s in (t_pe, a0_pe, m0_pe, f1_pe, s1_pe, w1_pe, m1_pe):
                pe.sem_inc(s.sem, s.per_trip)
            pe.sem_inc(ttt_full.mm, 1)
            pe.wait_ge(const_ready, N_CONST)

            def turn(layer, src, ready, done, first_bank=0):
                for t in range(NT):
                    if ready is not None:
                        pe.wait_ge(ready, t + 1)
                    ins = pe.transpose(PS[:, first_bank + t // 4, (t % 4) * P:(t % 4 + 1) * P], src[:, t, :],
                                       ident[:, :])
                    if t % 4 == 3:
                        ins.then_inc(done, 1)

            turn(0, XN, ln_done[0], xt_ps[0])
            pe.wait_ge(qkv_w, 1)
            for t in range(NT):
                pe.wait_ge(xt_done[0], t // 4 + 1)
                if t >= 4:
                    pe.wait_ge(qkv_done, t - 3)
                pe.matmul(PS[:, 4 + t % 4, 0:3 * D], XT[:, t * P:(t + 1) * P], wqkv_n[:, :], start=True, stop=True)\
                    .then_inc(qkv_ps, 1)

            def mm(*args, **kw):
                return pe.matmul(*args, skip_group_check=True, **kw)

            def ttt(run):
                def ps(bank, k):
                    return PS[:, bank, k * P:(k + 1) * P]

                xcv = xc[:, :, :].rearrange("p b s -> p (b s)")
                with pe.Fori(0, CHUNKS) as c:
                    pe.wait_ge(run.staged, c + 1)
                    pe.wait_ge(run.ew, c * run.td + 1)
                    wk, wv = w0("wk_ttt"), w0("wv_ttt")
                    mm(ps(0, 0), wk, xcv, start=True, stop=True)
                    mm(ps(0, 1), xcv, wk, start=True, stop=True)
                    mm(ps(0, 2), wv, xcv, start=True, stop=True)
                    mm(ps(0, 3), xcv, wv, start=True, stop=True).then_inc(run.mm, 1)
                    pe.wait_ge(run.th, run.ac(c))
                    mm(ps(1, 0), kv[:, 0, :], kv[:, 0, :], start=True, stop=True)
                    mm(ps(1, 1), ST_W1, kv[:, 0, :], start=True, stop=True)
                    mm(ps(1, 2), kv[:, 0, :], ST_W1, start=True, stop=True).then_inc(run.mm, 1)
                    with pe.Fori(0, run.trips) as trip:
                        for par in range(2):
                            sweep = trip * 2 + par
                            dyo, dzo = gr[:, 1 - par, 1, :], gr[:, 1 - par, 2, :]
                            dyt = gr[:, par, 0, :]
                            s_t, s_tm = sl[:, 0, :], sl[:, 1, :]
                            pe.wait_ge(run.ew, run.dv_before(c, sweep))
                            mm(ps(0, 0), dzo, g1[:, :], start=True, stop=True)
                            mm(ps(0, 1), g1[:, :], dzo, start=True, stop=True).then_inc(run.mm, 1)
                            pe.wait_ge(run.ew, run.dv(c, "s", sweep))
                            mm(ps(0, 2), s_t, s_t, start=True, stop=True)
                            mm(ps(1, 0), ST_W2, s_t, start=True, stop=False)
                            mm(ps(1, 1), s_t, ST_W2, start=False, stop=False).then_inc(run.mm, 1)
                            pe.wait_ge(run.ew, run.dv(c, "g2", sweep))
                            mm(ps(1, 0), dyo, g2[:, :], start=False, stop=False)
                            mm(ps(1, 1), g2[:, :], dyo, start=False, stop=True).then_inc(run.mm, 1)
                            pe.wait_ge(run.ew, run.dv(c, "dy", sweep))
                            mm(ps(0, 3), dyt, dyt, start=True, stop=True)
                            mm(ps(1, 2), dyt, ST_W2T, start=True, stop=False).then_inc(run.mm, 1)
                            pe.wait_ge(run.ew, run.dv(c, "g3", sweep))
                            mm(ps(1, 2), g3[:, :], s_tm, start=False, stop=True).then_inc(run.mm, 1)
                    pe.wait_ge(run.ew, run.dv_before(c, run.sweeps))
                    dy, dz, s_tm = gr[:, 1, 1, :], gr[:, 1, 2, :], sl[:, 1, :]
                    mm(ps(0, 0), kv[:, 1, :], dz, start=True, stop=True)
                    mm(ps(0, 1), s_tm, dy, start=True, stop=True)
                    mm(ps(0, 2), dy, s_tm, start=True, stop=True)
                    mm(ps(0, 3), ones[:, :], dz, start=True, stop=True)
                    mm(ps(1, 0), ones[:, :], dy, start=True, stop=True)
                    mm(PS[:, 1, P:P + 1], dz, ones[:, 0:1], start=True, stop=True)
                    mm(PS[:, 1, P + 1:P + 2], dy, ones[:, 0:1], start=True, stop=True).then_inc(run.mm, 1)

            def train_step(trip, q, name, k=None):
                def ps(bank, i):
                    return PS[:, bank, i * P:(i + 1) * P]

                def on(dep, *a):
                    wait(pe, t_dve, (q, dep) + a, trip)

                s_t, s_tm = sl[:, 0, :], sl[:, 1, :]
                p, back = chunk_before(q)
                if name == "base":
                    wait(pe, t_dve, (p, "b1c"), trip, back)
                    wait(pe, t_act, (p, "kvn"), trip, back)
                    mm(ps(0, 1), ST_W1, kvs[:, q, 0, :], start=True, stop=True)
                    mm(ps(0, 2), kvs[:, q, 0, :], ST_W1, start=True, stop=True).then_inc(t_pe.sem, 1)
                elif name == "zc" and k:
                    dzo = gr[:, 1 - parity(k), 2, :]
                    on("dz", k - 1)
                    mm(ps(0, 0), dzo, g1[:, :], start=True, stop=True)
                    mm(ps(0, 1), g1[:, :], dzo, start=True, stop=True).then_inc(t_pe.sem, 1)
                elif name == "kvn":
                    wait(pe, t_pool, (q, "xc"), trip)
                    on("g2", SWEEPS - 2)
                    keys_values().then_inc(t_pe.sem, 1)
                elif name == "y":
                    on("st", k)
                    if k + 1 == SWEEPS:
                        wait(pe, t_act, (q, "kvn"), trip)
                    ins = mm(ps(1, 0), ST_W2, s_t, start=True, stop=not k)
                    if k:
                        dyo = gr[:, 1 - parity(k), 1, :]
                        ins = mm(ps(1, 0), dyo, g2[:, :], start=False, stop=True)
                    ins.then_inc(t_pe.sem, 1)
                    ins = mm(ps(0, 2), s_t, ST_W2, start=True, stop=not k)
                    if k:
                        ins = mm(ps(0, 2), g2[:, :], dyo, start=False, stop=True)
                    ins.then_inc(t_pe.sem, 1)
                elif name == "ds":
                    dyt = gr[:, parity(k), 0, :]
                    on("dyt", k)
                    mm(ps(1, 3), dyt, dyt, start=True, stop=True).then_inc(t_pe.sem, 1)
                    on("dym", k)
                    mm(ps(0, 3), dyt, ST_W2T, start=True, stop=False)
                elif name == "dc":
                    on("g3", k)
                    mm(ps(0, 3), g3[:, :], s_tm, start=False, stop=True).then_inc(t_pe.sem, 1)
                    if k + 1 < SWEEPS:
                        mm(ps(1, 2), s_t, s_t, start=True, stop=True).then_inc(t_pe.sem, 1)
                    else:
                        kt = kvs[:, 1 - q, 0, :]
                        mm(ps(1, 2), kt, kt, start=True, stop=True).then_inc(t_pe.sem, 1)
                elif name == "up":
                    on("dz", SWEEPS - 1)
                    dy, dz = gr[:, 1, 1, :], gr[:, 1, 2, :]
                    mm(ps(0, 0), kvs[:, q, 1, :], dz, start=True, stop=True)
                    mm(ps(0, 1), ones[:, :], dz, start=True, stop=True)
                    mm(PS[:, 0, 2 * P:2 * P + 1], dz, ones[:, 0:1], start=True, stop=True).then_inc(t_pe.sem, 1)
                    on("g1")
                    mm(ps(1, 0), s_tm, dy, start=True, stop=True)
                    mm(ps(1, 1), dy, s_tm, start=True, stop=True)
                    mm(ps(1, 2), ones[:, :], dy, start=True, stop=True)
                    mm(PS[:, 1, 3 * P:3 * P + 1], dy, ones[:, 0:1], start=True, stop=True).then_inc(t_pe.sem, 1)

            def keys_values():
                xcv = xc[:, :, :].rearrange("p b s -> p (b s)")
                wk, wv = w0("wk_ttt"), w0("wv_ttt")
                mm(PS[:, 1, 0:P], wk, xcv, start=True, stop=True)
                mm(PS[:, 1, P:2 * P], xcv, wk, start=True, stop=True)
                mm(PS[:, 1, 2 * P:3 * P], wv, xcv, start=True, stop=True)
                return mm(PS[:, 1, 3 * P:4 * P], xcv, wv, start=True, stop=True)

            pe.wait_ge(first_xc, 1)
            keys_values().then_inc(first_kv, 1)
            pe.wait_ge(first_copy, 1)
            mm(PS[:, 1, 2 * P:3 * P], kvs[:, 0, 0, :], kvs[:, 0, 0, :], start=True, stop=True).then_inc(first_kk, 1)
            pe.wait_ge(hlo, 1)
            with pe.Fori(0, TRIPS) as trip:
                for r in TRIP:
                    if r[0] == "t":
                        train_step(trip, *r[1:])
                    elif r[0] in ("tq", "tk", "tq2", "to"):
                        kind, half = r
                        tm, bank = {"tk": tmk, "to": None}.get(kind, tmq), TURN_BANK[r]
                        if kind in ("tq", "tk"):
                            pe.wait_ge(a0_pool.sem, trip * 3 + (2 if kind == "tq" else 1))
                            if half:
                                s_, last = (a0_dve, ("ka", 0)) if kind == "tk" else (a0_act, ("qa", 0, HG - 1))
                                wait(pe, s_, last, trip)
                            else:
                                wait(pe, a0_dve, ("oc", 1) if kind == "tk" else ("zt", 1), trip, 1)
                        elif kind == "tq2":
                            wait(pe, a0_dve, ("cb", HG - 1) if half else ("mx", P0_HALF - 1), trip)
                            wait(pe, a0_act, ("qb", 0, HG - 1) if half else ("qa", 1, HG - 1), trip)
                        else:
                            wait(pe, a0_dve, ("oc", half), trip)
                            if half:
                                wait(pe, a0_dve, ("zt", 0), trip)
                            else:
                                wait(pe, a0_act, ("qb", 1, HG - 1), trip)
                        for i in range(4):
                            src = tm[:, 4 * half + i, :] if tm is not None else ots[:, half, i * P:(i + 1) * P]
                            ins = pe.transpose(PS[:, bank, i * P:(i + 1) * P], src, ident[:, :])
                        ins.then_inc(a0_pe.sem, 1)
                    elif r[0] == "a":
                        p = r[1]
                        c, h, i, k = PIECES0[p]
                        w = min(512, (i + 1) * P - 512 * k)
                        bank = 2 + p % 4
                        if (i, k) == (4 * c, 0):
                            wait(pe, a0_act, ("qa", c, h), trip)
                            wait(pe, a0_dve, ("ka", c), trip)
                        if p >= 4:
                            wait(pe, a0_dve, ("mx", p - 4), trip)
                        else:
                            wait(pe, a0_act, ("ex", NB - 1, p), trip, 1)
                        ins = pe.matmul(PS[:, bank, 0:w], qta[:, h, i * P:(i + 1) * P], kta[:, 512 * k:512 * k + w],
                                        start=True, stop=True)
                        if k == c:
                            ins = pe.matmul(PS[:, bank, w - P:w], ident_b[:, :], mask_qk[:, :], start=False,
                                            stop=True, skip_group_check=True)
                        ins.then_inc(a0_pe.sem, 1)
                    elif r[0] == "st":
                        _, n, h = r
                        c, j = SWEEP_B[n]
                        q0 = max(512 * c, P * j)
                        w = 512 * (c + 1) - q0
                        if n:
                            wait(pe, a0_act, ("ex", n - 1, h), trip)
                        if j == 0:
                            wait(pe, a0_act, ("qb", c, h), trip)
                        ins = pe.matmul(PS[:, 2 + h, 0:w], kta[:, j * P:(j + 1) * P], qtb[:, h, q0:q0 + w],
                                        start=True, stop=True)
                        if j >= 4 * c:
                            ins = pe.matmul(PS[:, 2 + h, 0:P], ident_b[:, :], mask_kq[:, :], start=False, stop=True,
                                            skip_group_check=True)
                        ins.then_inc(a0_pe.sem, 1)
                    elif r[0] == "pv":
                        n = r[1]
                        c, j = SWEEP_B[n]
                        q0 = max(512 * c, P * j)
                        if n == 0:
                            pe.wait_ge(a0_pool.sem, trip * 3 + 3)
                            wait(pe, a0_dve, ("ka", 1), trip)
                        elif j == 0:
                            wait(pe, a0_dve, ("oc", 0), trip)
                        for h in range(HG):
                            wait(pe, a0_act, ("ex", n, h), trip)
                            ins = pe.matmul(PS[32 * h:32 * h + 32, 6, q0 - 512 * c:512],
                                            tmv[:, j, 32 * h:32 * h + 32], pe_[:, h, n % 2, 0:512 * (c + 1) - q0],
                                            start=(j == 0), stop=(j == 4 * c + 3), skip_group_check=True)
                        ins.then_inc(a0_pe.sem, 1)
            pe.wait_ge(a0_dve.sem, a0_dve.at(("zt", 1), TRIPS - 1))

            turn(0, Z0, None, z0_ps, first_bank=4)

            pe.wait_ge(ttt_okay, 1)
            pe.matmul(PS[0:1, 2, 0:1], cok[:, 0:1], ones[:, 0:1], start=True, stop=True).then_inc(ttt_sum, 1)
            pe.wait_ge(ttt_flag, 1)
            settled = pe.value_load(flag_i[0:1, 0:1], min_val=0, max_val=1)
            with pe.If(settled == 0):
                pe.wait_ge(ttt_reset, 1)
                ttt(ttt_full)
            with pe.Else():
                pe.nop()

            for t in range(NT):
                pe.wait_ge(z0_cp, t // 4 + 1)
                ins = pe.matmul(PS[:, 4 + t // 4, (t % 4) * P:(t % 4) * P + D - M_ZERO], Z0T[:, t * P:(t + 1) * P],
                                w0("wo", M_ZERO), start=True, stop=True)
                if t % 4 == 3:
                    ins.then_inc(ao_ps, 1)
            pe.wait_ge(ttt_settled, 1)
            for c in range(NC):
                pe.matmul(PS[:, c, :], w0("wq_ttt"), XT[:, c * 512:(c + 1) * 512], start=True, stop=True)\
                    .then_inc(tq_q, 1)
            for c in range(NC):
                pe.wait_ge(tq_qc, c + 1)
                pe.wait_ge(ao_add, c + 1)
                pe.matmul(PS[:, 4 + c, :], ST_W1, QZ[:, c, :], start=True, stop=True).then_inc(tq_z, 1)
            for c in range(NC):
                pe.wait_ge(tq_s, c + 1)
                for i in range(4):
                    ins = pe.matmul(PS[:, c, i * P:(i + 1) * P], SZ[:, c, i * P:(i + 1) * P], ST_W2, start=True,
                                    stop=True)
                ins.then_inc(tq_y, 1)
            pe.wait_ge(tq_acc, NC)

            turn(0, Z0, xf_tile, xf_ps)
            pe.wait_ge(ao_add, NC)
            pe.wait_ge(xf_cp, NC)

            def gate(layer, weights, experts, bank):
                for t in range(NT):
                    ins = pe.matmul(PS[:, bank, t * experts:(t + 1) * experts], XT[:, t * P:(t + 1) * P], weights,
                                    start=True, stop=True)
                ins.then_inc(gl_ps[layer], 1)

            gate(0, w0("gate"), E0, 6)

            with pe.Fori(0, NC) as c:
                for kind, u in seq0:
                    if kind == "u":
                        name, blocks, rhs, then, dst = units[u]
                        if u >= 6:
                            s, step = unit_freed(u - 6)
                            wait(pe, s, step, c)
                        else:
                            s, step = unit_freed(max(v for v in range(15) if v % 6 == u))
                            wait(pe, s, step, c, 1)
                        for k, (lhs, r) in enumerate(zip(blocks, rhs)):
                            if r is None:
                                src = XT[:, bass.ts(c, 512)]
                            else:
                                made = next(v for v, s_ in enumerate(units) if s_[4] == r)
                                wait(pe, m0_act, ("u", made), c)
                                src = hid[:, r, :]
                            ins = pe.matmul(PS[:, u % 6, :], lhs, src, start=(k == 0), stop=(k == len(blocks) - 1))
                        ins.then_inc(m0_pe.sem, 1)
                    else:
                        wname, src = DOWN[u]
                        place = dn_order.index(u)
                        bank = 6 + place % 2
                        if place == 0:
                            pe.wait_ge(gl_sub[0], 1)
                        if u == 1:
                            wait(pe, m0_dve, ("tm", 5), c)
                        else:
                            made = next(v for v, s_ in enumerate(units) if s_[4] == HU[(src, 1)])
                            wait(pe, m0_act, ("u", made), c)
                        if place >= 2:
                            wait(pe, m0_dve, ("ac", dn_order[place - 2], 3), c)
                        else:
                            wait(pe, m0_dve, ("ac", dn_order[place + 2], 3), c, 1)
                        for i in range(4):
                            for k in range(2):
                                ins = pe.matmul(PS[:, bank, i * P:i * P + D - M_ZERO],
                                                hid[:, HU[(src, k)], i * P:(i + 1) * P],
                                                w0(wname, k * D + M_ZERO, (k + 1) * D), start=(k == 0), stop=(k == 1))
                        ins.then_inc(m0_pe.sem, 1)

            pe.wait_ge(m0_act.sem, m0_act.at(m0_act.names[-1], NC - 1))
            pe.wait_ge(m0_dve.sem, m0_dve.at(dve0[-1], NC - 1))
            turn(1, XN, ln_done[1], xt_ps[1])
            pe.wait_ge(xt_done[1], NC)
            pe.wait_ge(w1_loaded, 16)


            def do_round(s, b, hp, next_hp, second=True, first=True):
                nb = 1 - b
                for r in ROUND:
                    if r[0] == "st" and second:
                        _, n, h = r
                        c, j = SWEEP_B[n]
                        q0 = max(512 * c, P * j)
                        w = 512 * (c + 1) - q0
                        if n in (0, 4):
                            wait(pe, f1_act, ("me", c, h), s)
                        if n:
                            wait(pe, s1_act, ("ex", n - 1, h), s)
                        else:
                            wait(pe, s1_act, ("ex", NB - 1, h), s, 1)
                        pe.matmul(PS[:, h, 0:w], KA[:, b, h, j * P:(j + 1) * P], QA[:, b, h, q0:q0 + w],
                                  start=True, stop=False)
                        ins = pe.matmul(PS[:, h, 0:w], KB[0:HD1 + 2, b, h, j * P:(j + 1) * P],
                                        QB[0:HD1 + 2, b, h, q0:q0 + w], start=False, stop=True)
                        if j >= 4 * c:
                            ins = pe.matmul(PS[:, h, 0:P], ident_b[:, :], mask_kq[:, :], start=False, stop=True,
                                            skip_group_check=True)
                        ins.then_inc(s1_pe.sem, 1)
                    elif r[0] == "pv" and second:
                        _, n, h = r
                        c, j = SWEEP_B[n]
                        q0 = max(512 * c, P * j)
                        if n == 0:
                            wait(pe, s1_act, ("oc", 1, h), s, 1)
                            pe.wait_ge(gl_sub[1], 1)
                            if 2 + h == W_BANK[(1, 2)]:
                                wait(pe, w1_dve, ("x", 1, 7), s, 1)
                        elif j == 0:
                            wait(pe, s1_act, ("oc", 0, h), s)
                        wait(pe, s1_act, ("ex", n, h), s)
                        pe.matmul(PS[0:HD1 + 1, 2 + h, q0 - 512 * c:512], VH[:, b, h, j, :],
                                  pe_[:, h, n % 2, 0:512 * (c + 1) - q0], start=(j == 0), stop=(j == 4 * c + 3))\
                            .then_inc(s1_pe.sem, 1)
                    elif r[0] == "w" and second:
                        _, c, g = r
                        wait(pe, s1_act, ("oc", c, 1), s)
                        if g == 2:
                            if c == 0:
                                wait(pe, w1_dve, ("x", c, 2), s)
                        elif first and c == 0:
                            wait(pe, f1_act, ("me", 0, g), s + 1)
                        elif c == 0:
                            wait(pe, w1_dve, ("x", 1, 7), s, 1)
                        else:
                            wait(pe, w1_dve, ("x", 0, 7), s)
                        lo = GROUPS[g][0]
                        for q in GROUPS[g]:
                            t, h = q // 2, q % 2
                            ins = pe.matmul(PS[:, W_BANK[(c, g)], (q - lo) * (D + 1):(q - lo + 1) * (D + 1)],
                                            ZT[0:HD1 + 1, h, c, t * P:(t + 1) * P],
                                            WO[0:HD1 + 1, bass.ds(hp * 2 + h, 1), :], start=True, stop=True)
                        ins.then_inc(w1_pe.sem, 1)
                    elif r in ("q", "k") and first:
                        a = ("q", "k").index(r)
                        if a == 0:
                            pe.wait_ge(w1_stage, next_hp + 1)
                            wait(pe, f1_act, ("me", 1, 1), s + 1, 1)
                        else:
                            wait(pe, f1_act, ("me", 0, 1), s + 1, 1)
                            wait(pe, w1_dve, ("x", 1, 7), s, 1)
                        for c in range(2):
                            x0 = nb * S + c * 512
                            ins = pe.matmul(PS[:, 4 + 2 * a + c, :], wqk_s[:, a, :], XT[:, x0:x0 + 512], start=True,
                                            stop=True)
                        ins.then_inc(f1_pe.sem, 1)
                    elif r == "v" and first:
                        wait(pe, f1_dve, ("ql", 1), s + 1)
                        for t in range(TB):
                            x0 = nb * S + t * P
                            ins = pe.matmul(PS[:, 4 + t // 4, (t % 4) * P:(t % 4 + 1) * P], XT[:, x0:x0 + P],
                                            W1[:, bass.ds(next_hp * P + W1_AT["wv"][0], P)], start=True, stop=True)
                        ins.then_inc(f1_pe.sem, 1)
                    elif r[0] == "a" and first:
                        p = r[1]
                        c, h, i, k = PIECES[p]
                        w = min(512, (i + 1) * P - 512 * k)
                        if p == 6 and not second:
                            gate(1, w1("gate"), E1, 2)
                        if p == 0:
                            wait(pe, f1_dve, ("kd", 1), s + 1)
                            wait(pe, f1_act, ("qb", 1), s + 1)
                        if p < 2:
                            wait(pe, f1_act, ("v", p), s + 1)
                        else:
                            wait(pe, f1_dve, ("mx", p - 2), s + 1)
                        pe.matmul(PS[:, 4 + p % 2, 0:w], QA[:, nb, h, i * P:(i + 1) * P],
                                  KA[:, nb, h, 512 * k:512 * k + w], start=True, stop=False)
                        ins = pe.matmul(PS[:, 4 + p % 2, 0:w], QB[0:HD1, nb, h, i * P:(i + 1) * P],
                                        KB[0:HD1, nb, h, 512 * k:512 * k + w], start=False, stop=True)
                        if k == c:
                            ins = pe.matmul(PS[:, 4 + p % 2, w - P:w], ident_b[:, :], mask_qk[:, :], start=False,
                                            stop=True, skip_group_check=True)
                        ins.then_inc(f1_pe.sem, 1)
                    elif r[0] == "mr" and first:
                        _, c, h = r
                        wait(pe, f1_dve, ("nl", c, h), s + 1)
                        if c:
                            wait(pe, f1_dve, ("mx", 22 + h), s + 1)
                        else:
                            wait(pe, f1_dve, ("kl", 1), s + 1)
                        for i in range(4):
                            ins = pe.transpose(PS[0:2, MR_BANK[(c, h)], i * P:(i + 1) * P], NM2[:, h, 4 * c + i, :],
                                               ident[:, :])
                        ins.then_inc(f1_pe.sem, 1)

            do_round(-1, 1, None, 0, second=False)
            pe.wait_ge(a1_ones, 1)
            pe.wait_ge(wo_loaded, 32)
            with pe.Fori(0, H1 // 2 - 1) as hp:
                do_round(hp * 2, 0, hp, hp)
                do_round(hp * 2 + 1, 1, hp, hp + 1)
            do_round(ROUNDS - 2, 0, H1 // 2 - 1, H1 // 2 - 1)
            do_round(ROUNDS - 1, 1, H1 // 2 - 1, None, first=False)
            pe.wait_ge(w1_dve.sem, w1_dve.at(("x", 1, 7), ROUNDS - 1))

            with pe.Fori(0, E1 // 2) as ep:
                for m in range(NM1 + 1):
                    if m < NM1:
                        k = m // NC
                        if m % NC == 0:
                            pe.wait_ge(m1_low.sem, ep * 2 + k + 1)
                        for u in (2 * m, 2 * m + 1):
                            half = u % 2
                            if u >= 3:
                                wait(pe, m1_dve, ("mu", u - 3), ep)
                            else:
                                wait(pe, m1_dve, ("mu", max(v for v in range(2 * NM1) if v % 3 == u)), ep, 1)
                            if m < NC and half == 0:
                                pe.wait_ge(m1_tok_low, m % NC + 1)
                            cols = slice((m % NC) * 512, (m % NC + 1) * 512)
                            for a, w in enumerate((w11_s, w12_s)):
                                for i, (part, xs) in enumerate(((0, XH), (1, XH), (0, XL))):
                                    ins = pe.matmul(PS[:, 2 * (u % 3) + a, :], w[:, k, part, half * P:(half + 1) * P],
                                                    xs[:, cols], start=(i == 0), stop=(i == 2))
                            ins.then_inc(m1_pe.sem, 1)
                    if m >= 1:
                        d = m - 1
                        wait(pe, m1_dve, ("mu", 2 * d + 1), ep)
                        if d >= 2:
                            wait(pe, m1_dve, ("ac", d - 2, 3), ep)
                        else:
                            wait(pe, m1_dve, ("ac", NM1 - 2 + d, 3), ep, 1)
                        for i in range(4):
                            for half in range(2):
                                at = W1_AT["w2"][0] + (d // NC) * 2 * D + half * D
                                ins = pe.matmul(PS[:, 6 + d % 2, i * P:(i + 1) * P],
                                                HB[:, d % 2, half, i * P:(i + 1) * P],
                                                W1[:, bass.ds(ep * (4 * D) + at, D)], start=(half == 0),
                                                stop=(half == 1))
                        ins.then_inc(m1_pe.sem, 1)


def pack(parts, made):
    cols = []
    for name, n in parts:
        a = np.asarray(made[name], np.float32).reshape(P, n)
        cols.append(a)
    return np.ascontiguousarray(np.concatenate(cols, axis=1))


def blocks_of(wt):
    k, n = wt.shape
    return wt.reshape(k // P, P, n).transpose(1, 0, 2).reshape(P, -1)


def layout(i):
    g = {k: np.asarray(v) for k, v in i.items()}
    a, f = "L0_attn_", "L0_ffn_"
    rows = lambda v: np.broadcast_to(v[None, :], (P, v.shape[0]))
    w0 = {
        "wq_ttt": g[a + "W_Q"], "wk_ttt": g[a + "W_KV"][:, :D], "wv_ttt": g[a + "W_KV"][:, D:],
        "w1": g[a + "W1"], "w2": g[a + "W2"], "w2t": g[a + "W2"].T,
        "b1_rows": rows(g[a + "b1"]), "b2_rows": rows(g[a + "b2"]), "b1_col": g[a + "b1"], "b2_col": g[a + "b2"],
        "n1": g[f + "n1_w"], "n2": g[f + "n2_w"], "qn": rows(g[f + "qn_w"]), "kn": rows(g[f + "kn_w"]),
        "wqkv": np.concatenate([g[f + "wq"].T, g[f + "wk"].T, g[f + "wv"].T], axis=1), "wo": g[f + "wo"].T,
        "gate": g[f + "gate_w"].T,
    }
    for n in ("e0_up", "e0_down", "e1_w1", "e1_w2", "e1_down", "e2_l1", "e2_l2", "e2_l3", "e2_l4", "e3_down",
              "e3_up", "e3_out"):
        w0[n] = blocks_of(g[f + n].T)
    heads = lambda w: w.transpose(2, 0, 1).reshape(D, H1 * HD1)
    w1 = {
        "wq": heads(g["L1_attn_W_Q"]), "wk": heads(g["L1_attn_W_K"]), "wv": heads(g["L1_attn_W_V"]),
        "wo": blocks_of(g["L1_attn_W_O"].T), "gate": g["L1_ffn_Wg"],
        "w11": g["L1_ffn_W11"].transpose(1, 0, 2), "w12": g["L1_ffn_W12"].transpose(1, 0, 2),
        "w2": g["L1_ffn_W2"].reshape(E1, 2, P, D).transpose(2, 0, 1, 3),
    }
    return g["L0_attn_x"].reshape(B * S, D), pack(W0_PARTS, w0), pack(W1_PARTS, w1)


def kernel(**inputs):
    from concourse import bacc
    from concourse.bass_utils import run_bass_kernel_spmd

    x, w0, w1 = layout(inputs)
    nc = bacc.Bacc("TRN2", target_bir_lowering=False, num_devices=1)
    args = [nc.dram_tensor(n, a.shape, F32, kind="ExternalInput").ap()
            for n, a in (("x", x), ("w0", w0), ("w1", w1))]
    out = nc.dram_tensor("out", (B * S, D), F32, kind="ExternalOutput").ap()
    program(nc, *args, out)
    r = run_bass_kernel_spmd(nc, [{"x": x, "w0": w0, "w1": w1}], core_ids=[0])
    return r.results[0]["out"].reshape(B, S, D)
```
